# Optimizing a Trainium2 kernel written in Bass

```python
import numpy as np
import jax
import jax.numpy as jnp

def _softmax(x, axis=-1):
    return jax.nn.softmax(x, axis=axis)

def _gelu(x):
    return jax.nn.gelu(x, approximate=True)

def _silu(x):
    return jax.nn.silu(x)

def _sigmoid(x):
    return jax.nn.sigmoid(x)

def _layernorm(x, axis=-1, eps=1e-05):
    m = jnp.mean(x, axis=axis, keepdims=True)
    v = jnp.var(x, axis=axis, keepdims=True)
    return (x - m) / jnp.sqrt(v + eps)

def _scatter_add(tgt, idx, src, axis=0):
    return tgt.at[idx].add(src)

def _segment_sum(src, seg, n):
    return jax.ops.segment_sum(src, seg, n)
kernel_name = 'mk_decoder_postln_d1_seqx_r4_9bbc1a'

def setup_inputs(seed: int=0):
    np.random.seed(seed)
    _w = jnp.asarray

    def _rec_inputs():
        import jax
        import jax.numpy as jnp
        _rk = jax.random.key(seed)
        x = 7.22e-05 + 1 * jax.random.normal(jax.random.fold_in(_rk, 1), (8, 256, 512), jnp.float32)
        _lenS = 256 - jax.random.randint(jax.random.fold_in(_rk, 7), (8,), 0, max(1, 256 // 4) + 1, jnp.int32)
        _lenS2 = 256 - jax.random.randint(jax.random.fold_in(_rk, 8), (8,), 0, max(1, 256 // 4) + 1, jnp.int32)
        _ctx_512P = jax.random.normal(jax.random.fold_in(_rk, 11), (8, 16, 128), jnp.float32)
        _ctx_512c = jax.random.dirichlet(jax.random.fold_in(_rk, 511), 0.3 * jnp.ones((16,), jnp.float32), (8, 256))
        _ctx_512t = jnp.einsum('bsk,bkd->bsd', _ctx_512c, _ctx_512P)
        _ctx_512t = _ctx_512t * jax.lax.rsqrt(jnp.mean(jnp.square(_ctx_512t)) + 1e-12) * 0.953939
        ctx_512 = -0.000514642 + 1.00011 * (_ctx_512t + 0.3 * jax.random.normal(jax.random.fold_in(_rk, 611), (8, 256, 128), jnp.float32))
        return (x, ctx_512)
    x, ctx_512 = _rec_inputs()

    def _L0_attn_setup():
        import math
        import jax, jax.numpy as jnp
        import numpy as np
        N_EMBD = 512
        N_HEAD = 16
        N_KV_HEAD = 4
        HEAD_DIM = N_EMBD // N_HEAD
        GROUP = N_HEAD // N_KV_HEAD
        key = jax.random.key(seed)
        ks = jax.random.split(key, 6)
        B, T = (2, 512)
        s = 1.0 / math.sqrt(N_EMBD)
        x = jax.random.normal(ks[0], (B, T, N_EMBD), dtype=jnp.float32)
        Wq = jax.random.normal(ks[1], (N_EMBD, N_HEAD * HEAD_DIM), dtype=jnp.float32) * s
        Wk = jax.random.normal(ks[2], (N_EMBD, N_KV_HEAD * HEAD_DIM), dtype=jnp.float32) * s
        Wv = jax.random.normal(ks[3], (N_EMBD, N_KV_HEAD * HEAD_DIM), dtype=jnp.float32) * s
        Wo = jax.random.normal(ks[4], (N_EMBD, N_EMBD), dtype=jnp.float32) * s
        return {'x': x, 'Wq': Wq, 'Wk': Wk, 'Wv': Wv, 'Wo': Wo}
    _L0_attn_all = _L0_attn_setup()
    _L0_attn_in = {k: v for k, v in _L0_attn_all.items() if k in ('Wq', 'Wk', 'Wv', 'Wo')}
    del _L0_attn_all

    def _L0_xattn_setup():
        import jax, jax.numpy as jnp
        import numpy as np
        B, S, H, NH, L = (2, 512, 512, 16, 128)
        HD = H // NH
        key = jax.random.key(seed)
        k1, k2, k3, k4, k5 = jax.random.split(key, 5)
        scale = 0.02
        return {'q': jax.random.normal(k1, (B, S, H), dtype=jnp.float32), 'latent_kv': jax.random.normal(k2, (B, S, L), dtype=jnp.float32), 'Wq': jax.random.normal(k3, (H, H), dtype=jnp.float32) * scale, 'Wkv_expand': jax.random.normal(k4, (2 * H, L), dtype=jnp.float32) * scale, 'Wout': jax.random.normal(k5, (H, H), dtype=jnp.float32) * scale}
    _L0_xattn_all = _L0_xattn_setup()
    _L0_xattn_in = {k: v for k, v in _L0_xattn_all.items() if k in ('Wq', 'Wkv_expand', 'Wout')}
    del _L0_xattn_all

    def _L0_ffn_setup():
        import jax, jax.numpy as jnp
        import numpy as np
        import math
        B, S, D = (2, 512, 512)
        P = 4
        PW = 2
        L = 2
        STD = 0.02
        EPS = 1e-05

        def _layer_norm(x, g, b):
            m = jnp.mean(x, axis=-1, keepdims=True)
            v = jnp.mean(jnp.square(x - m), axis=-1, keepdims=True)
            return (x - m) * jax.lax.rsqrt(v + EPS) * g + b
        key = jax.random.key(seed)
        ks = jax.random.split(key, 16)
        n = lambda k, shape: jax.random.normal(k, shape, dtype=jnp.float32) * STD
        inp = {'x': jax.random.normal(ks[0], (B, S, D), dtype=jnp.float32), 'amp_w': n(ks[1], (D, D)), 'amp_b': jnp.zeros((D,), jnp.float32), 'ph_w': n(ks[2], (D, D)), 'ph_b': jnp.zeros((D,), jnp.float32), 'ent_w': n(ks[3], (L, D, P * D)), 'ent_b': jnp.zeros((L, P * D), jnp.float32), 'ent_pw': n(ks[4], (L, P * D, D)), 'ent_pb': jnp.zeros((L, D), jnp.float32), 'path_w': n(ks[5], (L, PW, D, D)), 'path_b': jnp.zeros((L, PW, D), jnp.float32), 'phase': jax.random.normal(ks[6], (L, PW, D), dtype=jnp.float32), 'ln3_g': jnp.ones((L, D), jnp.float32), 'ln3_b': jnp.zeros((L, D), jnp.float32), 'ln4_g': jnp.ones((L, D), jnp.float32), 'ln4_b': jnp.zeros((L, D), jnp.float32)}
        return inp
    _L0_ffn_all = _L0_ffn_setup()
    _L0_ffn_in = {k: v for k, v in _L0_ffn_all.items() if k in ('amp_w', 'amp_b', 'ph_w', 'ph_b', 'ent_w', 'ent_b', 'ent_pw', 'ent_pb', 'path_w', 'path_b', 'phase', 'ln3_g', 'ln3_b', 'ln4_g', 'ln4_b')}
    del _L0_ffn_all
    return {'x': x, 'ctx_512': ctx_512, 'L0_attn_Wq': _L0_attn_in['Wq'], 'L0_attn_Wk': _L0_attn_in['Wk'], 'L0_attn_Wv': _L0_attn_in['Wv'], 'L0_attn_Wo': _L0_attn_in['Wo'], 'L0_xattn_Wq': _L0_xattn_in['Wq'], 'L0_xattn_Wkv_expand': _L0_xattn_in['Wkv_expand'], 'L0_xattn_Wout': _L0_xattn_in['Wout'], 'L0_ffn_amp_w': _L0_ffn_in['amp_w'], 'L0_ffn_amp_b': _L0_ffn_in['amp_b'], 'L0_ffn_ph_w': _L0_ffn_in['ph_w'], 'L0_ffn_ph_b': _L0_ffn_in['ph_b'], 'L0_ffn_ent_w': _L0_ffn_in['ent_w'], 'L0_ffn_ent_b': _L0_ffn_in['ent_b'], 'L0_ffn_ent_pw': _L0_ffn_in['ent_pw'], 'L0_ffn_ent_pb': _L0_ffn_in['ent_pb'], 'L0_ffn_path_w': _L0_ffn_in['path_w'], 'L0_ffn_path_b': _L0_ffn_in['path_b'], 'L0_ffn_phase': _L0_ffn_in['phase'], 'L0_ffn_ln3_g': _L0_ffn_in['ln3_g'], 'L0_ffn_ln3_b': _L0_ffn_in['ln3_b'], 'L0_ffn_ln4_g': _L0_ffn_in['ln4_g'], 'L0_ffn_ln4_b': _L0_ffn_in['ln4_b']}

def reference(x, ctx_512, L0_attn_Wq, L0_attn_Wk, L0_attn_Wv, L0_attn_Wo, L0_xattn_Wq, L0_xattn_Wkv_expand, L0_xattn_Wout, L0_ffn_amp_w, L0_ffn_amp_b, L0_ffn_ph_w, L0_ffn_ph_b, L0_ffn_ent_w, L0_ffn_ent_b, L0_ffn_ent_pw, L0_ffn_ent_pb, L0_ffn_path_w, L0_ffn_path_b, L0_ffn_phase, L0_ffn_ln3_g, L0_ffn_ln3_b, L0_ffn_ln4_g, L0_ffn_ln4_b):
    import jax
    import jax.numpy as jnp

    def _L0_attn_ref(x, Wq, Wk, Wv, Wo):
        import math
        import jax, jax.numpy as jnp
        import numpy as np
        N_EMBD = 512
        N_HEAD = 16
        N_KV_HEAD = 4
        HEAD_DIM = N_EMBD // N_HEAD
        GROUP = N_HEAD // N_KV_HEAD
        B, T, _ = x.shape
        q = (x @ Wq).reshape(B, T, N_HEAD, HEAD_DIM).transpose(0, 2, 1, 3)
        k = (x @ Wk).reshape(B, T, N_KV_HEAD, HEAD_DIM).transpose(0, 2, 1, 3)
        v = (x @ Wv).reshape(B, T, N_KV_HEAD, HEAD_DIM).transpose(0, 2, 1, 3)
        k = jnp.repeat(k, GROUP, axis=1)
        v = jnp.repeat(v, GROUP, axis=1)
        scale = 1.0 / math.sqrt(HEAD_DIM)
        att = jnp.einsum('bhqd,bhkd->bhqk', q, k) * scale
        causal = jnp.tril(jnp.ones((T, T), dtype=bool))
        att = jnp.where(causal[None, None], att, -jnp.inf)
        att = jax.nn.softmax(att, axis=-1)
        y = jnp.einsum('bhqk,bhkd->bhqd', att, v)
        y = y.transpose(0, 2, 1, 3).reshape(B, T, N_EMBD)
        return y @ Wo

    def _L0_xattn_ref(q, latent_kv, Wq, Wkv_expand, Wout):
        import jax, jax.numpy as jnp
        import numpy as np
        B, S, H, NH, L = (2, 512, 512, 16, 128)
        HD = H // NH
        b, sq, _ = q.shape
        sk = latent_kv.shape[1]
        qp = q @ Wq.T
        kv = latent_kv @ Wkv_expand.T
        k, v = jnp.split(kv, 2, axis=-1)
        qh = qp.reshape(b, sq, NH, HD).transpose(0, 2, 1, 3)
        kh = k.reshape(b, sk, NH, HD).transpose(0, 2, 1, 3)
        vh = v.reshape(b, sk, NH, HD).transpose(0, 2, 1, 3)
        inv_sqrt_d = 1.0 / jnp.sqrt(jnp.float32(HD))
        scores = jnp.einsum('bhqd,bhkd->bhqk', qh, kh) * inv_sqrt_d
        causal = jnp.tril(jnp.ones((sq, sk), dtype=bool))
        scores = jnp.where(causal, scores, jnp.finfo(scores.dtype).min)
        attn = jax.nn.softmax(scores, axis=-1)
        out = jnp.einsum('bhqk,bhkd->bhqd', attn, vh)
        out = out.transpose(0, 2, 1, 3).reshape(b, sq, H)
        return out @ Wout.T

    def _L0_ffn_ref(x, amp_w, amp_b, ph_w, ph_b, ent_w, ent_b, ent_pw, ent_pb, path_w, path_b, phase, ln3_g, ln3_b, ln4_g, ln4_b):
        import jax, jax.numpy as jnp
        import numpy as np
        import math
        B, S, D = (2, 512, 512)
        P = 4
        PW = 2
        L = 2
        STD = 0.02
        EPS = 1e-05

        def _layer_norm(x, g, b):
            m = jnp.mean(x, axis=-1, keepdims=True)
            v = jnp.mean(jnp.square(x - m), axis=-1, keepdims=True)
            return (x - m) * jax.lax.rsqrt(v + EPS) * g + b
        amp = jax.nn.sigmoid(x @ amp_w + amp_b)
        ph = jnp.tanh(x @ ph_w + ph_b) * math.pi
        h = (jnp.cos(ph) + jnp.sin(ph)) * amp
        for l in range(L):
            e = h @ ent_w[l] + ent_b[l]
            ent = e @ ent_pw[l] + ent_pb[l]
            h = _layer_norm(h + ent, ln3_g[l], ln3_b[l])
            t = jnp.einsum('bsd,pdf->pbsf', h, path_w[l]) + path_b[l][:, None, None, :]
            mod = jnp.cos(phase[l]) + jnp.sin(phase[l])
            interf = jnp.sum(t * mod[:, None, None, :], axis=0)
            h = _layer_norm(h + interf, ln4_g[l], ln4_b[l])
        return h
    x = _layernorm(x + _L0_attn_ref(x, L0_attn_Wq, L0_attn_Wk, L0_attn_Wv, L0_attn_Wo), axis=-1)
    x = _layernorm(x + _L0_xattn_ref(x, ctx_512, L0_xattn_Wq, L0_xattn_Wkv_expand, L0_xattn_Wout), axis=-1)
    x = _layernorm(x + _L0_ffn_ref(x, L0_ffn_amp_w, L0_ffn_amp_b, L0_ffn_ph_w, L0_ffn_ph_b, L0_ffn_ent_w, L0_ffn_ent_b, L0_ffn_ent_pw, L0_ffn_ent_pb, L0_ffn_path_w, L0_ffn_path_b, L0_ffn_phase, L0_ffn_ln3_g, L0_ffn_ln3_b, L0_ffn_ln4_g, L0_ffn_ln4_b), axis=-1)
    return x

_drawn_inputs = setup_inputs


def setup_inputs(seed=0):
    import zlib

    import numpy as np

    out = dict(_drawn_inputs(seed))
    spreads = {'L0_ffn_amp_b': (0.0, 0.1),
     'L0_ffn_ph_b': (0.0, 0.1),
     'L0_ffn_ent_b': (0.0, 0.1),
     'L0_ffn_ent_pb': (0.0, 0.1),
     'L0_ffn_path_b': (0.0, 0.1),
     'L0_ffn_ln3_g': (1.0, 0.2),
     'L0_ffn_ln3_b': (0.0, 0.1),
     'L0_ffn_ln4_g': (1.0, 0.2),
     'L0_ffn_ln4_b': (0.0, 0.1)}
    factors = {'L0_xattn_Wq': 21.679}
    for name, (base, spread) in spreads.items():
        noise = np.random.default_rng([zlib.crc32(name.encode()), seed]).standard_normal(out[name].shape)
        drawn = base * np.exp(spread * noise) if base else spread * noise
        out[name] = jnp.asarray(drawn.astype(out[name].dtype))
    for name, factor in factors.items():
        out[name] = (out[name] * factor).astype(out[name].dtype)
    return out
```

```python
from contextlib import ExitStack

import concourse.bass as bass
from concourse import mybir

F32 = mybir.dt.float32
F32R = mybir.dt.float32r
BF16 = mybir.dt.bfloat16
ALU = mybir.AluOpType
ACT = mybir.ActivationFunctionType
AX = mybir.AxisListType

P = 128
B, S, D = 8, 256, 512
L = 128
NH, HD = 16, 32
NKV = 4
KT = D // P
TT = S // P
HG = P // HD
NG = NH // HG
EW = 4 * D
ET = EW // P
NL, NP = 2, 2
BT = 4
NB = B * S // (BT * P)
EPS = 1e-5
SCALE = HD ** -0.5
MASKED = -1e30
N_CONST = 8
SQRT_HALF = 0.5 ** 0.5
PI = 3.141592653589793

QKV = D + 2 * NKV * HD
OFF_QKV = 0
OFF_CKV = OFF_QKV + KT * QKV
OFF_WO = OFF_CKV + 2 * D
OFF_CQ = OFF_WO + KT * D
OFF_COUT = OFF_CQ + KT * D
W_ATT = OFF_COUT + KT * D
OFF_AMP, OFF_PH = 0, KT * D
OFF_ENT = [2 * KT * D, 4 * KT * D]
OFF_PATH = [3 * KT * D, 5 * KT * D]
W_FFN = 6 * KT * D


class Plan:

    def __init__(self, full, drained):
        self.full, self.drained = full, drained
        self.count = [0] * len(full)
        self.base = list(self.count)
        self.per = [0] * len(full)
        self.at = {}
        self.ring = 0

    def start(self):
        self.base, self.count, self.at, self.ring = [b + c for b, c in zip(self.base, self.count)], [0] * len(self.full), {}, 0

    def loop(self):
        self.per = list(self.count)

    def take(self, name, bank):
        self.count[bank] += 1
        self.at[name] = (bank, self.count[bank])

    def bank(self, name):
        return self.at[name][0]

    def value(self, it, name):
        bank, k = self.at[name]
        return it * self.per[bank] + (self.base[bank] + k)


class Banks:

    def __init__(self, eng, plan, it):
        self.eng, self.plan, self.it = eng, plan, it

    def wait_free(self, name):
        self.eng.wait_ge(self.plan.drained[self.plan.bank(name)], self.plan.value(self.it, name) - 1)

    def wait_full(self, name):
        self.eng.wait_ge(self.plan.full[self.plan.bank(name)], self.plan.value(self.it, name))

    def wait_drained(self, name):
        self.eng.wait_ge(self.plan.drained[self.plan.bank(name)], self.plan.value(self.it, name))

    def filled(self, name, ins):
        ins.then_inc(self.plan.full[self.plan.bank(name)], 1)

    def drain(self, name, ins):
        ins.then_inc(self.plan.drained[self.plan.bank(name)], 1)


def attention_plan(plan, last):
    def ring(name):
        plan.take(name, plan.ring % 4)
        plan.ring += 1

    def attention(a, before_tail, before_out):
        for step in range(NG):
            for j in range(HG):
                ring((a, "S", step, j))
            if step >= 1:
                for j in range(HG):
                    plan.take((a, "T", step - 1, j), 4 + j % 2)
            if step >= 2:
                plan.take((a, "O", step - 2), 6 + step % 2)
        for n in before_tail:
            ring(n)
        for j in range(HG):
            plan.take((a, "T", NG - 1, j), 4 + j % 2)
        plan.take((a, "O", NG - 2), 6 + (NG - 2) % 2)
        for n in before_out:
            ring(n)
        plan.take((a, "O", NG - 1), 6 + (NG - 1) % 2)

    attention("self", [("ck", m) for m in range(KT)], [] if last else ["sk"])
    for n in ([] if last else [("sv", i) for i in range(TT)]):
        ring(n)
    for n in ([("wo", i) for i in range(TT)] + [("cv", i) for i in range(TT)]
              + [("x1t", i) for i in range(TT)] + [("cq", m) for m in range(KT)]):
        ring(n)
    attention("cross", [] if last else [("sq", 0), ("sq", 1)], [])
    for n in ([] if last else [("sq", 2), ("sq", 3)]) + [("wout", i) for i in range(TT)]:
        ring(n)


def wait_alone(eng, sem, value, s_passed):
    eng.wait_ge(sem, value)
    eng.sem_inc(s_passed, 1)


def split_products(t, out, lhs, rhs, kts, first=True, last=True):
    for n, k in enumerate(kts):
        for m, (a, b) in enumerate(((0, 0), (0, 1), (1, 0))):
            ins = t.matmul(out, lhs(a, k), rhs(b, k), start=first and n == 0 and m == 0,
                           stop=last and n == len(kts) - 1 and m == 2, skip_group_check=True)
    return ins


def build(nc, A):
    with ExitStack() as whole:
        def sem(name):
            return whole.enter_context(nc.semaphore(name))

        def sb(ctx, name, shape, dt=F32):
            return ctx.enter_context(nc.sbuf_tensor(name, shape, dt))

        banks = [whole.enter_context(nc.psum_tensor(f"bank{i}", [P, 512], F32)) for i in range(8)]
        x2 = sb(whole, "x2", [P, B * TT, D])
        ident = sb(whole, "ident", [P, P])
        ident16 = sb(whole, "ident16", [P, P], BF16)
        mask16 = sb(whole, "mask16", [P, 2, P], BF16)
        ones = sb(whole, "ones", [P, P])
        s_const, s_passed = sem("s_const"), sem("s_passed")
        with ExitStack() as ctx:
            attention_phase(nc, ctx, sb, sem, A, banks, x2, ident, ident16, mask16, ones, s_const, s_passed)
        with ExitStack() as ctx:
            W = sb(ctx, "w_ffn", [P, 2, W_FFN], F32R)
            bias = sb(ctx, "stage_bias", [P, 2 * NL, D])
            with ExitStack() as inner:
                fusion_phase(nc, inner, sb, sem, A, banks, W, bias, ones, s_passed)
            with ExitStack() as inner:
                ffn_phase(nc, inner, sb, sem, A, banks, W, bias, x2, ident, s_passed)


def attention_phase(nc, ctx, sb, sem, A, banks, x2, ident, ident16, mask16, ones, s_const, s_passed):
    W = sb(ctx, "w_att", [P, 2, W_ATT], F32R)
    xT_raw = sb(ctx, "xT_raw", [P, KT, S])
    xT = sb(ctx, "xT", [P, 2, KT, S], F32R)
    ctx_raw = sb(ctx, "ctx_raw", [P, S])
    ctxT = sb(ctx, "ctxT", [P, 2, S], F32R)
    qT = sb(ctx, "qT", [P, 2, NG, S], F32R)
    skT = sb(ctx, "skT", [P, 2, S], F32R)
    sv = sb(ctx, "sv", [P, TT, NKV * HD])
    ckT = sb(ctx, "ckT", [P, 2, NG, S], F32R)
    cv = sb(ctx, "cv", [P, TT, D])
    PW = S // 2 + S
    RING = 2 * HG
    prob = sb(ctx, "prob", [P, RING, PW])
    probT = sb(ctx, "probT", [P, RING, PW])
    nmax = sb(ctx, "nmax", [P, RING, TT])
    rden = sb(ctx, "rden", [P, 2, S])
    o32 = sb(ctx, "o32", [P, 2, S])
    oT = sb(ctx, "oT", [P, 2, NG, S], F32R)
    xres = sb(ctx, "xres", [P, TT, D])
    x1T = sb(ctx, "x1T", [P, 2, KT, S], F32R)
    stats = sb(ctx, "stats", [P, TT, 6])
    mv = sb(ctx, "mv", [P, TT, 2])
    rstd = sb(ctx, "rstd", [P, TT, 2])
    half = sb(ctx, "half", [P, 1])

    s_wraw = [sem(f"s_wraw{i}") for i in range(5)]
    s_whi, s_wlo = sem("s_whi"), sem("s_wlo")
    s_xT, s_ctx, s_x = sem("s_xT"), sem("s_ctx"), sem("s_x")
    s_xh, s_xs = sem("s_xh"), sem("s_xs")
    s_ch, s_cs = sem("s_ch"), sem("s_cs")
    s_hi = sem("s_hi")
    s_max = sem("s_max")
    s_rden = sem("s_rden")
    s_oh, s_os = sem("s_oh"), sem("s_os")
    s_bn, s_agg = sem("s_bn"), sem("s_agg")
    s_var, s_rstd = sem("s_var"), sem("s_rstd")
    s_norm = sem("s_norm")
    full = [sem(f"s1_full{i}") for i in range(8)]
    drained = [sem(f"s1_drained{i}") for i in range(8)]

    HI_LOOP = 2 * KT + 1 + TT + KT
    HI_PRO = 1 + KT
    wq = lambda k, c, n: (lambda h: W[:, h, OFF_QKV + k * QKV + c:OFF_QKV + k * QKV + c + n])

    plan_pro = Plan(full, drained)
    for n, name in enumerate(["sk"] + [("sv", i) for i in range(TT)] + [("sq", m) for m in range(KT)]):
        plan_pro.take(name, n % 4)
    plan_body = Plan(full, drained)
    plan_body.base, plan_body.count = [0] * 8, list(plan_pro.count)
    plan_body.start()
    attention_plan(plan_body, False)
    plan_body.loop()
    plan_last = Plan(full, drained)
    plan_last.base = list(plan_body.base)
    plan_last.per = list(plan_body.per)
    plan_last.ring = 0
    attention_plan(plan_last, True)

    def every_iteration(eng, body):
        with eng.Fori(0, B - 1) as b:
            body(b, plan_body, False)
        body(B - 1, plan_last, True)

    x2f = x2[:, :, :].rearrange("p t d -> p (t d)")
    prf = prob[:, :, :].rearrange("p t d -> p (t d)")
    matrices = [(OFF_QKV, KT * QKV, prf[:, 0:KT * QKV], A["w_qkv"]),
                (OFF_CKV, 2 * D, x2f[:, 3 * KT * D:3 * KT * D + 2 * D], A["w_ckv"]),
                (OFF_WO, KT * D, x2f[:, 0:KT * D], A["w_o"]),
                (OFF_CQ, KT * D, x2f[:, KT * D:2 * KT * D], A["w_cq"]),
                (OFF_COUT, KT * D, x2f[:, 2 * KT * D:3 * KT * D], A["w_cout"])]
    pieces = [(n, off + c, src[:, c:c + D]) for n, (off, w, src, _) in enumerate(matrices) for c in range(0, w, D)]
    first_pieces = KT * QKV // D

    with nc.Block() as block:
        @block.sync
        def _(q):
            def load(b, first):
                q.dma_start(xT_raw[:, :, :], A["xT"].rearrange("(k p) (b s) -> b p k s", p=P, b=B)[b]).then_inc(s_xT, 16)
                q.dma_start(ctx_raw[:, :], A["ctxT"].rearrange("p (b s) -> b p s", b=B)[b]).then_inc(s_ctx, 16)
                q.dma_start(xres[:, :, :], A["x"].rearrange("b (t p) d -> b p t d", p=P)[b]).then_inc(s_x, 16)
            _, w, dst, src = matrices[0]
            q.dma_start(xT_raw[:, :, :], A["xT"].rearrange("(k p) (b s) -> b p k s", p=P, b=B)[0]).then_inc(s_xT, 16)
            for n, (_, w, dst, src) in enumerate(matrices):
                k = w // src.shape[1]
                q.dma_start(dst.rearrange("p (k n) -> p k n", k=k), src.rearrange("(k p) n -> p k n", p=P)).then_inc(s_wraw[n], 16)
            q.dma_start(ctx_raw[:, :], A["ctxT"].rearrange("p (b s) -> b p s", b=B)[0]).then_inc(s_ctx, 16)
            q.dma_start(xres[:, :, :], A["x"].rearrange("b (t p) d -> b p t d", p=P)[0]).then_inc(s_x, 16)
            with q.Fori(0, B - 1) as b:
                wait_alone(q, s_xs, b + 1, s_passed)
                q.dma_start(xT_raw[:, :, :], A["xT"].rearrange("(k p) (b s) -> b p k s", p=P, b=B)[b + 1]).then_inc(s_xT, 16)
                wait_alone(q, s_cs, b + 1, s_passed)
                q.dma_start(ctx_raw[:, :], A["ctxT"].rearrange("p (b s) -> b p s", b=B)[b + 1]).then_inc(s_ctx, 16)
                wait_alone(q, s_norm, b * (2 * TT) + 2 * TT, s_passed)
                q.dma_start(xres[:, :, :], A["x"].rearrange("b (t p) d -> b p t d", p=P)[b + 1]).then_inc(s_x, 16)

        @block.gpsimd
        def _(g):
            g.memset(ident[:, :], 0.0).then_inc(s_const, 1)
            g.memset(ident16[:, :], 0.0).then_inc(s_const, 1)
            g.memset(mask16[:, :, :], 0.0).then_inc(s_const, 1)
            g.memset(ones[:, :], 1.0).then_inc(s_const, 1)
            g.memset(half[:, :], -0.5).then_inc(s_const, 1)
            g.wait_ge(s_const, 5)
            for m in (ident, ident16):
                g.affine_select(out=m[:, :], in_=m[:, :], compare_op=ALU.not_equal, fill=1.0, base=0,
                                pattern=[[-1, P]], channel_multiplier=1).then_inc(s_const, 1)
            g.affine_select(out=mask16[:, :, :], in_=mask16[:, :, :], compare_op=ALU.is_ge, fill=MASKED, base=0,
                            pattern=[[0, 2], [-1, P]], channel_multiplier=1).then_inc(s_const, 1)

            def split(hi, lo, raw, s_h, s_l, n):
                g.tensor_scalar(hi, raw, 1.0, 1.0, ALU.mult, ALU.mult).then_inc(s_h, 1)
                g.wait_ge(s_h, n)
                g.tensor_tensor(lo, raw, hi.bitcast(F32), ALU.subtract).then_inc(s_l, 1)

            def split_x(n):
                wait_alone(g, s_xT, n * 16, s_passed)
                split(xT[:, 0, :, :], xT[:, 1, :, :], xT_raw[:, :, :], s_xh, s_xs, n)

            def split_ctx(n):
                wait_alone(g, s_ctx, n * 16, s_passed)
                split(ctxT[:, 0, :], ctxT[:, 1, :], ctx_raw[:, :], s_ch, s_cs, n)

            split_x(1)
            split_ctx(1)

            def body(b, plan, last):
                k = Banks(g, plan, b)

                def outputs(a, ai):
                    for t in range(NG):
                        n = b * (2 * NG) + (ai * NG + t + 1)
                        k.wait_drained((a, "O", t))
                        g.sem_inc(s_passed, 1)
                        split(oT[:, 0, t, :], oT[:, 1, t, :], o32[:, t % 2, :], s_oh, s_os, n)

                def rstds(ai):
                    for i in range(TT):
                        n = b * (2 * TT) + (ai * TT + i + 1)
                        wait_alone(g, s_agg, n, s_passed)
                        g.tensor_scalar(rstd[:, i, 0:1], mv[:, i, 1:2], EPS, None, ALU.add).then_inc(s_var, 1)
                        g.wait_ge(s_var, n)
                        g.tensor_tensor(rstd[:, i, 1:2], rstd[:, i, 0:1], half[:, :], ALU.pow).then_inc(s_rstd, 1)

                if not last:
                    for j in range(4):
                        g.wait_ge(full[j], b * plan.per[j] + plan.base[j])
                    split_x(b + 2)
                outputs("self", 0)
                rstds(0)
                if not last:
                    k.wait_full(("cv", TT - 1))
                    split_ctx(b + 2)
                outputs("cross", 1)
                rstds(1)

            every_iteration(g, body)

        @block.scalar
        def _(s):
            def weights(lot):
                for n, off, raw in lot:
                    s.wait_ge(s_wraw[n], 16)
                    s.activation(W[:, 0, off:off + D], raw, ACT.Copy).then_inc(s_whi, 1)

            def hi(k, name, out, scale=1.0):
                k.wait_full(name)
                src = banks[k.plan.bank(name)][:, 0:512 if len(out.shape) == 3 else S]
                if len(out.shape) == 3:
                    src = src.rearrange("p (k s) -> p k s", k=KT)
                s.activation(out, src, ACT.Copy, scale=scale).then_inc(s_hi, 1)

            def values(k, name, out):
                k.wait_full(name)
                k.drain(name, s.activation(out, banks[k.plan.bank(name)][:, 0:out.shape[1]], ACT.Copy))

            weights(pieces[:first_pieces])
            k = Banks(s, plan_pro, 0)
            hi(k, "sk", skT[:, 0, :])
            for i in range(TT):
                values(k, ("sv", i), sv[:, i, :])
            for m in range(KT):
                hi(k, ("sq", m), qT[:, 0, m, :], SCALE)
            weights(pieces[first_pieces:])

            def body(b, plan, last):
                k = Banks(s, plan, b)

                def probT_tile(a, t, j):
                    if t >= 2:
                        k.wait_full((a, "O", t - 2))
                    k.wait_full((a, "T", t, j))
                    k.drain((a, "T", t, j), s.activation(probT[:, (t % 2) * HG + j, :], banks[k.plan.bank((a, "T", t, j))][:, 0:PW], ACT.Copy))

                def attention(a, ai, before_tail, before_out):
                    for t in range(NG):
                        for j in range(HG):
                            slot = (t % 2) * HG + j
                            n = b * (2 * NH) + (ai * NH + t * HG + j + 1)
                            s.wait_ge(s_max, n)
                            if t >= 2:
                                k.wait_full((a, "T", t - 2, j))
                            bank = banks[k.plan.bank((a, "S", t, j))]
                            s.activation(prob[:, slot, 0:P], bank[:, 0:P], ACT.Exp, bias=nmax[:, slot, 0:1])
                            k.drain((a, "S", t, j), s.activation(prob[:, slot, P:PW], bank[:, P:PW], ACT.Exp, bias=nmax[:, slot, 1:2]))
                            if t >= 1 and j >= 2:
                                probT_tile(a, t - 1, 2 * (j - 2))
                    before_tail()
                    for j in range(0, HG, 2):
                        probT_tile(a, NG - 1, j)
                    before_out()

                def cross_keys():
                    for m in range(KT):
                        hi(k, ("ck", m), ckT[:, 0, m, :])

                def next_queries(ms):
                    for m in ([] if last else ms):
                        hi(k, ("sq", m), qT[:, 0, m, :], SCALE)

                attention("self", 0, cross_keys, lambda: None if last else hi(k, "sk", skT[:, 0, :]))
                if not last:
                    for i in range(TT):
                        values(k, ("sv", i), sv[:, i, :])
                for i in range(TT):
                    values(k, ("cv", i), cv[:, i, :])
                for i in range(TT):
                    hi(k, ("x1t", i), x1T[:, 0, :, i * P:(i + 1) * P])
                for m in range(KT):
                    hi(k, ("cq", m), qT[:, 0, m, :], SCALE)
                attention("cross", 1, lambda: next_queries([0, 1]), lambda: None)
                next_queries([2, 3])

            every_iteration(s, body)

        @block.vector
        def _(v):
            def weights(a, z):
                for i in range(a, z):
                    _, off, raw = pieces[i]
                    v.wait_ge(s_whi, i + 1)
                    v.tensor_tensor(W[:, 1, off:off + D], raw, W[:, 0, off:off + D].bitcast(F32), ALU.subtract).then_inc(s_wlo, 1)

            def lo(k, name, hi, out, n, scale=1.0):
                v.wait_ge(s_hi, n)
                src = banks[k.plan.bank(name)][:, 0:512 if len(out.shape) == 3 else S]
                if len(out.shape) == 3:
                    src = src.rearrange("p (k s) -> p k s", k=KT)
                k.drain(name, v.scalar_tensor_tensor(out, src, scale, hi.bitcast(F32), ALU.mult, ALU.subtract))

            weights(0, first_pieces)
            k = Banks(v, plan_pro, 0)
            lo(k, "sk", skT[:, 0, :], skT[:, 1, :], 1)
            for m in range(KT):
                lo(k, ("sq", m), qT[:, 0, m, :], qT[:, 1, m, :], 2 + m, SCALE)
            weights(first_pieces, len(pieces))

            def body(b, plan, last):
                k = Banks(v, plan, b)
                count = [0]

                def next_hi():
                    count[0] += 1
                    return b * HI_LOOP + (HI_PRO + count[0])

                def probT_tile(a, t, j):
                    if t >= 2:
                        k.wait_full((a, "O", t - 2))
                    k.wait_full((a, "T", t, j))
                    k.drain((a, "T", t, j), v.tensor_copy(probT[:, (t % 2) * HG + j, :], banks[k.plan.bank((a, "T", t, j))][:, 0:PW]))

                def output(a, ai, t):
                    n = b * (2 * NG) + (ai * NG + t + 1)
                    k.wait_full((a, "O", t))
                    bank = banks[k.plan.bank((a, "O", t))]
                    v.reciprocal(rden[:, t % 2, :], bank[:, S:2 * S]).then_inc(s_rden, 1)
                    v.wait_ge(s_rden, n)
                    if t >= 2:
                        v.wait_ge(s_os, n - 2)
                    k.drain((a, "O", t), v.tensor_tensor(o32[:, t % 2, :], bank[:, 0:S], rden[:, t % 2, :], ALU.mult))

                def attention(a, ai, before_tail, before_out):
                    for t in range(NG):
                        for j in range(HG):
                            slot = (t % 2) * HG + j
                            k.wait_full((a, "S", t, j))
                            bank = banks[k.plan.bank((a, "S", t, j))]
                            v.tensor_reduce(nmax[:, slot, 0:1], bank[:, 0:P], AX.X, ALU.max, negate=True)
                            v.tensor_reduce(nmax[:, slot, 1:2], bank[:, P:PW], AX.X, ALU.max, negate=True).then_inc(s_max, 1)
                        if t >= 1:
                            for j in range(1, HG, 2):
                                probT_tile(a, t - 1, j)
                        if t >= 2:
                            output(a, ai, t - 2)
                    before_tail()
                    for j in range(1, HG, 2):
                        probT_tile(a, NG - 1, j)
                    output(a, ai, NG - 2)
                    before_out()
                    output(a, ai, NG - 1)

                def layer_norm(ai, name, out):
                    for i in range(TT):
                        n = b * (2 * TT) + (ai * TT + i + 1)
                        k.wait_full((name, i))
                        if ai == 0:
                            v.wait_ge(s_x, b * 16 + 16)
                        else:
                            v.wait_ge(s_norm, b * (2 * TT) + (i + 1))
                        k.drain((name, i), v.tensor_tensor(xres[:, i, :], banks[k.plan.bank((name, i))][:, :], xres[:, i, :], ALU.add))
                        k.wait_drained((name, i))
                        v.bn_stats(stats[:, i, :], xres[:, i, :]).then_inc(s_bn, 1)
                        wait_alone(v, s_bn, n, s_passed)
                        v.bn_aggr(mv[:, i, :], stats[:, i, :]).then_inc(s_agg, 1)
                        v.wait_ge(s_rstd, n)
                        v.tensor_scalar(out(i), xres[:, i, :], mv[:, i, 0:1], rstd[:, i, 1:2], ALU.subtract, ALU.mult).then_inc(s_norm, 1)

                def cross_keys():
                    for m in range(KT):
                        lo(k, ("ck", m), ckT[:, 0, m, :], ckT[:, 1, m, :], next_hi())

                def next_queries(ms):
                    for m in ([] if last else ms):
                        lo(k, ("sq", m), qT[:, 0, m, :], qT[:, 1, m, :], next_hi(), SCALE)

                attention("self", 0, cross_keys, lambda: None if last else lo(k, "sk", skT[:, 0, :], skT[:, 1, :], next_hi()))
                layer_norm(0, "wo", lambda i: xres[:, i, :])
                for i in range(TT):
                    lo(k, ("x1t", i), x1T[:, 0, :, i * P:(i + 1) * P], x1T[:, 1, :, i * P:(i + 1) * P], next_hi())
                for m in range(KT):
                    lo(k, ("cq", m), qT[:, 0, m, :], qT[:, 1, m, :], next_hi(), SCALE)
                attention("cross", 1, lambda: next_queries([0, 1]), lambda: None)
                next_queries([2, 3])
                layer_norm(1, "wout", lambda i: x2[:, b * TT + i, :])

            every_iteration(v, body)
            v.wait_ge(s_norm, B * 2 * TT)

        @block.tensor
        def _(t_):
            t = t_

            def feature_major(k, name, w, src, kts):
                k.wait_free(name)
                k.filled(name, split_products(t, banks[k.plan.bank(name)][:, 0:S], w, src, kts))

            def token_major(k, name, src, w, kts, width):
                k.wait_free(name)
                k.filled(name, split_products(t, banks[k.plan.bank(name)][:, 0:width], src, w, kts))

            def self_keys(k):
                feature_major(k, "sk", lambda h, c: wq(c, D, NKV * HD)(h), lambda h, c: xT[:, h, c, :], range(KT))

            def self_values(k):
                for i in range(TT):
                    token_major(k, ("sv", i), lambda h, c: xT[:, h, c, i * P:(i + 1) * P],
                                lambda h, c: wq(c, D + NKV * HD, NKV * HD)(h), range(KT), NKV * HD)

            def self_queries(k, ms):
                for m in ms:
                    feature_major(k, ("sq", m), lambda h, c: wq(c, m * P, P)(h), lambda h, c: xT[:, h, c, :], range(KT))

            def weight(off, c, lo_, n):
                return lambda h: W[:, h, off + c * D + lo_:off + c * D + lo_ + n]

            k = Banks(t, plan_pro, 0)
            t.wait_ge(s_wlo, first_pieces)
            t.wait_ge(s_xs, 1)
            self_keys(k)
            self_values(k)
            self_queries(k, range(KT))
            t.wait_ge(s_const, N_CONST)

            def body(b, plan, last):
                k = Banks(t, plan, b)

                def scores(a, g, kT):
                    bank = [banks[plan.bank((a, "S", g, j))] for j in range(HG)]
                    for j in range(HG):
                        k.wait_free((a, "S", g, j))
                        diag = bank[j][:, :].rearrange("p (a b c) -> p a b c", a=2, b=2)[:, :, 0, :]
                        t.matmul(diag, ident16[:, :], mask16[:, :, :], start=True, stop=False, skip_group_check=True)
                    for qt in range(TT):
                        for m, (x, y) in enumerate(((0, 0), (0, 1), (1, 0))):
                            for j in range(HG):
                                rows = slice(HD * j, HD * (j + 1))
                                ins = t.matmul(bank[j][:, P * qt:P * qt + P * (qt + 1)], qT[rows, x, g, qt * P:(qt + 1) * P],
                                               kT(y)[rows, 0:P * (qt + 1)], start=False, stop=qt == TT - 1 and m == 2, skip_group_check=True)
                                if qt == TT - 1 and m == 2:
                                    k.filled((a, "S", g, j), ins)

                def transposes(a, g, j):
                    k.wait_drained((a, "S", g, j))
                    k.wait_free((a, "T", g, j))
                    bank = banks[plan.bank((a, "T", g, j))]
                    for c in range(3):
                        ins = t.transpose(bank[:, c * P:(c + 1) * P], prob[:, (g % 2) * HG + j, c * P:(c + 1) * P], ident[:, :])
                    k.filled((a, "T", g, j), ins)

                def outputs(a, g, js, v_of):
                    if js[0] == 0:
                        k.wait_free((a, "O", g))
                    bank = banks[plan.bank((a, "O", g))]
                    for j in js:
                        k.wait_drained((a, "T", g, j))
                    for what in range(4):
                        for j in js:
                            rows = slice(HD * j, HD * (j + 1))
                            pt = probT[:, (g % 2) * HG + j, :]
                            if what == 0:
                                ins = t.matmul(bank[rows, 0:S], v_of(0, j), pt[:, 0:S], start=True, stop=False, skip_group_check=True)
                            elif what == 1:
                                ins = t.matmul(bank[rows, P:S], v_of(1, j), pt[:, S:PW], start=False, stop=False, skip_group_check=True)
                            elif what == 2:
                                ins = t.matmul(bank[rows, S:2 * S], ones[:, 0:HD], pt[:, 0:S], start=False, stop=False, skip_group_check=True)
                            else:
                                ins = t.matmul(bank[rows, S + P:2 * S], ones[:, 0:HD], pt[:, S:PW], start=False, stop=True, skip_group_check=True)
                    if js[-1] == HG - 1:
                        k.filled((a, "O", g), ins)

                def attention(a, kT_of, v_of, before_tail, before_out):
                    for g in range(NG + 2):
                        if g < NG:
                            scores(a, g, kT_of(g))
                        if g == NG:
                            before_tail()
                        if g == NG + 1:
                            before_out()
                        if 1 <= g <= NG:
                            transposes(a, g - 1, 0)
                            transposes(a, g - 1, 1)
                        if g >= 2:
                            outputs(a, g - 2, [0, 1], lambda kt, j: v_of(g - 2, kt, j))
                        if 1 <= g <= NG:
                            transposes(a, g - 1, 2)
                            transposes(a, g - 1, 3)
                        if g >= 2:
                            outputs(a, g - 2, [2, 3], lambda kt, j: v_of(g - 2, kt, j))

                def project_out(name, ai, off):
                    for g in range(NG):
                        t.wait_ge(s_os, b * (2 * NG) + (ai * NG + g + 1))
                    for i in range(TT):
                        token_major(k, (name, i), lambda h, c: oT[:, h, c, i * P:(i + 1) * P],
                                    lambda h, c: weight(off, c, 0, D)(h), range(NG), D)

                def cross_keys():
                    t.wait_ge(s_cs, b + 1)
                    t.wait_ge(s_wlo, len(pieces))
                    for m in range(KT):
                        feature_major(k, ("ck", m), lambda h, c: W[:, h, OFF_CKV + m * P:OFF_CKV + (m + 1) * P],
                                      lambda h, c: ctxT[:, h, :], [0])

                def next_self_keys():
                    if not last:
                        t.wait_ge(s_xs, b + 2)
                        self_keys(k)

                attention("self", lambda g: lambda h: skT[:, h, :], lambda g, kt, j: sv[:, kt, HD * j:HD * (j + 1)],
                          cross_keys, next_self_keys)
                if not last:
                    self_values(k)
                project_out("wo", 0, OFF_WO)
                for i in range(TT):
                    token_major(k, ("cv", i), lambda h, c: ctxT[:, h, i * P:(i + 1) * P],
                                lambda h, c: W[:, h, OFF_CKV + D:OFF_CKV + 2 * D], [0], D)
                for i in range(TT):
                    t.wait_ge(s_norm, b * (2 * TT) + (i + 1))
                    k.wait_free(("x1t", i))
                    for c in range(KT):
                        ins = t.transpose(banks[plan.bank(("x1t", i))][:, c * P:(c + 1) * P], xres[:, i, c * P:(c + 1) * P], ident[:, :])
                    k.filled(("x1t", i), ins)
                for i in range(TT):
                    k.wait_drained(("x1t", i))
                for m in range(KT):
                    feature_major(k, ("cq", m), lambda h, c: weight(OFF_CQ, c, m * P, P)(h), lambda h, c: x1T[:, h, c, :], range(KT))
                attention("cross", lambda g: lambda h: ckT[:, h, g, :], lambda g, kt, j: cv[:, kt, HD * (HG * g + j):HD * (HG * g + j + 1)],
                          lambda: None if last else self_queries(k, [0, 1]), lambda: None)
                if not last:
                    self_queries(k, [2, 3])
                project_out("wout", 1, OFF_COUT)

            every_iteration(t, body)


def fusion_phase(nc, ctx, sb, sem, A, banks, W, bias, ones, s_passed):
    R, HR = 4, 2
    raw = sb(ctx, "raw", [P, R, 2, D])
    tile = sb(ctx, "tile", [P, HR, 2, 2, D], F32R)
    aux = sb(ctx, "aux", [P, 2, NP, D])
    prod = sb(ctx, "prod", [P, D])
    acc = sb(ctx, "acc", [P, D])
    t32 = sb(ctx, "t32", [P, 2, D])
    mod = sb(ctx, "mod", [P, NP, D])
    pbias = sb(ctx, "pbias", [P, NP, D])
    ebias = sb(ctx, "ebias", [P, D])
    eb = sb(ctx, "eb", [P, ET])
    wide = sb(ctx, "wide", [P, (2 * KT - 1) * P])
    s_raw = [sem(f"s_raw{i}") for i in range(R)]
    s_aux = [sem("s_aux0"), sem("s_aux1")]
    s_small = sem("s_small")
    s_wide = sem("s_wide")
    s_hi, s_lo = sem("s2_hi"), sem("s2_lo")
    s_tile = sem("s2_tile")
    s_prod, s_acc = sem("s2_prod"), sem("s2_acc")
    s_mod = sem("s2_mod")
    s_sin = sem("s2_sin")
    s_whi = sem("s2_whi")
    s_t32 = sem("s2_t32")
    s_wlo = sem("s2_wlo")
    s_sum = sem("s2_sum")
    full = [sem(f"s2_full{i}") for i in range(KT + 1)]
    drained = [sem(f"s2_drained{i}") for i in range(KT + 1)]
    layers = W[:, :, 2 * KT * D:].rearrange("p h (l z c) -> p h l z c", l=NL, z=2)
    gates = W[:, :, 0:2 * KT * D].rearrange("p h (l c) -> p h l c", l=2)
    MOD_LINKS, SUM_LINKS = 8, 2 * KT + 2
    AUX = 2 * KT
    FIN = 2 * KT

    def identity(m):
        return wide[:, (KT - 1 - m) * P:(2 * KT - 1 - m) * P]

    with nc.Block() as block:
        @block.sync
        def _(q):
            with q.Fori(0, NL) as l:
                def load(kt):
                    if kt >= R:
                        wait_alone(q, s_lo, l * ET + (kt - R + 1), s_passed)
                        wait_alone(q, s_prod, l * ET + (kt - R + 1), s_passed)
                    q.dma_start(raw[:, kt % R, 0, :], A["ent_wT"][l, kt * P:(kt + 1) * P, :]).then_inc(s_raw[kt % R], 16)
                    q.dma_start(raw[:, kt % R, 1, :], A["ent_pw"][l, kt * P:(kt + 1) * P, :]).then_inc(s_raw[kt % R], 16)

                def load_aux(n):
                    if n >= 2 and n - 2 < KT:
                        wait_alone(q, s_wlo, l * (FIN + KT) + (n - 1), s_passed)
                    if n - 2 >= KT:
                        wait_alone(q, s_t32, l * KT + (n - 1 - KT), s_passed)
                    if n < KT:
                        q.dma_start(aux[:, n % 2, 0, :], A["gate_w"][l, n * P:(n + 1) * P, :]).then_inc(s_aux[n % 2], 16)
                    else:
                        k = n - KT
                        q.dma_start(aux[:, n % 2, :, :], A["path_w"][l, :, k * P:(k + 1) * P, :].rearrange("w p d -> p w d")).then_inc(s_aux[n % 2], 16)

                wait_alone(q, s_lo, l * ET, s_passed)
                wait_alone(q, s_prod, l * ET, s_passed)
                for kt in range(2):
                    load(kt)
                wait_alone(q, s_t32, l * KT, s_passed)
                q.wait_ge(drained[KT], l)
                q.dma_start(mod[:, :, :], A["phase"][l].partition_broadcast(P)).then_inc(s_small, 16)
                q.dma_start(pbias[:, :, :], A["path_b"][l].partition_broadcast(P)).then_inc(s_small, 16)
                q.dma_start(ebias[:, :], A["ent_pb"][l].partition_broadcast(P)).then_inc(s_small, 16)
                q.dma_start(eb[:, :], A["ent_b"][l]).then_inc(s_small, 16)
                for kt in range(2, R):
                    load(kt)
                load_aux(0)
                load_aux(1)
                for kt in range(R, ET):
                    load(kt)
                    if kt % 2 and (kt - R) // 2 + 2 < AUX:
                        load_aux((kt - R) // 2 + 2)

        @block.gpsimd
        def _(g):
            g.memset(wide[:, :], 0.0).then_inc(s_wide, 1)
            g.wait_ge(s_wide, 1)
            g.affine_select(out=wide[:, :], in_=wide[:, :], compare_op=ALU.not_equal, fill=1.0, base=(KT - 1) * P,
                            pattern=[[-1, (2 * KT - 1) * P]], channel_multiplier=1).then_inc(s_wide, 1)
            with g.Fori(0, NL) as l:
                for kt in range(ET):
                    if kt >= 1:
                        g.wait_ge(s_acc, l * (ET - 1) + (kt - 1))
                    if kt == 0:
                        g.wait_ge(s_small, l * 64 + 64)
                        g.wait_ge(full[KT], l)
                    wait_alone(g, s_raw[kt % R], l * (32 * ET // R) + 32 * (kt // R + 1), s_passed)
                    out = acc if kt == 0 else prod
                    g.tensor_scalar(out[:, :], raw[:, kt % R, 1, :], eb[:, kt:kt + 1], 1.0, ALU.mult, ALU.mult).then_inc(s_prod, 1)
                    g.wait_ge(s_prod, l * ET + (kt + 1))
                    if kt >= 1:
                        g.tensor_tensor(acc[:, :], acc[:, :], prod[:, :], ALU.add).then_inc(s_acc, 1)

        @block.scalar
        def _(s):
            s.preload_act_table_set("silu_and_others")
            with s.Fori(0, NL) as l:
                def finished(n):
                    z, k = (1, n) if n < KT else (0, n - KT)
                    if z:
                        s.wait_ge(s_t32, l * KT + (k + 1))
                    else:
                        s.wait_ge(drained[k], l + 1)
                    s.activation(layers[:, 0, l, z, k * D:(k + 1) * D], t32[:, n % 2, :], ACT.Copy).then_inc(s_whi, 1)

                for kt in range(ET):
                    s.wait_ge(s_raw[kt % R], l * (32 * ET // R) + 32 * (kt // R + 1))
                    if kt < HR:
                        s.wait_ge(full[KT - 1], l)
                    else:
                        s.wait_ge(s_tile, l * (ET - 1) + (kt - HR + 1))
                    s.activation(tile[:, kt % HR, 0, :, :], raw[:, kt % R, :, :], ACT.Copy).then_inc(s_hi, 1)
                    if kt in (1, 3, 5, 7):
                        n = kt // 2
                        s.wait_ge(s_aux[n % 2], l * (16 * AUX // 2) + 16 * (n // 2 + 1))
                        s.activation(gates[:, 0, l, n * D:(n + 1) * D], aux[:, n % 2, 0, :], ACT.Copy).then_inc(s_whi, 1)
                    if kt == 8:
                        s.wait_ge(s_mod, l * MOD_LINKS + (MOD_LINKS - 1))
                        s.activation(mod[:, :, :], mod[:, :, :], ACT.Sin).then_inc(s_sin, 1)
                    if kt in (10, 12, 14):
                        finished((kt - 10) // 2)
                finished(KT - 1)
                for m in range(KT):
                    finished(KT + m)

        @block.vector
        def _(v):
            v.wait_ge(s_wide, 2)
            with v.Fori(0, NL) as l:
                links = {}

                def link(ins, sem_, per):
                    links[sem_.name] = links.get(sem_.name, 0) + 1
                    ins.then_inc(sem_, 1)
                    v.wait_ge(sem_, l * per + links[sem_.name])

                M = 1.5 * 2 ** 23
                n2 = t32[:, :, :]
                def reduce_step(i):
                    if i == 0:
                        v.wait_ge(s_small, l * 64 + 64)
                        v.wait_ge(s_wlo, l * (FIN + KT))
                        ins = v.tensor_scalar(n2, mod[:, :, :], 0.5 / PI, 0.125, ALU.mult, ALU.add)
                    elif i == 1:
                        ins = v.tensor_scalar(n2, n2, M, M, ALU.add, ALU.subtract)
                    elif i < 5:
                        c = (6.28125, 0.0019350051879882812, 3.0199159819885386e-07)[i - 2]
                        ins = v.scalar_tensor_tensor(mod[:, :, :], n2, -c, mod[:, :, :], ALU.mult, ALU.add)
                    elif i == 5:
                        ins = v.tensor_scalar(mod[:, :, :], mod[:, :, :], PI / 4, 3.1415925, ALU.add, ALU.min)
                    elif i == 6:
                        ins = v.tensor_scalar(mod[:, :, :], mod[:, :, :], -3.1415925, None, ALU.max)
                    else:
                        v.wait_ge(s_sin, l + 1)
                        ins = v.tensor_scalar(mod[:, :, :], mod[:, :, :], 2 ** 0.5, None, ALU.mult)
                    link(ins, s_mod, MOD_LINKS)

                def path_bias():
                    link(v.tensor_tensor(pbias[:, :, :], pbias[:, :, :], mod[:, :, :], ALU.mult), s_sum, SUM_LINKS)
                    link(v.tensor_tensor(bias[:, 2 * l + 1, :], pbias[:, 0, :], pbias[:, 1, :], ALU.add), s_sum, SUM_LINKS)

                def lo_of_finished(n):
                    v.wait_ge(s_whi, l * (FIN + KT) + (KT + n + 1))
                    z, k = (1, n) if n < KT else (0, n - KT)
                    v.tensor_tensor(layers[:, 1, l, z, k * D:(k + 1) * D], t32[:, n % 2, :],
                                    layers[:, 0, l, z, k * D:(k + 1) * D].bitcast(F32), ALU.subtract).then_inc(s_wlo, 1)

                def path(k):
                    n = KT + k
                    v.wait_ge(s_aux[n % 2], l * (16 * AUX // 2) + 16 * (n // 2 + 1))
                    a = aux[:, n % 2, :, :]
                    link(v.tensor_tensor(a, a, mod[:, :, :], ALU.mult), s_sum, SUM_LINKS)
                    link(v.tensor_tensor(a[:, 0, :], a[:, 0, :], identity(k), ALU.add), s_sum, SUM_LINKS)
                    if k >= 2:
                        v.wait_ge(s_wlo, l * (FIN + KT) + (KT + k - 1))
                    v.tensor_tensor(t32[:, k % 2, :], a[:, 0, :], a[:, 1, :], ALU.add).then_inc(s_t32, 1)

                extra = {k: [lambda k=k: reduce_step(k)] for k in range(MOD_LINKS - 1)}

                def gate_lo(n):
                    v.wait_ge(s_whi, l * (FIN + KT) + (n + 1))
                    v.tensor_tensor(gates[:, 1, l, n * D:(n + 1) * D], aux[:, n % 2, 0, :],
                                    gates[:, 0, l, n * D:(n + 1) * D].bitcast(F32), ALU.subtract).then_inc(s_wlo, 1)

                for n in range(KT):
                    extra.setdefault(2 * n + 2, []).append(lambda n=n: gate_lo(n))
                extra.setdefault(9, []).append(lambda: reduce_step(MOD_LINKS - 1))
                extra[9].append(path_bias)
                extra[9].append(lambda: path(0))
                extra[11] = [lambda: lo_of_finished(0), lambda: path(1)]
                extra[13] = [lambda: lo_of_finished(1), lambda: path(2)]
                extra[15] = [lambda: lo_of_finished(2), lambda: path(3), lambda: lo_of_finished(3)]
                for kt in range(ET):
                    v.wait_ge(s_hi, l * ET + (kt + 1))
                    v.tensor_tensor(tile[:, kt % HR, 1, :, :], raw[:, kt % R, :, :], tile[:, kt % HR, 0, :, :].bitcast(F32),
                                    ALU.subtract).then_inc(s_lo, 1)
                    for f in extra.get(kt, []):
                        f()
                for m in range(KT):
                    v.wait_ge(full[m], l + 1)
                    v.wait_ge(s_wlo, l * (FIN + KT) + (2 * KT + m - 1))
                    v.tensor_tensor(t32[:, m % 2, :], banks[m][:, :], identity(m), ALU.add).then_inc(drained[m], 1)
                    if m >= 1:
                        lo_of_finished(KT + m - 1)
                lo_of_finished(2 * KT - 1)
                v.wait_ge(full[KT], l + 1)
                v.tensor_tensor(bias[:, 2 * l, :], banks[KT][:, :], ebias[:, :], ALU.add).then_inc(drained[KT], 1)
                assert links[s_mod.name] == MOD_LINKS and links[s_sum.name] == SUM_LINKS, links

        @block.tensor
        def _(t):
            with t.Fori(0, NL) as l:
                for kt in range(ET):
                    t.wait_ge(s_lo, l * ET + (kt + 1))
                    for m in range(KT):
                        if kt == 0:
                            t.wait_ge(drained[m], l)
                        ins = split_products(t, banks[m][:, :], lambda h, c: tile[:, kt % HR, h, 0, m * P:(m + 1) * P],
                                             lambda h, c: tile[:, kt % HR, h, 1, :], [0], first=kt == 0, last=kt == ET - 1)
                        if kt == ET - 1:
                            ins.then_inc(full[m], 1)
                    if kt < ET - 1:
                        ins.then_inc(s_tile, 1)
                t.wait_ge(s_acc, l * (ET - 1) + (ET - 1))
                t.wait_ge(drained[KT], l)
                t.matmul(banks[KT][:, :], ones[:, :], acc[:, :], start=True, stop=True).then_inc(full[KT], 1)


def ffn_plan(plan, last):
    def ring(name):
        plan.take(name, plan.ring % 8)
        plan.ring += 1

    for m in range(KT):
        ring(("amp", m))
        ring(("ph", m))
    if not last:
        for i in range(BT):
            ring(("xt", i))
    for u in range(2 * NL * BT + 2):
        if u < 2 * NL * BT:
            ring(("mm", u))
        if 2 <= u < (2 * NL - 1) * BT + 2:
            ring(("tr", u - 2))


def ffn_phase(nc, ctx, sb, sem, A, banks, W, bias, x2, ident, s_passed):
    BS = BT * P
    UN = 2 * NL * BT
    xb = sb(ctx, "xb", [P, BT, D])
    xT = sb(ctx, "x2T", [P, 2, KT, BS], F32R)
    hT = sb(ctx, "hT", [P, 2, KT, BS], F32R)
    y = sb(ctx, "y", [P, BT, D])
    amp = sb(ctx, "amp", [P, 2, BS])
    wave = sb(ctx, "wave", [P, 2, BS])
    ht = sb(ctx, "ht", [P, 2, KT, P])
    lng = sb(ctx, "lng", [P, D])
    lnb = sb(ctx, "lnb", [P, D])
    NCOL = 2 * KT + 2 * (2 * NL - 1) * KT
    cols = sb(ctx, "cols", [P, NCOL])
    stats = sb(ctx, "stats3", [P, BT, 6])
    mv = sb(ctx, "mv3", [P, BT, 2])
    rstd = sb(ctx, "rstd3", [P, BT, 2])
    nhalf = sb(ctx, "nhalf", [P, 1])
    half_ampb = sb(ctx, "half_ampb", [P, KT])
    angles = sb(ctx, "angles", [P, 2])

    s_cols, s_ln = sem("s3_cols"), sem("s3_ln")
    s_c = sem("s3_const")
    s_xb = sem("s3_xb")
    s_hi = sem("s3_hi")
    s_u, s_sin = sem("s3_u"), sem("s3_sin")
    s_gate, s_h0 = sem("s3_gate"), sem("s3_h0")
    s_h0hi, s_h0lo = sem("s3_h0hi"), sem("s3_h0lo")
    s_bn, s_agg, s_var, s_rstd = sem("s3_bn"), sem("s3_agg"), sem("s3_var"), sem("s3_rstd")
    s_norm = sem("s3_norm")
    s_hhi, s_hlo = sem("s3_hhi"), sem("s3_hlo")
    s_g, s_gb = sem("s3_g"), sem("s3_gb")
    s_res = sem("s3_res")
    s_fin = sem("s3_fin")
    s_out = sem("s3_out")
    full = [sem(f"s3_full{i}") for i in range(8)]
    drained = [sem(f"s3_drained{i}") for i in range(8)]
    LN = UN + BT

    plan_pro = Plan(full, drained)
    for i in range(BT):
        plan_pro.take(("xt", i), i)
    plan_body = Plan(full, drained)
    plan_body.count = list(plan_pro.count)
    plan_body.start()
    plan_body.ring = BT
    ffn_plan(plan_body, False)
    assert plan_body.ring % 8 == BT
    plan_body.loop()
    plan_last = Plan(full, drained)
    plan_last.base, plan_last.per, plan_last.ring = list(plan_body.base), list(plan_body.per), BT
    ffn_plan(plan_last, True)

    def every_block(eng, body):
        with eng.Fori(0, NB - 1) as b:
            body(b, plan_body, False)
        body(NB - 1, plan_last, True)

    def gain(s, k):
        c = 2 * KT + 2 * KT * s + k
        return cols[:, c:c + 1]

    def shift(s, k):
        c = 2 * KT + 2 * KT * s + KT + k
        return cols[:, c:c + 1]

    with nc.Block() as block:
        @block.sync
        def _(q):
            q.dma_start(xb[:, :, :], x2[:, 0:BT, :]).then_inc(s_xb, 16)
            q.dma_start(cols[:, :], A["cols"]).then_inc(s_cols, 16)
            q.dma_start(lng[:, :], A["ln_g"].partition_broadcast(P)).then_inc(s_ln, 16)
            q.dma_start(lnb[:, :], A["ln_b"].partition_broadcast(P)).then_inc(s_ln, 16)
            out = A["out"].rearrange("b (t p) d -> (b t) p d", p=P)

            def body(b, plan, last):
                k = Banks(q, plan, b)
                if not last:
                    for i in range(BT):
                        wait_alone(q, full[i], b * plan.per[i] + plan.base[i], s_passed)
                    q.dma_start(xb[:, :, :], x2[:, :, :].rearrange("p (b t) d -> p b t d", t=BT)[:, b + 1, :, :]).then_inc(s_xb, 16)
                for i in range(BT):
                    wait_alone(q, s_fin, b * BT + (i + 1), s_passed)
                    q.dma_start(out[b * BT + i], y[:, i, :]).then_inc(s_out, 16)
                wait_alone(q, s_out, b * (16 * BT) + 16 * BT, s_passed)

            every_block(q, body)

        @block.gpsimd
        def _(g):
            g.memset(nhalf[:, :], -0.5).then_inc(s_c, 1)
            g.memset(angles[:, 0:1], PI / 2).then_inc(s_c, 1)
            g.memset(angles[:, 1:2], -0.25).then_inc(s_c, 1)
            g.wait_ge(s_c, 4)
            g.wait_ge(s_ln, 32)

            def body(b, plan, last):
                def rstd_of(n):
                    i = (n - 1) % BT
                    m = b * LN + n
                    wait_alone(g, s_agg, m, s_passed)
                    g.tensor_scalar(rstd[:, i, 0:1], mv[:, i, 1:2], EPS, None, ALU.add).then_inc(s_var, 1)
                    g.wait_ge(s_var, m)
                    g.tensor_tensor(rstd[:, i, 1:2], rstd[:, i, 0:1], nhalf[:, :], ALU.pow).then_inc(s_rstd, 1)

                def lo(u):
                    i = u % BT
                    g.wait_ge(s_hhi, b * (UN - BT) + (u + 1))
                    g.tensor_tensor(hT[:, 1, :, i * P:(i + 1) * P], ht[:, u % 2, :, :],
                                    hT[:, 0, :, i * P:(i + 1) * P].bitcast(F32), ALU.subtract).then_inc(s_hlo, 1)

                def last_norm(i):
                    n = b * BT + (i + 1)
                    g.wait_ge(s_norm, b * UN + (UN - BT + i + 1))
                    g.tensor_tensor(y[:, i, :], y[:, i, :], lng[:, :], ALU.mult).then_inc(s_g, 1)
                    g.wait_ge(s_g, n)
                    g.tensor_tensor(y[:, i, :], y[:, i, :], lnb[:, :], ALU.add).then_inc(s_gb, 1)

                for u in range(UN):
                    rstd_of(u + 1)
                    if 2 <= u < UN - BT + 2:
                        lo(u - 2)
                for i in range(BT):
                    last_norm(i)
                    if i >= 1:
                        rstd_of(UN + i)
                rstd_of(UN + BT)

            every_block(g, body)

        @block.scalar
        def _(s):
            s.wait_ge(s_c, 4)
            s.wait_ge(s_cols, 16)

            def x2T_hi(k, i):
                k.wait_full(("xt", i))
                bank = banks[k.plan.bank(("xt", i))][:, :].rearrange("p (k s) -> p k s", k=KT)
                s.activation(xT[:, 0, :, i * P:(i + 1) * P], bank, ACT.Copy).then_inc(s_hi, 1)

            k = Banks(s, plan_pro, 0)
            for i in range(BT):
                x2T_hi(k, i)

            def body(b, plan, last):
                k = Banks(s, plan, b)

                def h0_hi(m):
                    s.wait_ge(s_h0, b * KT + (m + 1))
                    s.activation(hT[:, 0, m, :], wave[:, m % 2, :], ACT.Copy).then_inc(s_h0hi, 1)

                def sine(m):
                    k.wait_drained(("ph", m))
                    s.activation(wave[:, m % 2, :], wave[:, m % 2, :], ACT.Abs, bias=angles[:, 1:2]).then_inc(s_u, 1)
                    s.wait_ge(s_u, b * KT + (m + 1))
                    s.activation(wave[:, m % 2, :], wave[:, m % 2, :], ACT.Sin, bias=angles[:, 0:1], scale=-PI).then_inc(s_sin, 1)

                for m in range(KT):
                    if m >= 2:
                        s.wait_ge(s_h0lo, b * KT + (m - 1))
                    k.wait_full(("amp", m))
                    k.drain(("amp", m), s.activation(amp[:, m % 2, :], banks[plan.bank(("amp", m))][:, :], ACT.Tanh, bias=half_ampb[:, m:m + 1], scale=0.5))
                    k.wait_full(("ph", m))
                    k.drain(("ph", m), s.activation(wave[:, m % 2, :], banks[plan.bank(("ph", m))][:, :], ACT.Tanh, bias=cols[:, KT + m:KT + m + 1]))
                    sine(m)
                    h0_hi(m)
                if not last:
                    for i in range(BT):
                        x2T_hi(k, i)
                for u in range(UN - BT):
                    k.wait_full(("tr", u))
                    if u >= 2:
                        s.wait_ge(s_hlo, b * (UN - BT) + (u - 1))
                    bank = banks[plan.bank(("tr", u))]
                    for c in range(KT):
                        ins = s.activation(ht[:, u % 2, c, :], bank[:, c * P:(c + 1) * P], ACT.Identity,
                                           bias=shift(u // BT, c), scale=gain(u // BT, c))
                    k.drain(("tr", u), ins)

            every_block(s, body)

        @block.vector
        def _(v):
            v.wait_ge(s_cols, 16)
            v.tensor_scalar(half_ampb[:, :], cols[:, 0:KT], 0.5, None, ALU.mult).then_inc(s_c, 1)

            def x2T_lo(k, i, n):
                v.wait_ge(s_hi, n)
                bank = banks[k.plan.bank(("xt", i))][:, :].rearrange("p (k s) -> p k s", k=KT)
                k.drain(("xt", i), v.tensor_tensor(xT[:, 1, :, i * P:(i + 1) * P], bank, xT[:, 0, :, i * P:(i + 1) * P].bitcast(F32), ALU.subtract))

            k = Banks(v, plan_pro, 0)
            for i in range(BT):
                x2T_lo(k, i, i + 1)

            def body(b, plan, last):
                k = Banks(v, plan, b)

                def h0(m):
                    n = b * KT + (m + 1)
                    k.wait_drained(("amp", m))
                    v.tensor_scalar(amp[:, m % 2, :], amp[:, m % 2, :], SQRT_HALF, SQRT_HALF, ALU.mult, ALU.add).then_inc(s_gate, 1)
                    v.wait_ge(s_gate, n)
                    v.wait_ge(s_sin, n)
                    v.tensor_tensor(wave[:, m % 2, :], wave[:, m % 2, :], amp[:, m % 2, :], ALU.mult).then_inc(s_h0, 1)
                    v.wait_ge(s_h0hi, n)
                    v.tensor_tensor(hT[:, 1, m, :], wave[:, m % 2, :], hT[:, 0, m, :].bitcast(F32), ALU.subtract).then_inc(s_h0lo, 1)

                def statistics(i, n):
                    v.bn_stats(stats[:, i, :], y[:, i, :]).then_inc(s_bn, 1)
                    wait_alone(v, s_bn, b * LN + n, s_passed)
                    v.bn_aggr(mv[:, i, :], stats[:, i, :]).then_inc(s_agg, 1)

                def normalise(i, n, s_done):
                    v.wait_ge(s_rstd, b * LN + n)
                    v.tensor_scalar(y[:, i, :], y[:, i, :], mv[:, i, 0:1], rstd[:, i, 1:2], ALU.subtract, ALU.mult).then_inc(s_done, 1)

                def unit(u):
                    s_, i = divmod(u, BT)
                    k.wait_full(("mm", u))
                    if s_ == 0:
                        v.wait_ge(s_out, b * (16 * BT))
                    k.drain(("mm", u), v.tensor_tensor(y[:, i, :], banks[plan.bank(("mm", u))][:, :], bias[:, s_, :], ALU.add))
                    k.wait_drained(("mm", u))
                    statistics(i, u + 1)

                def hi(u):
                    i = u % BT
                    k.wait_drained(("tr", u))
                    v.tensor_copy(hT[:, 0, :, i * P:(i + 1) * P], ht[:, u % 2, :, :]).then_inc(s_hhi, 1)

                def finish(i):
                    v.wait_ge(s_gb, b * BT + (i + 1))
                    v.tensor_tensor(y[:, i, :], y[:, i, :], x2[:, b * BT + i, :], ALU.add).then_inc(s_res, 1)
                    v.wait_ge(s_res, b * BT + (i + 1))
                    statistics(i, UN + i + 1)

                for m in range(KT):
                    h0(m)
                if not last:
                    for i in range(BT):
                        x2T_lo(k, i, b * BT + (BT + i + 1))
                for u in range(UN + 1):
                    if u < UN:
                        unit(u)
                    if u >= 1:
                        normalise((u - 1) % BT, u, s_norm)
                    if 2 <= u < UN - BT + 2:
                        hi(u - 2)
                for i in range(BT):
                    finish(i)
                    if i >= 1:
                        normalise(i - 1, UN + i, s_fin)
                normalise(BT - 1, UN + BT, s_fin)

            every_block(v, body)

        @block.tensor
        def _(t):
            def x2T(k, i):
                k.wait_free(("xt", i))
                for c in range(KT):
                    ins = t.transpose(banks[k.plan.bank(("xt", i))][:, c * P:(c + 1) * P], xb[:, i, c * P:(c + 1) * P], ident[:, :])
                k.filled(("xt", i), ins)

            k = Banks(t, plan_pro, 0)
            t.wait_ge(s_xb, 16)
            for i in range(BT):
                x2T(k, i)
            k.wait_drained(("xt", BT - 1))

            def body(b, plan, last):
                k = Banks(t, plan, b)

                def gate(name, m, off):
                    k.wait_free((name, m))
                    k.filled((name, m), split_products(t, banks[plan.bank((name, m))][:, :],
                                                       lambda h, c: W[:, h, off + c * D + m * P:off + c * D + (m + 1) * P],
                                                       lambda h, c: xT[:, h, c, :], range(KT)))

                for m in range(KT):
                    gate("amp", m, OFF_AMP)
                    gate("ph", m, OFF_PH)
                if not last:
                    t.wait_ge(s_xb, b * 16 + 32)
                    for i in range(BT):
                        x2T(k, i)
                t.wait_ge(s_h0lo, b * KT + KT)
                for u in range(UN + 2):
                    if u < UN:
                        s_, i = divmod(u, BT)
                        off = (OFF_ENT, OFF_PATH)[s_ % 2][s_ // 2]
                        if s_ >= 1:
                            t.wait_ge(s_hlo, b * (UN - BT) + (u - BT + 1))
                        k.wait_free(("mm", u))
                        k.filled(("mm", u), split_products(t, banks[plan.bank(("mm", u))][:, :],
                                                           lambda h, c: hT[:, h, c, i * P:(i + 1) * P],
                                                           lambda h, c: W[:, h, off + c * D:off + (c + 1) * D], range(KT)))
                    if 2 <= u < UN - BT + 2:
                        w = u - 2
                        t.wait_ge(s_norm, b * UN + (w + 1))
                        k.wait_free(("tr", w))
                        for c in range(KT):
                            ins = t.transpose(banks[plan.bank(("tr", w))][:, c * P:(c + 1) * P], y[:, w % BT, c * P:(c + 1) * P], ident[:, :])
                        k.filled(("tr", w), ins)

            every_block(t, body)


def layout(inputs):
    import numpy as np
    a = {k.replace("L0_", ""): np.asarray(v) for k, v in inputs.items()}
    c = np.ascontiguousarray
    x = c(a["x"])
    wq = a["attn_Wq"].reshape(D, NKV, NH // NKV, HD).transpose(0, 2, 1, 3).reshape(D, D)
    wo = a["attn_Wo"].reshape(NKV, NH // NKV, HD, D).transpose(1, 0, 2, 3).reshape(D, D)
    col = lambda v: v.reshape(-1, P).T
    g3, b3, g4, b4 = (a[f"ffn_{n}"] for n in ("ln3_g", "ln3_b", "ln4_g", "ln4_b"))
    return {
        "x": x,
        "xT": c(x.reshape(B * S, D).T),
        "ctxT": c(a["ctx_512"].reshape(B * S, L).T),
        "w_qkv": c(np.concatenate([wq, a["attn_Wk"], a["attn_Wv"]], axis=1)),
        "w_o": c(wo),
        "w_cq": c(a["xattn_Wq"].T),
        "w_ckv": c(a["xattn_Wkv_expand"].T),
        "w_cout": c(a["xattn_Wout"].T),
        "ent_wT": c(a["ffn_ent_w"].transpose(0, 2, 1)),
        "ent_pw": c(a["ffn_ent_pw"]),
        "ent_b": c(a["ffn_ent_b"].reshape(NL, ET, P).transpose(0, 2, 1)),
        "ent_pb": c(a["ffn_ent_pb"]),
        "gate_w": c(np.stack([a["ffn_amp_w"], a["ffn_ph_w"]])),
        "path_w": c(a["ffn_path_w"]),
        "path_b": c(a["ffn_path_b"]),
        "phase": c(a["ffn_phase"]),
        "cols": c(np.concatenate([col(v) for v in (a["ffn_amp_b"], a["ffn_ph_b"], g3[0], b3[0], g4[0], b4[0], g3[1], b3[1])], axis=1)),
        "ln_g": c(g4[1]),
        "ln_b": c(b4[1]),
    }


def kernel(**inputs):
    import concourse.bacc as bacc
    from concourse.bass_utils import run_bass_kernel_spmd

    nc = bacc.Bacc("TRN2", target_bir_lowering=False, num_devices=1)
    arrays = layout(inputs)
    A = {n: nc.dram_tensor(f"in_{n}", v.shape, mybir.dt.from_np(v.dtype), kind="ExternalInput").ap() for n, v in arrays.items()}
    A["out"] = nc.dram_tensor("out", (B, S, D), F32, kind="ExternalOutput").ap()
    build(nc, A)
    r = run_bass_kernel_spmd(nc, [{f"in_{n}": v for n, v in arrays.items()}], core_ids=[0])
    return r.results[0]["out"]
```

```python
from contextlib import ExitStack

import concourse.bass as bass
from concourse import mybir

F32 = mybir.dt.float32
F32R = mybir.dt.float32r
BF16 = mybir.dt.bfloat16
ALU = mybir.AluOpType
ACT = mybir.ActivationFunctionType
AX = mybir.AxisListType

P = 128
B, S, D = 8, 256, 512
L = 128
NH, HD = 16, 32
NKV = 4
KT = D // P
TT = S // P
HG = P // HD
NG = NH // HG
EW = 4 * D
ET = EW // P
NL, NP = 2, 2
BT = 4
NB = B * S // (BT * P)
EPS = 1e-5
SCALE = HD ** -0.5
MASKED = -1e30
SQRT_HALF = 0.5 ** 0.5
PI = 3.141592653589793

KV = NKV * HD
OFF_K = 0
OFF_V = OFF_K + KT * KV
OFF_Q = OFF_V + KT * KV
OFF_CKV = OFF_Q + KT * D
OFF_WO = OFF_CKV + 2 * D
OFF_CQ = OFF_WO + KT * D
OFF_COUT = OFF_CQ + KT * D
W_ATT = OFF_COUT + KT * D
OFF_AMP, OFF_PH = 0, KT * D
OFF_ENT = [2 * KT * D, 4 * KT * D]
OFF_PATH = [3 * KT * D, 5 * KT * D]
W_FFN = 6 * KT * D


class Plan:

    def __init__(self, full, drained, s_hi=None):
        self.full, self.drained = full + [s_hi], drained + [None]
        self.base = [1] * len(self.full)
        self.count = [0] * len(self.full)
        self.per = [0] * len(self.full)
        self.at = {}
        self.ring = 0

    def after(self, it=0):
        p = Plan(self.full[:-1], self.drained[:-1], self.full[-1])
        p.base = [b + it * n + c for b, n, c in zip(self.base, self.per, self.count)]
        p.ring = self.ring
        return p

    def loop(self):
        self.per = list(self.count)
        return self

    def take(self, name, bank):
        self.count[bank] += 1
        self.at[name] = (bank, self.count[bank])

    def take_hi(self, name):
        self.take(("hi", name), len(self.full) - 1)

    def bank(self, name):
        return self.at[name][0]

    def value(self, it, name):
        bank, k = self.at[name]
        return it * self.per[bank] + (self.base[bank] + k)

    def begin(self, eng):
        for sem in self.full + self.drained:
            if sem is not None:
                eng.sem_inc(sem, 1)


class Banks:

    def __init__(self, eng, plan, it):
        self.eng, self.plan, self.it = eng, plan, it

    def wait_free(self, name):
        self.eng.wait_ge(self.plan.drained[self.plan.bank(name)], self.plan.value(self.it, name) - 1)

    def wait_full(self, name):
        self.eng.wait_ge(self.plan.full[self.plan.bank(name)], self.plan.value(self.it, name))

    def wait_hi(self, name):
        self.wait_full(("hi", name))

    def wait_drained(self, name):
        self.eng.wait_ge(self.plan.drained[self.plan.bank(name)], self.plan.value(self.it, name))

    def filled(self, name, ins):
        ins.then_inc(self.plan.full[self.plan.bank(name)], 1)

    def drain(self, name, ins):
        ins.then_inc(self.plan.drained[self.plan.bank(name)], 1)



def groups_of(cross, nxt):
    return (list(range(NG)) if cross else []) + (list(range(NG, 2 * NG)) if nxt else [])


def schedule(cross, nxt, proj):
    n = len(groups_of(cross, nxt))
    ev = []
    if cross:
        ev += [("ck", 0), ("ck", 1), ("wo", 0), ("wo", 1)]
    if nxt:
        ev += [("sv", 0), ("sv", 1)]
    if cross:
        ev += [("x1t", 0)]
    if nxt:
        ev += [("sq", 1)]
    if cross:
        ev += [("x1t", 1)]
    if nxt:
        ev += [("sq", 2)]
    if cross:
        ev += [("cq", 0), ("cq", 1)]
    for i in range(n + 2):
        ev.append(("step", i))
        if i == 0 and cross:
            ev += [("cq", 2), ("cq", 3), ("ck", 2), ("ck", 3)] + [("cv", t) for t in range(TT)]
        if i == 0 and nxt:
            ev.append(("sq", 3))
        if i == 0 and not cross:
            ev.append(("weights", 0))
        if i == 1 and not cross:
            ev.append(("weights", 1))
        if i == n - 2 and cross and nxt:
            ev.append(("wout", 0))
        if i == n - 1 and cross and nxt:
            ev.append(("wout", 1))
        if i == n and proj:
            ev.append(("sk", 0))
    if cross and not nxt:
        ev += [("wout", 0), ("wout", 1)]
    if proj:
        ev.append(("sq", 0))
    return ev


N_RING = 5
T_BANKS, O_BANK = (5, 6), 7
SPLIT = ("sk", "sq", "ck", "x1t", "cq")


def attention_plan(plan, cross, nxt, proj):
    def ring(name):
        plan.take(name, plan.ring % N_RING)
        plan.ring += 1

    n = len(groups_of(cross, nxt))
    for kind, i in schedule(cross, nxt, proj):
        if kind == "step":
            if i < n:
                for j in range(HG):
                    ring(("S", i, j))
            for js in ((0, 1), (2, 3)):
                if 1 <= i <= n:
                    for j in js:
                        plan.take(("T", i - 1, j), T_BANKS[j % 2])
                if i >= 2 and js[0] == 0:
                    plan.take(("O", i - 2), O_BANK)
        elif kind != "weights":
            ring((kind, i))
            if kind in SPLIT:
                plan.take_hi((kind, i))
    return plan


def wait_alone(eng, sem, value, s_passed):
    eng.wait_ge(sem, value)
    eng.sem_inc(s_passed, 1)


def split_products(t, out, lhs, rhs, kts, first=True, last=True):
    for n, k in enumerate(kts):
        for m, (a, b) in enumerate(((0, 0), (0, 1), (1, 0))):
            ins = t.matmul(out, lhs(a, k), rhs(b, k), start=first and n == 0 and m == 0,
                           stop=last and n == len(kts) - 1 and m == 2, skip_group_check=True)
    return ins


def build(nc, A):
    with ExitStack() as whole:
        def sem(name):
            return whole.enter_context(nc.semaphore(name))

        def sb(ctx, name, shape, dt=F32):
            return ctx.enter_context(nc.sbuf_tensor(name, shape, dt))

        banks = [whole.enter_context(nc.psum_tensor(f"bank{i}", [P, 512], F32)) for i in range(8)]
        x2 = sb(whole, "x2", [P, B * TT, D])
        ident = sb(whole, "ident", [P, P])
        ident16 = sb(whole, "ident16", [P, P], BF16)
        mask16 = sb(whole, "mask16", [P, 2, P], BF16)
        s_const, s_passed = sem("s_const"), sem("s_passed")
        with ExitStack() as ctx:
            attention_phase(nc, ctx, sb, sem, A, banks, x2, ident, ident16, mask16, s_const, s_passed)
        with ExitStack() as ctx:
            W = sb(ctx, "w_ffn", [P, 2, W_FFN], F32R)
            bias = sb(ctx, "stage_bias", [P, 2 * NL, D])
            with ExitStack() as inner:
                fusion_phase(nc, inner, sb, sem, A, banks, W, bias, s_passed)
            with ExitStack() as inner:
                ffn_phase(nc, inner, sb, sem, A, banks, W, bias, x2, ident, s_passed)


def attention_phase(nc, ctx, sb, sem, A, banks, x2, ident, ident16, mask16, s_const, s_passed):
    W = sb(ctx, "w_att", [P, 2, W_ATT], F32R)
    xT_raw = x2[:, (B - 1) * TT:, :].rearrange("p t (k s) -> p (t k) s", k=KT // TT)
    xT = sb(ctx, "xT", [P, 2, KT, S], F32R)
    ctx_raw = sb(ctx, "ctx_raw", [P, S])
    ctxT = sb(ctx, "ctxT", [P, 2, S], F32R)
    sqT = sb(ctx, "sqT", [P, 2, NG, S], F32R)
    skT = sb(ctx, "skT", [P, 2, S], F32R)
    sv = sb(ctx, "sv", [P, TT, KV])
    cqT = sb(ctx, "cqT", [P, 2, NG, S], F32R)
    ckT = sb(ctx, "ckT", [P, 2, NG, S], F32R)
    cv = sb(ctx, "cv", [P, TT, D])
    PW = S // 2 + S
    RING = 2 * HG
    prob = sb(ctx, "prob", [P, RING, PW])
    probT = sb(ctx, "probT", [P, RING, PW])
    nmax = sb(ctx, "nmax", [P, RING, TT])
    den = sb(ctx, "den", [P, 2, HG, TT])
    rden = sb(ctx, "rden", [P, 2, HG, TT])
    rwide = sb(ctx, "rwide", [P, 2, TT, P])
    rT = sb(ctx, "rT", [P, 2, S])
    o32 = sb(ctx, "o32", [P, 2, S])
    oT_self = sb(ctx, "oT_self", [P, 2, NG, S], F32R)
    oT_cross = sb(ctx, "oT_cross", [P, 2, NG, S], F32R)
    x1T = oT_self
    xres = sb(ctx, "xres", [P, TT, D])
    stats = sb(ctx, "stats", [P, TT, 6])
    mv = sb(ctx, "mv", [P, TT, 2])
    rstd = sb(ctx, "rstd", [P, TT, 2])
    half = sb(ctx, "half", [P, 1])

    s_xT, s_ctx, s_x = sem("s_xT"), sem("s_ctx"), sem("s_x")
    s_x0 = sem("s_x0")
    s_xh, s_xs = sem("s_xh"), sem("s_xs")
    s_ch, s_cs = sem("s_ch"), sem("s_cs")
    s_hi = sem("s_hi")
    s_max = sem("s_max")
    s_rden, s_wide = sem("s_rden"), sem("s_wide_r")
    s_rT = sem("s_rT")
    s_oh, s_os = sem("s_oh"), sem("s_os")
    s_bn, s_agg = sem("s_bn"), sem("s_agg")
    s_var, s_rstd = sem("s_var"), sem("s_rstd")
    s_norm = sem("s_norm")
    full = [sem(f"s1_full{i}") for i in range(8)]
    drained = [sem(f"s1_drained{i}") for i in range(8)]

    PRO = [("sk", 0), ("sq", 0)]
    plan_pro = Plan(full, drained, s_hi)
    for n, name in enumerate(PRO):
        plan_pro.take(name, n)
        plan_pro.take_hi(name)
    FIRST, LOOP, SECOND_LAST, LAST = (0, 1, 1), (1, 1, 1), (1, 1, 0), (1, 0, 0)
    plan_first = attention_plan(plan_pro.after(), *FIRST)
    plan_loop = plan_first.after()
    plan_loop.ring = 0
    attention_plan(plan_loop, *LOOP).loop()
    plan_6 = plan_loop.after(B - 3)
    plan_6.ring = 0
    attention_plan(plan_6, *SECOND_LAST)
    plan_7 = plan_6.after()
    attention_plan(plan_7, *LAST)

    def every_iteration(eng, body):
        body(-1, plan_first, *FIRST)
        with eng.Fori(0, B - 2) as b:
            body(b, plan_loop, *LOOP)
        body(B - 2, plan_6, *SECOND_LAST)
        body(B - 1, plan_7, *LAST)

    def group_number(b, groups, i):
        return b * (2 * NG) + (NG + groups[i] + 1)

    x2f = x2[:, :, :].rearrange("p t d -> p (t d)")
    prf = prob[:, :, :].rearrange("p t d -> p (t d)")
    matrices = [(OFF_K, prf[:, 0:KT * KV], A["w_k"]),
                (OFF_Q, prf[:, 2 * KT * KV:2 * KT * KV + KT * D], A["w_q"]),
                (OFF_V, prf[:, KT * KV:2 * KT * KV], A["w_v"]),
                (OFF_CKV, x2f[:, 3 * KT * D:3 * KT * D + 2 * D], A["w_ckv"]),
                (OFF_WO, x2f[:, 0:KT * D], A["w_o"]),
                (OFF_CQ, x2f[:, KT * D:2 * KT * D], A["w_cq"]),
                (OFF_COUT, x2f[:, 2 * KT * D:3 * KT * D], A["w_cout"])]
    s_wraw = [sem(f"s_wraw{i}") for i in range(len(matrices))]
    s_whi, s_wlo = sem("s_whi"), sem("s_wlo")
    pieces = [(n, off + c, src[:, c:c + D]) for n, (off, src, _) in enumerate(matrices) for c in range(0, src.shape[1], D)]
    KEYS, QUERIES, VALUES = 1, 1 + KT, 2 + KT
    LOTS = [(0, KEYS), (KEYS, VALUES), (VALUES, VALUES + 6), (VALUES + 6, len(pieces))]

    with nc.Block() as block:
        @block.sync
        def _(q):
            xT_of = A["xT"].rearrange("(k p) (b s) -> b p k s", p=P, b=B)
            ctx_of = A["ctxT"].rearrange("p (b s) -> b p s", b=B)
            x_of = A["x"].rearrange("b (t p) d -> b p t d", p=P)

            def load(what, b):
                dst, src, s_ = {"xT": (xT_raw[:, :, :], xT_of, s_xT), "ctx": (ctx_raw[:, :], ctx_of, s_ctx),
                                "x": (xres[:, :, :], x_of, s_x)}[what]
                q.dma_start(dst, src[b]).then_inc(s_, 16)

            def load_weights(n):
                _, dst, src = matrices[n]
                k = dst.shape[1] // src.shape[1]
                q.dma_start(dst.rearrange("p (k n) -> p k n", k=k), src.rearrange("(k p) n -> p k n", p=P)).then_inc(s_wraw[n], 16)

            load("xT", 0)
            load_weights(0)
            load_weights(1)
            load_weights(2)
            q.wait_ge(s_xs, 1)
            load("xT", 1)
            load("ctx", 0)
            for n in range(3, len(matrices)):
                load_weights(n)
            load("x", 0)

            def next_loads(b, last):
                wait_alone(q, s_cs, b + 1, s_passed)
                load("ctx", b + 1)
                if not last:
                    wait_alone(q, s_xs, b + 2, s_passed)
                    load("xT", b + 2)
                wait_alone(q, s_norm, b * (2 * TT) + 2 * TT, s_passed)
                load("x", b + 1)

            with q.Fori(0, B - 2) as b:
                next_loads(b, False)
            next_loads(B - 2, True)

        @block.gpsimd
        def _(g):
            plan_pro.begin(g)
            g.memset(ident[:, :], 0.0).then_inc(s_const, 1)
            g.memset(ident16[:, :], 0.0).then_inc(s_const, 1)
            g.memset(mask16[:, :, :], 0.0).then_inc(s_const, 1)
            g.memset(half[:, :], -0.5).then_inc(s_const, 1)
            g.wait_ge(s_const, 4)
            for m in (ident, ident16):
                g.affine_select(out=m[:, :], in_=m[:, :], compare_op=ALU.not_equal, fill=1.0, base=0,
                                pattern=[[-1, P]], channel_multiplier=1).then_inc(s_const, 1)
            g.affine_select(out=mask16[:, :, :], in_=mask16[:, :, :], compare_op=ALU.is_ge, fill=MASKED, base=0,
                            pattern=[[0, 2], [-1, P]], channel_multiplier=1).then_inc(s_const, 1)

            def split(hi, lo, raw, s_h, s_l, n):
                g.tensor_scalar(hi, raw, 1.0, 1.0, ALU.mult, ALU.mult).then_inc(s_h, 1)
                g.wait_ge(s_h, n)
                g.tensor_tensor(lo, raw, hi.bitcast(F32), ALU.subtract).then_inc(s_l, 1)

            def split_x(b):
                wait_alone(g, s_xT, b * 16 + 16, s_passed)
                split(xT[:, 0, :, :], xT[:, 1, :, :], xT_raw[:, :, :], s_xh, s_xs, b)

            def split_ctx(b):
                wait_alone(g, s_ctx, b * 16 + 16, s_passed)
                split(ctxT[:, 0, :], ctxT[:, 1, :], ctx_raw[:, :], s_ch, s_cs, b + 1)

            def body(b, plan, cross, nxt, proj):
                k = Banks(g, plan, b)
                groups = groups_of(cross, nxt)

                def copies(i):
                    n = group_number(b, groups, i)
                    wait_alone(g, s_rden, n, s_passed)
                    src = rden[:, i % 2, :, :].rearrange("p (j o) t -> p t j o", o=1).broadcast_to([P, TT, HG, HD])
                    g.tensor_scalar(rwide[:, i % 2, :, :].rearrange("p t (j d) -> p t j d", j=HG), src, 1.0, 1.0, ALU.mult, ALU.mult).then_inc(s_wide, 1)

                def split_output(i):
                    k.wait_drained(("O", i))
                    g.sem_inc(s_passed, 1)
                    oT = oT_cross if groups[i] < NG else oT_self
                    t = groups[i] % NG
                    split(oT[:, 0, t, :], oT[:, 1, t, :], o32[:, i % 2, :], s_oh, s_os, group_number(b, groups, i))

                def rstd_of(ai, i):
                    n = b * (2 * TT) + (ai * TT + i + 1)
                    wait_alone(g, s_agg, n, s_passed)
                    g.tensor_scalar(rstd[:, i, 0:1], mv[:, i, 1:2], EPS, None, ALU.add).then_inc(s_var, 1)
                    g.wait_ge(s_var, n)
                    g.tensor_tensor(rstd[:, i, 1:2], rstd[:, i, 0:1], half[:, :], ALU.pow).then_inc(s_rstd, 1)

                for kind, i in schedule(cross, nxt, proj):
                    if kind == "wo":
                        rstd_of(0, i)
                    elif kind == "wout":
                        rstd_of(1, i)
                    elif kind == "step":
                        if 1 <= i <= len(groups):
                            copies(i - 1)
                        if i >= 2:
                            split_output(i - 2)
                    elif (kind, i) == ("sq", KT - 1) and proj:
                        k.wait_full((kind, i))
                        split_x(b + 2)
                        if not cross:
                            split_ctx(0)
                    elif (kind, i) == ("cv", TT - 1) and nxt:
                        k.wait_full((kind, i))
                        split_ctx(b + 1)

            every_iteration(g, body)

        @block.scalar
        def _(s):
            def weights(lot):
                for n, off, raw in pieces[slice(*lot)]:
                    s.wait_ge(s_wraw[n], 16)
                    s.activation(W[:, 0, off:off + D], raw, ACT.Copy).then_inc(s_whi, 1)

            def hi(k, name, out, scale=1.0):
                k.wait_full(name)
                src = banks[k.plan.bank(name)][:, 0:512 if len(out.shape) == 3 else S]
                if len(out.shape) == 3:
                    src = src.rearrange("p (k s) -> p k s", k=KT)
                s.activation(out, src, ACT.Copy, scale=scale).then_inc(s_hi, 1)

            def values(k, name, out):
                k.wait_full(name)
                k.drain(name, s.activation(out, banks[k.plan.bank(name)][:, 0:out.shape[1]], ACT.Copy))

            def projection(k, kind, i):
                if kind == "sk":
                    hi(k, (kind, i), skT[:, 0, :])
                elif kind == "sq":
                    hi(k, (kind, i), sqT[:, 0, i, :], SCALE)
                elif kind == "ck":
                    hi(k, (kind, i), ckT[:, 0, i, :])
                elif kind == "cq":
                    hi(k, (kind, i), cqT[:, 0, i, :], SCALE)
                elif kind == "x1t":
                    hi(k, (kind, i), x1T[:, 0, :, i * P:(i + 1) * P])
                elif kind == "sv":
                    values(k, (kind, i), sv[:, i, :])
                elif kind == "cv":
                    values(k, (kind, i), cv[:, i, :])

            s.wait_ge(s_xT, 16)
            s.activation(xT[:, 0, :, :], xT_raw[:, :, :], ACT.Copy).then_inc(s_x0, 1)
            weights(LOTS[0])
            k = Banks(s, plan_pro, 0)
            weights(LOTS[1])
            projection(k, "sk", 0)
            projection(k, "sq", 0)

            def body(b, plan, cross, nxt, proj):
                k = Banks(s, plan, b)
                groups = groups_of(cross, nxt)

                def step(i):
                    if 1 <= i <= len(groups):
                        k.wait_full(("T", i - 1, 0))
                        k.drain(("T", i - 1, 0), s.activation(probT[:, ((i - 1) % 2) * HG, :], banks[plan.bank(("T", i - 1, 0))][:, 0:PW], ACT.Copy))
                    if i >= len(groups):
                        return
                    for j in range(HG):
                        slot = (i % 2) * HG + j
                        s.wait_ge(s_max, b * (2 * NG * HG) + (NG + groups[i]) * HG + j + 1)
                        bank = banks[plan.bank(("S", i, j))]
                        s.activation(prob[:, slot, 0:P], bank[:, 0:P], ACT.Exp, bias=nmax[:, slot, 0:1], accum_out=den[:, i % 2, j, 0:1])
                        k.drain(("S", i, j), s.activation(prob[:, slot, P:PW], bank[:, P:PW], ACT.Exp, bias=nmax[:, slot, 1:2],
                                                          accum_out=den[:, i % 2, j, 1:2]))

                for kind, i in schedule(cross, nxt, proj):
                    if kind == "step":
                        step(i)
                    elif kind == "weights":
                        weights(LOTS[2 + i])
                    else:
                        projection(k, kind, i)

            every_iteration(s, body)

        @block.vector
        def _(v):
            def weights(lot):
                for i in range(*lot):
                    _, off, raw = pieces[i]
                    v.wait_ge(s_whi, i + 1)
                    v.tensor_tensor(W[:, 1, off:off + D], raw, W[:, 0, off:off + D].bitcast(F32), ALU.subtract).then_inc(s_wlo, 1)

            def lo(k, name, hi, out, scale=1.0):
                k.wait_hi(name)
                src = banks[k.plan.bank(name)][:, 0:512 if len(out.shape) == 3 else S]
                if len(out.shape) == 3:
                    src = src.rearrange("p (k s) -> p k s", k=KT)
                k.drain(name, v.scalar_tensor_tensor(out, src, scale, hi.bitcast(F32), ALU.mult, ALU.subtract))

            def projection(k, kind, i):
                if kind == "sk":
                    lo(k, (kind, i), skT[:, 0, :], skT[:, 1, :])
                elif kind == "sq":
                    lo(k, (kind, i), sqT[:, 0, i, :], sqT[:, 1, i, :], SCALE)
                elif kind == "ck":
                    lo(k, (kind, i), ckT[:, 0, i, :], ckT[:, 1, i, :])
                elif kind == "cq":
                    lo(k, (kind, i), cqT[:, 0, i, :], cqT[:, 1, i, :], SCALE)
                elif kind == "x1t":
                    lo(k, (kind, i), x1T[:, 0, :, i * P:(i + 1) * P], x1T[:, 1, :, i * P:(i + 1) * P])

            v.wait_ge(s_x0, 1)
            v.tensor_tensor(xT[:, 1, :, :], xT_raw[:, :, :], xT[:, 0, :, :].bitcast(F32), ALU.subtract).then_inc(s_xs, 1)
            weights(LOTS[0])
            k = Banks(v, plan_pro, 0)
            weights(LOTS[1])
            projection(k, "sk", 0)
            projection(k, "sq", 0)

            def body(b, plan, cross, nxt, proj):
                k = Banks(v, plan, b)
                groups = groups_of(cross, nxt)

                def maxima(i, j):
                    slot = (i % 2) * HG + j
                    k.wait_full(("S", i, j))
                    bank = banks[plan.bank(("S", i, j))]
                    v.tensor_reduce(nmax[:, slot, 0:1], bank[:, 0:P], AX.X, ALU.max, negate=True)
                    v.tensor_reduce(nmax[:, slot, 1:2], bank[:, P:PW], AX.X, ALU.max, negate=True).then_inc(s_max, 1)

                def probT_tile(i, j):
                    k.wait_full(("T", i, j))
                    k.drain(("T", i, j), v.tensor_copy(probT[:, (i % 2) * HG + j, :], banks[plan.bank(("T", i, j))][:, 0:PW]))

                def reciprocals(i):
                    k.wait_drained(("S", i, HG - 1))
                    v.reciprocal(rden[:, i % 2, :, :], den[:, i % 2, :, :]).then_inc(s_rden, 1)

                def output(i):
                    n = group_number(b, groups, i)
                    k.wait_full(("O", i))
                    bank = banks[plan.bank(("O", i))]
                    v.tensor_copy(rT[:, i % 2, :], bank[:, S:2 * S]).then_inc(s_rT, 1)
                    v.wait_ge(s_rT, n)
                    if i >= 2:
                        v.wait_ge(s_os, n - 2)
                    k.drain(("O", i), v.tensor_tensor(o32[:, i % 2, :], bank[:, 0:S], rT[:, i % 2, :], ALU.mult))

                def step(i):
                    n = len(groups)
                    if i < n:
                        maxima(i, 0)
                    if 1 <= i <= n:
                        probT_tile(i - 1, 1)
                    if i < n:
                        for j in range(1, HG):
                            maxima(i, j)
                    if 1 <= i <= n:
                        reciprocals(i - 1)
                    if i >= 2:
                        output(i - 2)
                    if 1 <= i <= n:
                        probT_tile(i - 1, 2)
                        probT_tile(i - 1, 3)

                def add_and_measure(ai, i):
                    name, n = (("wo", "wout")[ai], i), b * (2 * TT) + (ai * TT + i + 1)
                    k.wait_full(name)
                    if ai == 0:
                        v.wait_ge(s_x, b * 16 + 16)
                    else:
                        v.wait_ge(s_norm, b * (2 * TT) + (i + 1))
                    k.drain(name, v.tensor_tensor(xres[:, i, :], banks[plan.bank(name)][:, :], xres[:, i, :], ALU.add))
                    k.wait_drained(name)
                    v.bn_stats(stats[:, i, :], xres[:, i, :]).then_inc(s_bn, 1)
                    wait_alone(v, s_bn, n, s_passed)
                    v.bn_aggr(mv[:, i, :], stats[:, i, :]).then_inc(s_agg, 1)

                def normalise(ai, i, out):
                    v.wait_ge(s_rstd, b * (2 * TT) + (ai * TT + i + 1))
                    v.tensor_scalar(out, xres[:, i, :], mv[:, i, 0:1], rstd[:, i, 1:2], ALU.subtract, ALU.mult).then_inc(s_norm, 1)

                ready = None
                for kind, i in schedule(cross, nxt, proj):
                    if kind == "step":
                        step(i)
                    elif kind == "weights":
                        weights(LOTS[2 + i])
                    elif kind == "wo":
                        add_and_measure(0, i)
                        normalise(0, i, xres[:, i, :])
                    elif kind == "wout":
                        add_and_measure(1, i)
                    else:
                        projection(k, kind, i)
                    if ready is not None:
                        normalise(1, ready, x2[:, b * TT + ready, :])
                    ready = i if kind == "wout" else None
                if ready is not None:
                    normalise(1, ready, x2[:, b * TT + ready, :])

            every_iteration(v, body)
            v.wait_ge(s_norm, B * 2 * TT)

        @block.tensor
        def _(t):
            def feature_major(k, name, w, src, kts):
                k.wait_free(name)
                k.filled(name, split_products(t, banks[k.plan.bank(name)][:, 0:S], w, src, kts))

            def token_major(k, name, src, w, kts, width):
                k.wait_free(name)
                k.filled(name, split_products(t, banks[k.plan.bank(name)][:, 0:width], src, w, kts))

            def weight(off, h, row, first, n):
                return W[:, h, off + row * D + first:off + row * D + first + n]

            def projection(k, kind, i):
                name, tok = (kind, i), slice(i * P, (i + 1) * P)
                if kind == "sk":
                    feature_major(k, name, lambda h, c: W[:, h, OFF_K + c * KV:OFF_K + (c + 1) * KV], lambda h, c: xT[:, h, c, :], range(KT))
                elif kind == "sv":
                    token_major(k, name, lambda h, c: xT[:, h, c, tok], lambda h, c: W[:, h, OFF_V + c * KV:OFF_V + (c + 1) * KV], range(KT), KV)
                elif kind == "sq":
                    feature_major(k, name, lambda h, c: weight(OFF_Q, h, c, i * P, P), lambda h, c: xT[:, h, c, :], range(KT))
                elif kind == "ck":
                    feature_major(k, name, lambda h, c: weight(OFF_CKV, h, 0, i * P, P), lambda h, c: ctxT[:, h, :], [0])
                elif kind == "cv":
                    token_major(k, name, lambda h, c: ctxT[:, h, tok], lambda h, c: weight(OFF_CKV, h, 1, 0, D), [0], D)
                elif kind == "cq":
                    feature_major(k, name, lambda h, c: weight(OFF_CQ, h, c, i * P, P), lambda h, c: x1T[:, h, c, :], range(KT))

            k = Banks(t, plan_pro, 0)
            t.wait_ge(s_xs, 1)
            t.wait_ge(s_wlo, KEYS)
            projection(k, "sk", 0)
            t.wait_ge(s_wlo, QUERIES)
            projection(k, "sq", 0)
            t.wait_ge(s_wlo, VALUES)
            t.wait_ge(s_const, 7)

            def body(b, plan, cross, nxt, proj):
                k = Banks(t, plan, b)
                groups = groups_of(cross, nxt)

                def scores(i):
                    g = groups[i] % NG
                    qT, kT = (cqT, lambda h: ckT[:, h, g, :]) if groups[i] < NG else (sqT, lambda h: skT[:, h, :])
                    if groups[i] < NG:
                        k.wait_drained(("cq", g))
                        k.wait_drained(("ck", g))
                    elif g > 0:
                        k.wait_drained(("sq", g))
                    bank = [banks[plan.bank(("S", i, j))] for j in range(HG)]
                    for j in range(HG):
                        k.wait_free(("S", i, j))
                        diag = bank[j][:, :].rearrange("p (a b c) -> p a b c", a=2, b=2)[:, :, 0, :]
                        t.matmul(diag, ident16[:, :], mask16[:, :, :], start=True, stop=False, skip_group_check=True)
                    for qt in range(TT):
                        for m, (x, y) in enumerate(((0, 0), (0, 1), (1, 0))):
                            for j in range(HG):
                                rows = slice(HD * j, HD * (j + 1))
                                ins = t.matmul(bank[j][:, P * qt:P * qt + P * (qt + 1)], qT[rows, x, g, qt * P:(qt + 1) * P],
                                               kT(y)[rows, 0:P * (qt + 1)], start=False, stop=qt == TT - 1 and m == 2, skip_group_check=True)
                                if qt == TT - 1 and m == 2:
                                    k.filled(("S", i, j), ins)

                def transposes(i, j):
                    k.wait_drained(("S", i, j))
                    k.wait_free(("T", i, j))
                    bank = banks[plan.bank(("T", i, j))]
                    for c in range(3):
                        ins = t.transpose(bank[:, c * P:(c + 1) * P], prob[:, (i % 2) * HG + j, c * P:(c + 1) * P], ident[:, :])
                    k.filled(("T", i, j), ins)

                def outputs(i):
                    g = groups[i] % NG
                    k.wait_free(("O", i))
                    bank = banks[O_BANK]
                    for j in range(HG):
                        k.wait_drained(("T", i, j))
                    for kt in range(2):
                        for j in range(HG):
                            v_ = cv[:, kt, HD * (HG * g + j):HD * (HG * g + j + 1)] if groups[i] < NG else sv[:, kt, HD * j:HD * (j + 1)]
                            t.matmul(bank[HD * j:HD * (j + 1), kt * P:S], v_, probT[:, (i % 2) * HG + j, kt * S:S + kt * P],
                                     start=kt == 0, stop=kt == 1, skip_group_check=True)
                    t.wait_ge(s_wide, group_number(b, groups, i))
                    for qt in range(TT):
                        ins = t.transpose(bank[:, S + qt * P:S + (qt + 1) * P], rwide[:, i % 2, qt, :], ident[:, :])
                    k.filled(("O", i), ins)

                def project_out(ai, i):
                    name, off, oT = ((("wo", i), OFF_WO, oT_self), (("wout", i), OFF_COUT, oT_cross))[ai]
                    k.wait_free(name)
                    for c in range(KT):
                        if i == 0:
                            t.wait_ge(s_os, b * (2 * NG) + (ai * NG + c + 1))
                        ins = split_products(t, banks[plan.bank(name)][:, :], lambda h, c: oT[:, h, c, i * P:(i + 1) * P],
                                             lambda h, c: weight(off, h, c, 0, D), [c], first=c == 0, last=c == KT - 1)
                    k.filled(name, ins)

                for kind, i in schedule(cross, nxt, proj):
                    if kind == "step":
                        if i < len(groups):
                            scores(i)
                        if 1 <= i <= len(groups):
                            transposes(i - 1, 0)
                            transposes(i - 1, 1)
                        if i >= 2:
                            outputs(i - 2)
                        if 1 <= i <= len(groups):
                            transposes(i - 1, 2)
                            transposes(i - 1, 3)
                    elif kind == "wo":
                        project_out(0, i)
                    elif kind == "wout":
                        project_out(1, i)
                    elif kind == "x1t":
                        t.wait_ge(s_norm, b * (2 * TT) + (i + 1))
                        k.wait_free((kind, i))
                        for c in range(KT):
                            ins = t.transpose(banks[plan.bank((kind, i))][:, c * P:(c + 1) * P], xres[:, i, c * P:(c + 1) * P], ident[:, :])
                        k.filled((kind, i), ins)
                    elif kind != "weights":
                        if (kind, i) == ("ck", 0):
                            t.wait_ge(s_cs, b + 1)
                            t.wait_ge(s_wlo, len(pieces))
                        if (kind, i) == ("sk", 0):
                            t.wait_ge(s_xs, b + 3)
                        if (kind, i) == ("cq", 0):
                            for u in range(TT):
                                k.wait_drained(("x1t", u))
                        projection(k, kind, i)

            every_iteration(t, body)


def fusion_phase(nc, ctx, sb, sem, A, banks, W, bias, s_passed):
    R, HR = 4, 2
    raw = sb(ctx, "raw", [P, R, 2, D])
    tile = sb(ctx, "tile", [P, HR, 2, 2, D], F32R)
    aux = sb(ctx, "aux", [P, 2, NP, D])
    ones = sb(ctx, "ones", [P, P])
    prod = sb(ctx, "prod", [P, D])
    acc = sb(ctx, "acc", [P, D])
    t32 = sb(ctx, "t32", [P, 2, D])
    mod = sb(ctx, "mod", [P, NP, D])
    pbias = sb(ctx, "pbias", [P, NP, D])
    ebias = sb(ctx, "ebias", [P, D])
    eb = sb(ctx, "eb", [P, ET])
    wide = sb(ctx, "wide", [P, (2 * KT - 1) * P])
    s_raw = [sem(f"s_raw{i}") for i in range(R)]
    s_aux = [sem("s_aux0"), sem("s_aux1")]
    s_small = sem("s_small")
    s_wide = sem("s_wide")
    s_hi, s_lo = sem("s2_hi"), sem("s2_lo")
    s_tile = sem("s2_tile")
    s_prod, s_acc = sem("s2_prod"), sem("s2_acc")
    s_mod = sem("s2_mod")
    s_sin = sem("s2_sin")
    s_whi = sem("s2_whi")
    s_t32 = sem("s2_t32")
    s_wlo = sem("s2_wlo")
    s_sum = sem("s2_sum")
    full = [sem(f"s2_full{i}") for i in range(KT + 1)]
    drained = [sem(f"s2_drained{i}") for i in range(KT + 1)]
    layers = W[:, :, 2 * KT * D:].rearrange("p h (l z c) -> p h l z c", l=NL, z=2)
    gates = W[:, :, 0:2 * KT * D].rearrange("p h (l c) -> p h l c", l=2)
    MOD_LINKS, SUM_LINKS = 8, 2 * KT + 2
    AUX = 2 * KT
    FIN = 2 * KT

    def identity(m):
        return wide[:, (KT - 1 - m) * P:(2 * KT - 1 - m) * P]

    with nc.Block() as block:
        @block.sync
        def _(q):
            with q.Fori(0, NL) as l:
                def load(kt):
                    if kt >= R:
                        wait_alone(q, s_lo, l * ET + (kt - R + 1), s_passed)
                        wait_alone(q, s_prod, l * ET + (kt - R + 1), s_passed)
                    q.dma_start(raw[:, kt % R, 0, :], A["ent_wT"][l, kt * P:(kt + 1) * P, :]).then_inc(s_raw[kt % R], 16)
                    q.dma_start(raw[:, kt % R, 1, :], A["ent_pw"][l, kt * P:(kt + 1) * P, :]).then_inc(s_raw[kt % R], 16)

                def load_aux(n):
                    if n >= 2 and n - 2 < KT:
                        wait_alone(q, s_wlo, l * (FIN + KT) + (n - 1), s_passed)
                    if n - 2 >= KT:
                        wait_alone(q, s_t32, l * KT + (n - 1 - KT), s_passed)
                    if n < KT:
                        q.dma_start(aux[:, n % 2, 0, :], A["gate_w"][l, n * P:(n + 1) * P, :]).then_inc(s_aux[n % 2], 16)
                    else:
                        k = n - KT
                        q.dma_start(aux[:, n % 2, :, :], A["path_w"][l, :, k * P:(k + 1) * P, :].rearrange("w p d -> p w d")).then_inc(s_aux[n % 2], 16)

                wait_alone(q, s_lo, l * ET, s_passed)
                wait_alone(q, s_prod, l * ET, s_passed)
                for kt in range(2):
                    load(kt)
                wait_alone(q, s_t32, l * KT, s_passed)
                q.wait_ge(drained[KT], l)
                q.dma_start(mod[:, :, :], A["phase"][l].partition_broadcast(P)).then_inc(s_small, 16)
                q.dma_start(pbias[:, :, :], A["path_b"][l].partition_broadcast(P)).then_inc(s_small, 16)
                q.dma_start(ebias[:, :], A["ent_pb"][l].partition_broadcast(P)).then_inc(s_small, 16)
                q.dma_start(eb[:, :], A["ent_b"][l]).then_inc(s_small, 16)
                for kt in range(2, R):
                    load(kt)
                load_aux(0)
                load_aux(1)
                for kt in range(R, ET):
                    load(kt)
                    if kt % 2 and (kt - R) // 2 + 2 < AUX:
                        load_aux((kt - R) // 2 + 2)

        @block.gpsimd
        def _(g):
            g.memset(wide[:, :], 0.0).then_inc(s_wide, 1)
            g.memset(ones[:, :], 1.0).then_inc(s_wide, 1)
            g.wait_ge(s_wide, 2)
            g.affine_select(out=wide[:, :], in_=wide[:, :], compare_op=ALU.not_equal, fill=1.0, base=(KT - 1) * P,
                            pattern=[[-1, (2 * KT - 1) * P]], channel_multiplier=1).then_inc(s_wide, 1)
            with g.Fori(0, NL) as l:
                for kt in range(ET):
                    if kt >= 1:
                        g.wait_ge(s_acc, l * (ET - 1) + (kt - 1))
                    if kt == 0:
                        g.wait_ge(s_small, l * 64 + 64)
                        g.wait_ge(full[KT], l)
                    wait_alone(g, s_raw[kt % R], l * (32 * ET // R) + 32 * (kt // R + 1), s_passed)
                    out = acc if kt == 0 else prod
                    g.tensor_scalar(out[:, :], raw[:, kt % R, 1, :], eb[:, kt:kt + 1], 1.0, ALU.mult, ALU.mult).then_inc(s_prod, 1)
                    g.wait_ge(s_prod, l * ET + (kt + 1))
                    if kt >= 1:
                        g.tensor_tensor(acc[:, :], acc[:, :], prod[:, :], ALU.add).then_inc(s_acc, 1)

        @block.scalar
        def _(s):
            s.preload_act_table_set("silu_and_others")
            with s.Fori(0, NL) as l:
                def finished(n):
                    z, k = (1, n) if n < KT else (0, n - KT)
                    if z:
                        s.wait_ge(s_t32, l * KT + (k + 1))
                    else:
                        s.wait_ge(drained[k], l + 1)
                    s.activation(layers[:, 0, l, z, k * D:(k + 1) * D], t32[:, n % 2, :], ACT.Copy).then_inc(s_whi, 1)

                for kt in range(ET):
                    s.wait_ge(s_raw[kt % R], l * (32 * ET // R) + 32 * (kt // R + 1))
                    if kt < HR:
                        s.wait_ge(full[KT - 1], l)
                    else:
                        s.wait_ge(s_tile, l * (ET - 1) + (kt - HR + 1))
                    s.activation(tile[:, kt % HR, 0, :, :], raw[:, kt % R, :, :], ACT.Copy).then_inc(s_hi, 1)
                    if kt in (1, 3, 5, 7):
                        n = kt // 2
                        s.wait_ge(s_aux[n % 2], l * (16 * AUX // 2) + 16 * (n // 2 + 1))
                        s.activation(gates[:, 0, l, n * D:(n + 1) * D], aux[:, n % 2, 0, :], ACT.Copy).then_inc(s_whi, 1)
                    if kt == 8:
                        s.wait_ge(s_mod, l * MOD_LINKS + (MOD_LINKS - 1))
                        s.activation(mod[:, :, :], mod[:, :, :], ACT.Sin).then_inc(s_sin, 1)
                    if kt in (10, 12, 14):
                        finished((kt - 10) // 2)
                finished(KT - 1)
                for m in range(KT):
                    finished(KT + m)

        @block.vector
        def _(v):
            v.wait_ge(s_wide, 3)
            with v.Fori(0, NL) as l:
                links = {}

                def link(ins, sem_, per):
                    links[sem_.name] = links.get(sem_.name, 0) + 1
                    ins.then_inc(sem_, 1)
                    v.wait_ge(sem_, l * per + links[sem_.name])

                M = 1.5 * 2 ** 23
                n2 = t32[:, :, :]
                def reduce_step(i):
                    if i == 0:
                        v.wait_ge(s_small, l * 64 + 64)
                        v.wait_ge(s_wlo, l * (FIN + KT))
                        ins = v.tensor_scalar(n2, mod[:, :, :], 0.5 / PI, 0.125, ALU.mult, ALU.add)
                    elif i == 1:
                        ins = v.tensor_scalar(n2, n2, M, M, ALU.add, ALU.subtract)
                    elif i < 5:
                        c = (6.28125, 0.0019350051879882812, 3.0199159819885386e-07)[i - 2]
                        ins = v.scalar_tensor_tensor(mod[:, :, :], n2, -c, mod[:, :, :], ALU.mult, ALU.add)
                    elif i == 5:
                        ins = v.tensor_scalar(mod[:, :, :], mod[:, :, :], PI / 4, 3.1415925, ALU.add, ALU.min)
                    elif i == 6:
                        ins = v.tensor_scalar(mod[:, :, :], mod[:, :, :], -3.1415925, None, ALU.max)
                    else:
                        v.wait_ge(s_sin, l + 1)
                        ins = v.tensor_scalar(mod[:, :, :], mod[:, :, :], 2 ** 0.5, None, ALU.mult)
                    link(ins, s_mod, MOD_LINKS)

                def path_bias():
                    link(v.tensor_tensor(pbias[:, :, :], pbias[:, :, :], mod[:, :, :], ALU.mult), s_sum, SUM_LINKS)
                    link(v.tensor_tensor(bias[:, 2 * l + 1, :], pbias[:, 0, :], pbias[:, 1, :], ALU.add), s_sum, SUM_LINKS)

                def lo_of_finished(n):
                    v.wait_ge(s_whi, l * (FIN + KT) + (KT + n + 1))
                    z, k = (1, n) if n < KT else (0, n - KT)
                    v.tensor_tensor(layers[:, 1, l, z, k * D:(k + 1) * D], t32[:, n % 2, :],
                                    layers[:, 0, l, z, k * D:(k + 1) * D].bitcast(F32), ALU.subtract).then_inc(s_wlo, 1)

                def path(k):
                    n = KT + k
                    v.wait_ge(s_aux[n % 2], l * (16 * AUX // 2) + 16 * (n // 2 + 1))
                    a = aux[:, n % 2, :, :]
                    link(v.tensor_tensor(a, a, mod[:, :, :], ALU.mult), s_sum, SUM_LINKS)
                    link(v.tensor_tensor(a[:, 0, :], a[:, 0, :], identity(k), ALU.add), s_sum, SUM_LINKS)
                    if k >= 2:
                        v.wait_ge(s_wlo, l * (FIN + KT) + (KT + k - 1))
                    v.tensor_tensor(t32[:, k % 2, :], a[:, 0, :], a[:, 1, :], ALU.add).then_inc(s_t32, 1)

                extra = {k: [lambda k=k: reduce_step(k)] for k in range(MOD_LINKS - 1)}

                def gate_lo(n):
                    v.wait_ge(s_whi, l * (FIN + KT) + (n + 1))
                    v.tensor_tensor(gates[:, 1, l, n * D:(n + 1) * D], aux[:, n % 2, 0, :],
                                    gates[:, 0, l, n * D:(n + 1) * D].bitcast(F32), ALU.subtract).then_inc(s_wlo, 1)

                for n in range(KT):
                    extra.setdefault(2 * n + 2, []).append(lambda n=n: gate_lo(n))
                extra.setdefault(9, []).append(lambda: reduce_step(MOD_LINKS - 1))
                extra[9].append(path_bias)
                extra[9].append(lambda: path(0))
                extra[11] = [lambda: lo_of_finished(0), lambda: path(1)]
                extra[13] = [lambda: lo_of_finished(1), lambda: path(2)]
                extra[15] = [lambda: lo_of_finished(2), lambda: path(3), lambda: lo_of_finished(3)]
                for kt in range(ET):
                    v.wait_ge(s_hi, l * ET + (kt + 1))
                    v.tensor_tensor(tile[:, kt % HR, 1, :, :], raw[:, kt % R, :, :], tile[:, kt % HR, 0, :, :].bitcast(F32),
                                    ALU.subtract).then_inc(s_lo, 1)
                    for f in extra.get(kt, []):
                        f()
                for m in range(KT):
                    v.wait_ge(full[m], l + 1)
                    v.wait_ge(s_wlo, l * (FIN + KT) + (2 * KT + m - 1))
                    v.tensor_tensor(t32[:, m % 2, :], banks[m][:, :], identity(m), ALU.add).then_inc(drained[m], 1)
                    if m >= 1:
                        lo_of_finished(KT + m - 1)
                lo_of_finished(2 * KT - 1)
                v.wait_ge(full[KT], l + 1)
                v.tensor_tensor(bias[:, 2 * l, :], banks[KT][:, :], ebias[:, :], ALU.add).then_inc(drained[KT], 1)
                assert links[s_mod.name] == MOD_LINKS and links[s_sum.name] == SUM_LINKS, links

        @block.tensor
        def _(t):
            with t.Fori(0, NL) as l:
                for kt in range(ET):
                    t.wait_ge(s_lo, l * ET + (kt + 1))
                    for m in range(KT):
                        if kt == 0:
                            t.wait_ge(drained[m], l)
                        ins = split_products(t, banks[m][:, :], lambda h, c: tile[:, kt % HR, h, 0, m * P:(m + 1) * P],
                                             lambda h, c: tile[:, kt % HR, h, 1, :], [0], first=kt == 0, last=kt == ET - 1)
                        if kt == ET - 1:
                            ins.then_inc(full[m], 1)
                    if kt < ET - 1:
                        ins.then_inc(s_tile, 1)
                t.wait_ge(s_acc, l * (ET - 1) + (ET - 1))
                t.wait_ge(drained[KT], l)
                t.matmul(banks[KT][:, :], ones[:, :], acc[:, :], start=True, stop=True).then_inc(full[KT], 1)


def ffn_order(last):
    UN = 2 * NL * BT
    order = [("mm", 0), ("mm", 1)]
    for u in range(2, UN + 2):
        if u < UN:
            order.append(("mm", u))
        if not last and u == 2:
            order += [("xt", i) for i in range(BT)]
        if u - 2 < UN - BT:
            order.append(("tr", u - 2))
    return order + ([] if last else [(w, m) for m in range(KT) for w in ("ph", "amp")])


def ffn_phase(nc, ctx, sb, sem, A, banks, W, bias, x2, ident, s_passed):
    BS = BT * P
    UN = 2 * NL * BT
    xb = sb(ctx, "xb", [P, BT, D])
    xT = sb(ctx, "x2T", [P, 2, KT, BS], F32R)
    hT = sb(ctx, "hT", [P, 2, KT, BS], F32R)
    y = sb(ctx, "y", [P, BT, D])
    amp = sb(ctx, "amp", [P, 2, BS])
    wave = sb(ctx, "wave", [P, 2, BS])
    HT = 4
    ht = sb(ctx, "ht", [P, HT, KT, P])
    lng = sb(ctx, "lng", [P, D])
    lnb = sb(ctx, "lnb", [P, D])
    NCOL = 2 * KT + 2 * (2 * NL - 1) * KT
    cols = sb(ctx, "cols", [P, NCOL])
    stats = sb(ctx, "stats3", [P, BT, 6])
    mv = sb(ctx, "mv3", [P, BT, 2])
    rstd = sb(ctx, "rstd3", [P, BT, 2])
    nhalf = sb(ctx, "nhalf", [P, 1])
    half_ampb = sb(ctx, "half_ampb", [P, KT])
    angles = sb(ctx, "angles", [P, 2])

    s_cols, s_ln = sem("s3_cols"), sem("s3_ln")
    s_c = sem("s3_const")
    s_xb = sem("s3_xb")
    s_hi = sem("s3_hi")
    s_u, s_sin = sem("s3_u"), sem("s3_sin")
    s_h0 = sem("s3_h0")
    s_h0hi, s_h0lo = sem("s3_h0hi"), sem("s3_h0lo")
    s_bn, s_agg, s_var, s_rstd = sem("s3_bn"), sem("s3_agg"), sem("s3_var"), sem("s3_rstd")
    s_norm = sem("s3_norm")
    s_hhi, s_hlo = sem("s3_hhi"), sem("s3_hlo")
    s_res = sem("s3_res")
    s_g, s_sum = sem("s3_g"), sem("s3_sum")
    s_fin = sem("s3_fin")
    s_out = sem("s3_out")
    full = [sem(f"s3_full{i}") for i in range(8)]
    drained = [sem(f"s3_drained{i}") for i in range(8)]
    LN = UN + BT

    plan_pro = Plan(full, drained)

    def ring(plan, names):
        for name in names:
            plan.take(name, plan.ring % 8)
            plan.ring += 1
        return plan

    ring(plan_pro, [("xt", i) for i in range(BT)] + [(w, m) for m in range(KT) for w in ("ph", "amp")])
    plan_body = ring(plan_pro.after(), ffn_order(False)).loop()
    assert plan_body.ring % 8 == plan_pro.ring % 8
    plan_last = ring(plan_body.after(NB - 2), ffn_order(True))

    def every_block(eng, body):
        with eng.Fori(0, NB - 1) as b:
            body(b, plan_body, False)
        body(NB - 1, plan_last, True)

    def gain(s, k):
        c = 2 * KT + 2 * KT * s + k
        return cols[:, c:c + 1]

    def shift(s, k):
        c = 2 * KT + 2 * KT * s + KT + k
        return cols[:, c:c + 1]

    with nc.Block() as block:
        @block.sync
        def _(q):
            q.dma_start(xb[:, :, :], x2[:, BT:2 * BT, :]).then_inc(s_xb, 16)
            q.dma_start(cols[:, :], A["cols"]).then_inc(s_cols, 16)
            q.dma_start(lng[:, :], A["ln_g"].partition_broadcast(P)).then_inc(s_ln, 16)
            q.dma_start(lnb[:, :], A["ln_b"].partition_broadcast(P)).then_inc(s_ln, 16)
            out = A["out"].rearrange("b (t p) d -> (b t) p d", p=P)
            blocks = x2[:, :, :].rearrange("p (b t) d -> p b t d", t=BT)

            def body(b, plan, load):
                if load:
                    Banks(q, plan, b).wait_full(("xt", BT - 1))
                    q.sem_inc(s_passed, 1)
                    q.dma_start(xb[:, :, :], blocks[:, b + 2, :, :]).then_inc(s_xb, 16)
                for i in range(BT):
                    wait_alone(q, s_fin, b * BT + (i + 1), s_passed)
                    q.dma_start(out[b * BT + i], y[:, i, :]).then_inc(s_out, 16)

            with q.Fori(0, NB - 2) as b:
                body(b, plan_body, True)
            body(NB - 2, plan_body, False)
            body(NB - 1, plan_last, False)
            q.wait_ge(s_out, 16 * NB * BT + 1)

        @block.gpsimd
        def _(g):
            g.memset(nhalf[:, :], -0.5).then_inc(s_c, 1)
            g.memset(angles[:, 0:1], PI / 2).then_inc(s_c, 1)
            g.memset(angles[:, 1:2], -0.25).then_inc(s_c, 1)
            plan_pro.begin(g)
            g.sem_inc(s_out, 1)
            g.wait_ge(s_c, 4)
            g.wait_ge(s_ln, 32)

            def body(b, plan, last):
                def rstd_of(n):
                    i = (n - 1) % BT
                    m = b * LN + n
                    wait_alone(g, s_agg, m, s_passed)
                    g.tensor_scalar(rstd[:, i, 0:1], mv[:, i, 1:2], EPS, None, ALU.add).then_inc(s_var, 1)
                    g.wait_ge(s_var, m)
                    g.tensor_tensor(rstd[:, i, 1:2], rstd[:, i, 0:1], nhalf[:, :], ALU.pow).then_inc(s_rstd, 1)

                def lo(u):
                    i = u % BT
                    g.wait_ge(s_hhi, b * (UN - BT) + (u + 1))
                    g.tensor_tensor(hT[:, 1, :, i * P:(i + 1) * P], ht[:, u % HT, :, :],
                                    hT[:, 0, :, i * P:(i + 1) * P].bitcast(F32), ALU.subtract).then_inc(s_hlo, 1)

                def residual(i):
                    x = x2[:, b * BT + i, :]
                    g.tensor_tensor(x, x, lnb[:, :], ALU.add).then_inc(s_res, 1)

                spare = (0, 1, UN - 2, UN - 1)
                for u in range(UN):
                    if 2 <= u < UN - BT + 2:
                        lo(u - 2)
                    rstd_of(u + 1)
                    if u in spare:
                        residual(spare.index(u))
                for i in range(BT):
                    rstd_of(UN + i + 1)

            every_block(g, body)

        @block.scalar
        def _(s):
            s.wait_ge(s_c, 4)
            s.wait_ge(s_cols, 16)

            def x2T_hi(k, i):
                k.wait_full(("xt", i))
                bank = banks[k.plan.bank(("xt", i))][:, :].rearrange("p (k s) -> p k s", k=KT)
                s.activation(xT[:, 0, :, i * P:(i + 1) * P], bank, ACT.Copy).then_inc(s_hi, 1)

            def gates(k, block):
                for m in range(KT):
                    n = block * KT + (m + 1)
                    if m >= 2:
                        s.wait_ge(s_h0lo, n - 2)
                    k.wait_full(("ph", m))
                    k.drain(("ph", m), s.activation(wave[:, m % 2, :], banks[k.plan.bank(("ph", m))][:, :], ACT.Tanh, bias=cols[:, KT + m:KT + m + 1]))
                    k.wait_drained(("ph", m))
                    s.activation(wave[:, m % 2, :], wave[:, m % 2, :], ACT.Abs, bias=angles[:, 1:2]).then_inc(s_u, 1)
                    s.wait_ge(s_u, n)
                    s.activation(wave[:, m % 2, :], wave[:, m % 2, :], ACT.Sin, bias=angles[:, 0:1], scale=-PI).then_inc(s_sin, 1)
                    k.wait_full(("amp", m))
                    k.drain(("amp", m), s.activation(amp[:, m % 2, :], banks[k.plan.bank(("amp", m))][:, :], ACT.Tanh, bias=half_ampb[:, m:m + 1], scale=0.5))
                    s.wait_ge(s_h0, n)
                    s.activation(hT[:, 0, m, :], wave[:, m % 2, :], ACT.Copy, scale=SQRT_HALF).then_inc(s_h0hi, 1)

            k = Banks(s, plan_pro, 0)
            for i in range(BT):
                x2T_hi(k, i)
            gates(k, 0)

            def body(b, plan, last):
                k = Banks(s, plan, b)

                def hT_of(u):
                    k.wait_full(("tr", u))
                    if u >= HT:
                        s.wait_ge(s_hlo, b * (UN - BT) + (u - HT + 1))
                    bank = banks[plan.bank(("tr", u))]
                    for c in range(KT):
                        ins = s.activation(ht[:, u % HT, c, :], bank[:, c * P:(c + 1) * P], ACT.Identity,
                                           bias=shift(u // BT, c), scale=gain(u // BT, c))
                    k.drain(("tr", u), ins)
                    k.wait_drained(("tr", u))
                    i = u % BT
                    s.activation(hT[:, 0, :, i * P:(i + 1) * P], ht[:, u % HT, :, :], ACT.Copy).then_inc(s_hhi, 1)

                for kind, n in ffn_order(last):
                    if kind == "tr":
                        hT_of(n)
                    elif kind == "xt":
                        x2T_hi(k, n)
                if not last:
                    gates(k, b + 1)

            every_block(s, body)

        @block.vector
        def _(v):
            v.wait_ge(s_cols, 16)
            v.tensor_scalar(half_ampb[:, :], cols[:, 0:KT], 0.5, None, ALU.mult).then_inc(s_c, 1)

            def x2T_lo(k, i, n):
                v.wait_ge(s_hi, n)
                bank = banks[k.plan.bank(("xt", i))][:, :].rearrange("p (k s) -> p k s", k=KT)
                k.drain(("xt", i), v.tensor_tensor(xT[:, 1, :, i * P:(i + 1) * P], bank, xT[:, 0, :, i * P:(i + 1) * P].bitcast(F32), ALU.subtract))

            def h0(k, block, m):
                n = block * KT + (m + 1)
                k.wait_drained(("amp", m))
                v.wait_ge(s_sin, n)
                v.scalar_tensor_tensor(wave[:, m % 2, :], amp[:, m % 2, :], 1.0, wave[:, m % 2, :], ALU.add, ALU.mult).then_inc(s_h0, 1)
                v.wait_ge(s_h0hi, n)
                v.scalar_tensor_tensor(hT[:, 1, m, :], wave[:, m % 2, :], SQRT_HALF, hT[:, 0, m, :].bitcast(F32), ALU.mult, ALU.subtract).then_inc(s_h0lo, 1)

            k = Banks(v, plan_pro, 0)
            for i in range(BT):
                x2T_lo(k, i, i + 1)
            for m in range(KT):
                h0(k, 0, m)

            def body(b, plan, last):
                k = Banks(v, plan, b)

                def statistics(i, n):
                    v.bn_stats(stats[:, i, :], y[:, i, :]).then_inc(s_bn, 1)
                    wait_alone(v, s_bn, b * LN + n, s_passed)
                    v.bn_aggr(mv[:, i, :], stats[:, i, :]).then_inc(s_agg, 1)

                def normalise(i, n, s_done):
                    v.wait_ge(s_rstd, b * LN + n)
                    v.tensor_scalar(y[:, i, :], y[:, i, :], mv[:, i, 0:1], rstd[:, i, 1:2], ALU.subtract, ALU.mult).then_inc(s_done, 1)

                def unit(u):
                    s_, i = divmod(u, BT)
                    k.wait_full(("mm", u))
                    if s_ == 0:
                        v.wait_ge(s_out, b * (16 * BT) + 1)
                    k.drain(("mm", u), v.tensor_tensor(y[:, i, :], banks[plan.bank(("mm", u))][:, :], bias[:, s_, :], ALU.add))
                    if u >= 1:
                        normalise((u - 1) % BT, u, s_norm)
                    k.wait_drained(("mm", u))
                    statistics(i, u + 1)

                def finish(i):
                    n = b * BT + (i + 1)
                    v.wait_ge(s_norm, b * UN + (UN - BT + i + 1))
                    v.tensor_tensor(y[:, i, :], y[:, i, :], lng[:, :], ALU.mult).then_inc(s_g, 1)
                    v.wait_ge(s_g, n)
                    v.wait_ge(s_res, n)
                    v.tensor_tensor(y[:, i, :], y[:, i, :], x2[:, b * BT + i, :], ALU.add).then_inc(s_sum, 1)
                    v.wait_ge(s_sum, n)
                    statistics(i, UN + i + 1)

                for kind, n in ffn_order(last):
                    if kind == "mm":
                        unit(n)
                    elif kind == "xt":
                        x2T_lo(k, n, b * BT + (BT + n + 1))
                normalise(BT - 1, UN, s_norm)
                for i in range(BT):
                    finish(i)
                    if i >= 1:
                        normalise(i - 1, UN + i, s_fin)
                    if not last:
                        h0(k, b + 1, i)
                normalise(BT - 1, UN + BT, s_fin)

            every_block(v, body)

        @block.tensor
        def _(t):
            def x2T(k, i, src):
                k.wait_free(("xt", i))
                for c in range(KT):
                    ins = t.transpose(banks[k.plan.bank(("xt", i))][:, c * P:(c + 1) * P], src[:, i, c * P:(c + 1) * P], ident[:, :])
                k.filled(("xt", i), ins)

            def gate(k, name, m):
                off = {"amp": OFF_AMP, "ph": OFF_PH}[name]
                k.wait_free((name, m))
                k.filled((name, m), split_products(t, banks[k.plan.bank((name, m))][:, :],
                                                   lambda h, c: W[:, h, off + c * D + m * P:off + c * D + (m + 1) * P],
                                                   lambda h, c: xT[:, h, c, :], range(KT)))

            k = Banks(t, plan_pro, 0)
            for i in range(BT):
                x2T(k, i, x2[:, 0:BT, :])
            for i in range(BT):
                k.wait_drained(("xt", i))
            for m in range(KT):
                gate(k, "ph", m)
                gate(k, "amp", m)

            def body(b, plan, last):
                k = Banks(t, plan, b)

                def mm(u, cs):
                    s_, i = divmod(u, BT)
                    off = (OFF_ENT, OFF_PATH)[s_ % 2][s_ // 2]
                    if cs[0] == 0:
                        k.wait_free(("mm", u))
                    ins = split_products(t, banks[plan.bank(("mm", u))][:, :], lambda h, c: hT[:, h, c, i * P:(i + 1) * P],
                                         lambda h, c: W[:, h, off + c * D:off + (c + 1) * D], cs, first=cs[0] == 0, last=cs[-1] == KT - 1)
                    if cs[-1] == KT - 1:
                        k.filled(("mm", u), ins)

                def transpose_norm(u):
                    t.wait_ge(s_norm, b * UN + (u + 1))
                    k.wait_free(("tr", u))
                    for c in range(KT):
                        ins = t.transpose(banks[plan.bank(("tr", u))][:, c * P:(c + 1) * P], y[:, u % BT, c * P:(c + 1) * P], ident[:, :])
                    k.filled(("tr", u), ins)

                for c in range(KT):
                    t.wait_ge(s_h0lo, b * KT + (c + 1))
                    for u in (0, 1):
                        mm(u, [c])
                for kind, n in ffn_order(last):
                    if kind == "mm" and n >= 2:
                        if n >= BT:
                            t.wait_ge(s_hlo, b * (UN - BT) + (n - BT + 1))
                        mm(n, list(range(KT // 2)))
                        if n == 2 and not last:
                            t.wait_ge(s_xb, b * 16 + 16)
                            for i in range(BT):
                                x2T(k, i, xb)
                        if n - 2 < UN - BT:
                            transpose_norm(n - 2)
                        mm(n, list(range(KT // 2, KT)))
                    elif kind in ("ph", "amp"):
                        if (kind, n) == ("ph", 0):
                            for i in range(BT):
                                k.wait_drained(("xt", i))
                        gate(k, kind, n)

            every_block(t, body)


def layout(inputs):
    import numpy as np
    a = {k.replace("L0_", ""): np.asarray(v) for k, v in inputs.items()}
    c = np.ascontiguousarray
    x = c(a["x"])
    wq = a["attn_Wq"].reshape(D, NKV, NH // NKV, HD).transpose(0, 2, 1, 3).reshape(D, D)
    wo = a["attn_Wo"].reshape(NKV, NH // NKV, HD, D).transpose(1, 0, 2, 3).reshape(D, D)
    col = lambda v: v.reshape(-1, P).T
    g3, b3, g4, b4 = (a[f"ffn_{n}"] for n in ("ln3_g", "ln3_b", "ln4_g", "ln4_b"))
    return {
        "x": x,
        "xT": c(x.reshape(B * S, D).T),
        "ctxT": c(a["ctx_512"].reshape(B * S, L).T),
        "w_k": c(a["attn_Wk"]),
        "w_v": c(a["attn_Wv"]),
        "w_q": c(wq),
        "w_o": c(wo),
        "w_cq": c(a["xattn_Wq"].T),
        "w_ckv": c(a["xattn_Wkv_expand"].T),
        "w_cout": c(a["xattn_Wout"].T),
        "ent_wT": c(a["ffn_ent_w"].transpose(0, 2, 1)),
        "ent_pw": c(a["ffn_ent_pw"]),
        "ent_b": c(a["ffn_ent_b"].reshape(NL, ET, P).transpose(0, 2, 1)),
        "ent_pb": c(a["ffn_ent_pb"]),
        "gate_w": c(np.stack([a["ffn_amp_w"], a["ffn_ph_w"]])),
        "path_w": c(a["ffn_path_w"]),
        "path_b": c(a["ffn_path_b"]),
        "phase": c(a["ffn_phase"]),
        "cols": c(np.concatenate([col(v) for v in (a["ffn_amp_b"], a["ffn_ph_b"], g3[0], b3[0], g4[0], b4[0], g3[1], b3[1])], axis=1)),
        "ln_g": c(g4[1]),
        "ln_b": c(b4[1]),
    }


def kernel(**inputs):
    import concourse.bacc as bacc
    from concourse.bass_utils import run_bass_kernel_spmd

    nc = bacc.Bacc("TRN2", target_bir_lowering=False, num_devices=1)
    arrays = layout(inputs)
    A = {n: nc.dram_tensor(f"in_{n}", v.shape, mybir.dt.from_np(v.dtype), kind="ExternalInput").ap() for n, v in arrays.items()}
    A["out"] = nc.dram_tensor("out", (B, S, D), F32, kind="ExternalOutput").ap()
    build(nc, A)
    r = run_bass_kernel_spmd(nc, [{f"in_{n}": v for n, v in arrays.items()}], core_ids=[0])
    return r.results[0]["out"]
```

```python
from contextlib import ExitStack

import concourse.bass as bass
from concourse import mybir

F32 = mybir.dt.float32
F32R = mybir.dt.float32r
BF16 = mybir.dt.bfloat16
ALU = mybir.AluOpType
ACT = mybir.ActivationFunctionType
AX = mybir.AxisListType

P = 128
B, S, D = 8, 256, 512
L = 128
NH, HD = 16, 32
NKV = 4
KT = D // P
TT = S // P
HG = P // HD
NG = NH // HG
EW = 4 * D
ET = EW // P
NL, NP = 2, 2
BT = 4
NB = B * S // (BT * P)
EPS = 1e-5
SCALE = HD ** -0.5
MASKED = -1e30
SQRT_HALF = 0.5 ** 0.5
PI = 3.141592653589793
N_COLS = 2 * KT + 2 * (2 * NL - 1) * KT
MOD_LINKS = 8

KV = NKV * HD
OFF_K = 0
OFF_V = OFF_K + KT * KV
OFF_Q = OFF_V + KT * KV
OFF_CKV = OFF_Q + KT * D
OFF_WO = OFF_CKV + 2 * D
OFF_CQ = OFF_WO + KT * D
OFF_COUT = OFF_CQ + KT * D
W_ATT = OFF_COUT + KT * D
OFF_AMP, OFF_PH = 0, KT * D
OFF_ENT = [2 * KT * D, 4 * KT * D]
OFF_PATH = [3 * KT * D, 5 * KT * D]
W_FFN = 6 * KT * D


class Plan:

    def __init__(self, full, drained, s_hi=None):
        self.full, self.drained = full + [s_hi], drained + [None]
        self.base = [1] * len(self.full)
        self.count = [0] * len(self.full)
        self.per = [0] * len(self.full)
        self.at = {}
        self.ring = 0

    def after(self, it=0):
        p = Plan(self.full[:-1], self.drained[:-1], self.full[-1])
        p.base = [b + it * n + c for b, n, c in zip(self.base, self.per, self.count)]
        p.ring = self.ring
        return p

    def loop(self):
        self.per = list(self.count)
        return self

    def take(self, name, bank):
        self.count[bank] += 1
        self.at[name] = (bank, self.count[bank])

    def take_hi(self, name):
        self.take(("hi", name), len(self.full) - 1)

    def bank(self, name):
        return self.at[name][0]

    def value(self, it, name):
        bank, k = self.at[name]
        return it * self.per[bank] + (self.base[bank] + k)

    def begin(self, eng):
        for sem in self.full + self.drained:
            if sem is not None:
                eng.sem_inc(sem, 1)


class Banks:

    def __init__(self, eng, plan, it):
        self.eng, self.plan, self.it = eng, plan, it

    def wait_free(self, name):
        self.eng.wait_ge(self.plan.drained[self.plan.bank(name)], self.plan.value(self.it, name) - 1)

    def wait_full(self, name):
        self.eng.wait_ge(self.plan.full[self.plan.bank(name)], self.plan.value(self.it, name))

    def wait_hi(self, name):
        self.wait_full(("hi", name))

    def wait_drained(self, name):
        self.eng.wait_ge(self.plan.drained[self.plan.bank(name)], self.plan.value(self.it, name))

    def filled(self, name, ins):
        ins.then_inc(self.plan.full[self.plan.bank(name)], 1)

    def drain(self, name, ins):
        ins.then_inc(self.plan.drained[self.plan.bank(name)], 1)



def groups_of(cross, nxt):
    return (list(range(NG)) if cross else []) + (list(range(NG, 2 * NG)) if nxt else [])


def schedule(cross, nxt, proj):
    n = len(groups_of(cross, nxt))
    if cross:
        ev = [("ck", 0), ("ck", 1), ("wo", 0), ("wo", 1)] + ([("sq", 1)] if nxt else []) + [("ck", 2), ("x1t", 0)]
        ev += ([("sq", 2), ("sv", 0)] if nxt else []) + [("x1t", 1)] + ([("sv", 1)] if nxt else []) + [("ck", 3), ("cq", 0), ("cq", 1)]
        after = {0: [("cq", 2)], 1: [("cq", 3), ("cv", 0), ("cv", 1)]}
        if nxt:
            after[0] += [("sq", 3)]
            after[6], after[7] = [("wout", 0)], [("wout", 1)]
    else:
        ev = [("sv", 0), ("sv", 1), ("sq", 1), ("sq", 2)]
        after = {0: [("sq", 3), ("weights", 0)], 1: [("weights", 1)]}
    if proj:
        after[n] = [("sk", 0)]
    for i in range(n + 2):
        ev += [("step", i)] + after.get(i, [])
    if cross and not nxt:
        ev += [("wout", 0), ("wout", 1)]
    if proj:
        ev.append(("sq", 0))
    return ev


N_RING = 5
T_BANKS, O_BANK = (5, 6), 7
SPLIT = ("sk", "sq", "ck", "x1t", "cq")


def attention_plan(plan, cross, nxt, proj):
    def ring(name):
        plan.take(name, plan.ring % N_RING)
        plan.ring += 1

    n = len(groups_of(cross, nxt))
    for kind, i in schedule(cross, nxt, proj):
        if kind == "step":
            if i < n:
                for j in range(HG):
                    ring(("S", i, j))
            for js in ((0, 1), (2, 3)):
                if 1 <= i <= n:
                    for j in js:
                        plan.take(("T", i - 1, j), T_BANKS[j % 2])
                if i >= 2 and js[0] == 0:
                    plan.take(("O", i - 2), O_BANK)
        elif kind != "weights":
            ring((kind, i))
            if kind in SPLIT:
                plan.take_hi((kind, i))
    return plan


def wait_alone(eng, sem, value, s_passed):
    eng.wait_ge(sem, value)
    eng.sem_inc(s_passed, 1)


def split_products(t, out, lhs, rhs, kts, first=True, last=True):
    for n, k in enumerate(kts):
        for m, (a, b) in enumerate(((0, 0), (0, 1), (1, 0))):
            ins = t.matmul(out, lhs(a, k), rhs(b, k), start=first and n == 0 and m == 0,
                           stop=last and n == len(kts) - 1 and m == 2, skip_group_check=True)
    return ins


def build(nc, A):
    with ExitStack() as whole:
        def sem(name):
            return whole.enter_context(nc.semaphore(name))

        def sb(ctx, name, shape, dt=F32):
            return ctx.enter_context(nc.sbuf_tensor(name, shape, dt))

        banks = [whole.enter_context(nc.psum_tensor(f"bank{i}", [P, 512], F32)) for i in range(8)]
        x2 = sb(whole, "x2", [P, B * TT, D])
        ident = sb(whole, "ident", [P, P])
        s_const, s_passed = sem("s_const"), sem("s_passed")
        with ExitStack() as ctx:
            attention_phase(nc, ctx, sb, sem, A, banks, x2, ident, s_const, s_passed)
        with ExitStack() as ctx:
            W = sb(ctx, "w_ffn", [P, 2, W_FFN], F32R)
            bias = sb(ctx, "stage_bias", [P, 2 * NL, D])
            xT = sb(ctx, "x2T", [P, 2, KT, BT * P], F32R)
            cols = sb(ctx, "cols", [P, N_COLS])
            half_ampb = sb(ctx, "half_ampb", [P, KT])
            with ExitStack() as inner:
                fusion_phase(nc, inner, sb, sem, A, banks, W, bias, x2, xT, cols, half_ampb, ident, s_passed)
            with ExitStack() as inner:
                ffn_phase(nc, inner, sb, sem, A, banks, W, bias, x2, xT, cols, half_ampb, ident, s_passed)


def attention_phase(nc, ctx, sb, sem, A, banks, x2, ident, s_const, s_passed):
    W = sb(ctx, "w_att", [P, 2, W_ATT], F32R)
    xT_raw = x2[:, (B - 1) * TT:, :].rearrange("p t (k s) -> p (t k) s", k=KT // TT)
    xT = sb(ctx, "xT", [P, 2, KT, S], F32R)
    ctx_raw = sb(ctx, "ctx_raw", [P, S])
    ctxT = sb(ctx, "ctxT", [P, 2, S], F32R)
    sqT = sb(ctx, "sqT", [P, 2, NG, S], F32R)
    skT = sb(ctx, "skT", [P, 2, S], F32R)
    sv = sb(ctx, "sv", [P, TT, KV])
    cqT = sb(ctx, "cqT", [P, 2, NG, S], F32R)
    ckT = sb(ctx, "ckT", [P, 2, NG, S], F32R)
    cv = sb(ctx, "cv", [P, TT, D])
    PW = S // 2 + S
    RING = 2 * HG
    prob = sb(ctx, "prob", [P, RING, PW])
    probT = sb(ctx, "probT", [P, RING, PW])
    nmax = sb(ctx, "nmax", [P, RING, TT])
    den = sb(ctx, "den", [P, 2, HG, TT])
    rden = sb(ctx, "rden", [P, 2, HG, TT])
    rwide = sb(ctx, "rwide", [P, 2, TT, P])
    rT = sb(ctx, "rT", [P, 2, S])
    o32 = sb(ctx, "o32", [P, 2, S])
    oT_self = sb(ctx, "oT_self", [P, 2, NG, S], F32R)
    oT_cross = sb(ctx, "oT_cross", [P, 2, NG, S], F32R)
    x1T = oT_self
    xres = sb(ctx, "xres", [P, TT, D])
    stats = sb(ctx, "stats", [P, TT, 6])
    mv = sb(ctx, "mv", [P, TT, 2])
    rstd = sb(ctx, "rstd", [P, TT, 2])
    half = sb(ctx, "half", [P, 1])
    ident16 = sb(ctx, "ident16", [P, P], BF16)
    mask16 = sb(ctx, "mask16", [P, 2, P], BF16)

    s_xT, s_ctx, s_x = sem("s_xT"), sem("s_ctx"), sem("s_x")
    s_x0 = sem("s_x0")
    s_xh, s_xs = sem("s_xh"), sem("s_xs")
    s_ch, s_cs = sem("s_ch"), sem("s_cs")
    s_hi = sem("s_hi")
    s_max = sem("s_max")
    s_rden, s_wide = sem("s_rden"), sem("s_wide_r")
    s_rT = sem("s_rT")
    s_oh, s_os = sem("s_oh"), sem("s_os")
    s_bn, s_agg = sem("s_bn"), sem("s_agg")
    s_var, s_rstd = sem("s_var"), sem("s_rstd")
    s_norm = sem("s_norm")
    full = [sem(f"s1_full{i}") for i in range(8)]
    drained = [sem(f"s1_drained{i}") for i in range(8)]

    PRO = [("sk", 0), ("sq", 0)]
    plan_pro = Plan(full, drained, s_hi)
    for n, name in enumerate(PRO):
        plan_pro.take(name, n)
        plan_pro.take_hi(name)
    FIRST, LOOP, SECOND_LAST, LAST = (0, 1, 1), (1, 1, 1), (1, 1, 0), (1, 0, 0)
    plan_first = attention_plan(plan_pro.after(), *FIRST)
    plan_loop = plan_first.after()
    plan_loop.ring = 0
    attention_plan(plan_loop, *LOOP).loop()
    plan_6 = plan_loop.after(B - 3)
    plan_6.ring = 0
    attention_plan(plan_6, *SECOND_LAST)
    plan_7 = plan_6.after()
    attention_plan(plan_7, *LAST)

    def every_iteration(eng, body):
        body(-1, plan_first, *FIRST)
        with eng.Fori(0, B - 2) as b:
            body(b, plan_loop, *LOOP)
        body(B - 2, plan_6, *SECOND_LAST)
        body(B - 1, plan_7, *LAST)

    def group_number(b, groups, i):
        return b * (2 * NG) + (NG + groups[i] + 1)

    x2f = x2[:, :, :].rearrange("p t d -> p (t d)")
    prf = prob[:, :, :].rearrange("p t d -> p (t d)")
    matrices = [(OFF_K, prf[:, 0:KT * KV], A["w_k"]),
                (OFF_Q, prf[:, 2 * KT * KV:2 * KT * KV + KT * D], A["w_q"]),
                (OFF_V, prf[:, KT * KV:2 * KT * KV], A["w_v"]),
                (OFF_CKV, x2f[:, 3 * KT * D:3 * KT * D + 2 * D], A["w_ckv"]),
                (OFF_WO, x2f[:, 0:KT * D], A["w_o"]),
                (OFF_CQ, x2f[:, KT * D:2 * KT * D], A["w_cq"]),
                (OFF_COUT, x2f[:, 2 * KT * D:3 * KT * D], A["w_cout"])]
    s_wraw = [sem(f"s_wraw{i}") for i in range(len(matrices))]
    s_whi, s_wlo = sem("s_whi"), sem("s_wlo")
    pieces = [(n, off + c, src[:, c:c + D]) for n, (off, src, _) in enumerate(matrices) for c in range(0, src.shape[1], D)]
    KEYS, QUERIES, VALUES = 1, 1 + KT, 2 + KT
    LOTS = [(0, KEYS), (KEYS, VALUES), (VALUES, VALUES + 6), (VALUES + 6, len(pieces))]

    with nc.Block() as block:
        @block.sync
        def _(q):
            xT_of = A["xT"].rearrange("(k p) (b s) -> b p k s", p=P, b=B)
            ctx_of = A["ctxT"].rearrange("p (b s) -> b p s", b=B)
            x_of = A["x"].rearrange("b (t p) d -> b p t d", p=P)

            def load(what, b):
                dst, src, s_ = {"xT": (xT_raw[:, :, :], xT_of, s_xT), "ctx": (ctx_raw[:, :], ctx_of, s_ctx),
                                "x": (xres[:, :, :], x_of, s_x)}[what]
                q.dma_start(dst, src[b]).then_inc(s_, 16)

            def load_weights(n):
                _, dst, src = matrices[n]
                k = dst.shape[1] // src.shape[1]
                q.dma_start(dst.rearrange("p (k n) -> p k n", k=k), src.rearrange("(k p) n -> p k n", p=P)).then_inc(s_wraw[n], 16)

            load("xT", 0)
            load_weights(0)
            load_weights(1)
            load_weights(2)
            q.wait_ge(s_xs, 1)
            load("xT", 1)
            load("ctx", 0)
            for n in range(3, len(matrices)):
                load_weights(n)
            load("x", 0)

            def next_loads(b, last):
                wait_alone(q, s_cs, b + 1, s_passed)
                load("ctx", b + 1)
                if not last:
                    wait_alone(q, s_xs, b + 2, s_passed)
                    load("xT", b + 2)
                wait_alone(q, s_norm, b * (2 * TT) + 2 * TT, s_passed)
                load("x", b + 1)

            with q.Fori(0, B - 2) as b:
                next_loads(b, False)
            next_loads(B - 2, True)

        @block.gpsimd
        def _(g):
            plan_pro.begin(g)
            g.memset(ident[:, :], 0.0).then_inc(s_const, 1)
            g.memset(ident16[:, :], 0.0).then_inc(s_const, 1)
            g.memset(mask16[:, :, :], 0.0).then_inc(s_const, 1)
            g.memset(half[:, :], -0.5).then_inc(s_const, 1)
            g.wait_ge(s_const, 4)
            for m in (ident, ident16):
                g.affine_select(out=m[:, :], in_=m[:, :], compare_op=ALU.not_equal, fill=1.0, base=0,
                                pattern=[[-1, P]], channel_multiplier=1).then_inc(s_const, 1)
            g.affine_select(out=mask16[:, :, :], in_=mask16[:, :, :], compare_op=ALU.is_ge, fill=MASKED, base=0,
                            pattern=[[0, 2], [-1, P]], channel_multiplier=1).then_inc(s_const, 1)

            def split(hi, lo, raw, s_h, s_l, n):
                g.tensor_scalar(hi, raw, 1.0, 1.0, ALU.mult, ALU.mult).then_inc(s_h, 1)
                g.wait_ge(s_h, n)
                g.tensor_tensor(lo, raw, hi.bitcast(F32), ALU.subtract).then_inc(s_l, 1)

            def split_x(b):
                wait_alone(g, s_xT, b * 16 + 16, s_passed)
                split(xT[:, 0, :, :], xT[:, 1, :, :], xT_raw[:, :, :], s_xh, s_xs, b)

            def split_ctx(b):
                wait_alone(g, s_ctx, b * 16 + 16, s_passed)
                split(ctxT[:, 0, :], ctxT[:, 1, :], ctx_raw[:, :], s_ch, s_cs, b + 1)

            def body(b, plan, cross, nxt, proj):
                k = Banks(g, plan, b)
                groups = groups_of(cross, nxt)

                def copies(i):
                    n = group_number(b, groups, i)
                    wait_alone(g, s_rden, n, s_passed)
                    src = rden[:, i % 2, :, :].rearrange("p (j o) t -> p t j o", o=1).broadcast_to([P, TT, HG, HD])
                    g.tensor_scalar(rwide[:, i % 2, :, :].rearrange("p t (j d) -> p t j d", j=HG), src, 1.0, 1.0, ALU.mult, ALU.mult).then_inc(s_wide, 1)

                def split_output(i):
                    k.wait_drained(("O", i))
                    g.sem_inc(s_passed, 1)
                    oT = oT_cross if groups[i] < NG else oT_self
                    t = groups[i] % NG
                    split(oT[:, 0, t, :], oT[:, 1, t, :], o32[:, i % 2, :], s_oh, s_os, group_number(b, groups, i))

                def rstd_of(ai, i):
                    n = b * (2 * TT) + (ai * TT + i + 1)
                    wait_alone(g, s_agg, n, s_passed)
                    g.tensor_scalar(rstd[:, i, 0:1], mv[:, i, 1:2], EPS, None, ALU.add).then_inc(s_var, 1)
                    g.wait_ge(s_var, n)
                    g.tensor_tensor(rstd[:, i, 1:2], rstd[:, i, 0:1], half[:, :], ALU.pow).then_inc(s_rstd, 1)

                last_of_x = [(kind, i) for kind, i in schedule(cross, nxt, proj) if kind == "sv" or kind == "sq" and i > 0][-1:]
                last_of_x = last_of_x[0] if last_of_x else None
                for kind, i in schedule(cross, nxt, proj):
                    if kind == "wo":
                        rstd_of(0, i)
                    elif kind == "wout":
                        rstd_of(1, i)
                    elif kind == "step":
                        if 1 <= i <= len(groups):
                            copies(i - 1)
                        if i >= 2:
                            split_output(i - 2)
                    elif proj and (kind, i) == last_of_x:
                        k.wait_full((kind, i))
                        split_x(b + 2)
                        if not cross:
                            split_ctx(0)
                    elif (kind, i) == ("cv", TT - 1) and nxt:
                        k.wait_full((kind, i))
                        split_ctx(b + 1)

            every_iteration(g, body)

        @block.scalar
        def _(s):
            def weights(lot):
                for n, off, raw in pieces[slice(*lot)]:
                    s.wait_ge(s_wraw[n], 16)
                    s.activation(W[:, 0, off:off + D], raw, ACT.Copy).then_inc(s_whi, 1)

            def hi(k, name, out, scale=1.0):
                k.wait_full(name)
                src = banks[k.plan.bank(name)][:, 0:512 if len(out.shape) == 3 else S]
                if len(out.shape) == 3:
                    src = src.rearrange("p (k s) -> p k s", k=KT)
                s.activation(out, src, ACT.Copy, scale=scale).then_inc(s_hi, 1)

            def values(k, name, out):
                k.wait_full(name)
                k.drain(name, s.activation(out, banks[k.plan.bank(name)][:, 0:out.shape[1]], ACT.Copy))

            def projection(k, kind, i):
                if kind == "sk":
                    hi(k, (kind, i), skT[:, 0, :])
                elif kind == "sq":
                    hi(k, (kind, i), sqT[:, 0, i, :], SCALE)
                elif kind == "ck":
                    hi(k, (kind, i), ckT[:, 0, i, :])
                elif kind == "cq":
                    hi(k, (kind, i), cqT[:, 0, i, :], SCALE)
                elif kind == "x1t":
                    hi(k, (kind, i), x1T[:, 0, :, i * P:(i + 1) * P])
                elif kind == "sv":
                    values(k, (kind, i), sv[:, i, :])
                elif kind == "cv":
                    values(k, (kind, i), cv[:, i, :])

            s.wait_ge(s_xT, 16)
            s.activation(xT[:, 0, :, :], xT_raw[:, :, :], ACT.Copy).then_inc(s_x0, 1)
            weights(LOTS[0])
            k = Banks(s, plan_pro, 0)
            weights(LOTS[1])
            projection(k, "sk", 0)
            projection(k, "sq", 0)

            def body(b, plan, cross, nxt, proj):
                k = Banks(s, plan, b)
                groups = groups_of(cross, nxt)

                def step(i):
                    if 1 <= i <= len(groups):
                        k.wait_full(("T", i - 1, 0))
                        k.drain(("T", i - 1, 0), s.activation(probT[:, ((i - 1) % 2) * HG, :], banks[plan.bank(("T", i - 1, 0))][:, 0:PW], ACT.Copy))
                    if i >= len(groups):
                        return
                    for j in range(HG):
                        slot = (i % 2) * HG + j
                        s.wait_ge(s_max, b * (2 * NG * HG) + (NG + groups[i]) * HG + j + 1)
                        bank = banks[plan.bank(("S", i, j))]
                        s.activation(prob[:, slot, 0:P], bank[:, 0:P], ACT.Exp, bias=nmax[:, slot, 0:1], accum_out=den[:, i % 2, j, 0:1])
                        k.drain(("S", i, j), s.activation(prob[:, slot, P:PW], bank[:, P:PW], ACT.Exp, bias=nmax[:, slot, 1:2],
                                                          accum_out=den[:, i % 2, j, 1:2]))

                for kind, i in schedule(cross, nxt, proj):
                    if kind == "step":
                        step(i)
                    elif kind == "weights":
                        weights(LOTS[2 + i])
                    else:
                        projection(k, kind, i)

            every_iteration(s, body)

        @block.vector
        def _(v):
            def weights(lot):
                for i in range(*lot):
                    _, off, raw = pieces[i]
                    v.wait_ge(s_whi, i + 1)
                    v.tensor_tensor(W[:, 1, off:off + D], raw, W[:, 0, off:off + D].bitcast(F32), ALU.subtract).then_inc(s_wlo, 1)

            def lo(k, name, hi, out, scale=1.0):
                k.wait_hi(name)
                src = banks[k.plan.bank(name)][:, 0:512 if len(out.shape) == 3 else S]
                if len(out.shape) == 3:
                    src = src.rearrange("p (k s) -> p k s", k=KT)
                k.drain(name, v.scalar_tensor_tensor(out, src, scale, hi.bitcast(F32), ALU.mult, ALU.subtract))

            def projection(k, kind, i):
                if kind == "sk":
                    lo(k, (kind, i), skT[:, 0, :], skT[:, 1, :])
                elif kind == "sq":
                    lo(k, (kind, i), sqT[:, 0, i, :], sqT[:, 1, i, :], SCALE)
                elif kind == "ck":
                    lo(k, (kind, i), ckT[:, 0, i, :], ckT[:, 1, i, :])
                elif kind == "cq":
                    lo(k, (kind, i), cqT[:, 0, i, :], cqT[:, 1, i, :], SCALE)
                elif kind == "x1t":
                    lo(k, (kind, i), x1T[:, 0, :, i * P:(i + 1) * P], x1T[:, 1, :, i * P:(i + 1) * P])

            v.wait_ge(s_x0, 1)
            v.tensor_tensor(xT[:, 1, :, :], xT_raw[:, :, :], xT[:, 0, :, :].bitcast(F32), ALU.subtract).then_inc(s_xs, 1)
            weights(LOTS[0])
            k = Banks(v, plan_pro, 0)
            weights(LOTS[1])
            projection(k, "sk", 0)
            projection(k, "sq", 0)

            def body(b, plan, cross, nxt, proj):
                k = Banks(v, plan, b)
                groups = groups_of(cross, nxt)

                def maxima(i, j):
                    slot = (i % 2) * HG + j
                    k.wait_full(("S", i, j))
                    bank = banks[plan.bank(("S", i, j))]
                    v.tensor_reduce(nmax[:, slot, 0:1], bank[:, 0:P], AX.X, ALU.max, negate=True)
                    v.tensor_reduce(nmax[:, slot, 1:2], bank[:, P:PW], AX.X, ALU.max, negate=True).then_inc(s_max, 1)

                def probT_tile(i, j):
                    k.wait_full(("T", i, j))
                    k.drain(("T", i, j), v.tensor_copy(probT[:, (i % 2) * HG + j, :], banks[plan.bank(("T", i, j))][:, 0:PW]))

                def reciprocals(i):
                    k.wait_drained(("S", i, HG - 1))
                    v.reciprocal(rden[:, i % 2, :, :], den[:, i % 2, :, :]).then_inc(s_rden, 1)

                def output(i):
                    n = group_number(b, groups, i)
                    k.wait_full(("O", i))
                    bank = banks[plan.bank(("O", i))]
                    v.tensor_copy(rT[:, i % 2, :], bank[:, S:2 * S]).then_inc(s_rT, 1)
                    v.wait_ge(s_rT, n)
                    if i >= 2:
                        v.wait_ge(s_os, n - 2)
                    k.drain(("O", i), v.tensor_tensor(o32[:, i % 2, :], bank[:, 0:S], rT[:, i % 2, :], ALU.mult))

                def step(i):
                    n = len(groups)
                    if i < n:
                        maxima(i, 0)
                        maxima(i, 1)
                    if 1 <= i <= n:
                        probT_tile(i - 1, 1)
                    if i < n:
                        for j in range(2, HG):
                            maxima(i, j)
                    if 1 <= i <= n:
                        reciprocals(i - 1)
                    if i >= 2:
                        output(i - 2)
                    if 1 <= i <= n:
                        probT_tile(i - 1, 2)
                        probT_tile(i - 1, 3)

                def add_and_measure(ai, i):
                    name, n = (("wo", "wout")[ai], i), b * (2 * TT) + (ai * TT + i + 1)
                    k.wait_full(name)
                    if ai == 0:
                        v.wait_ge(s_x, b * 16 + 16)
                    else:
                        v.wait_ge(s_norm, b * (2 * TT) + (i + 1))
                    k.drain(name, v.tensor_tensor(xres[:, i, :], banks[plan.bank(name)][:, :], xres[:, i, :], ALU.add))
                    k.wait_drained(name)
                    v.bn_stats(stats[:, i, :], xres[:, i, :]).then_inc(s_bn, 1)
                    wait_alone(v, s_bn, n, s_passed)
                    v.bn_aggr(mv[:, i, :], stats[:, i, :]).then_inc(s_agg, 1)

                def normalise(ai, i, out):
                    v.wait_ge(s_rstd, b * (2 * TT) + (ai * TT + i + 1))
                    v.tensor_scalar(out, xres[:, i, :], mv[:, i, 0:1], rstd[:, i, 1:2], ALU.subtract, ALU.mult).then_inc(s_norm, 1)

                ready = None
                for kind, i in schedule(cross, nxt, proj):
                    if kind == "step":
                        step(i)
                    elif kind == "weights":
                        weights(LOTS[2 + i])
                    elif kind == "wo":
                        add_and_measure(0, i)
                        normalise(0, i, xres[:, i, :])
                    elif kind == "wout":
                        add_and_measure(1, i)
                    else:
                        projection(k, kind, i)
                    if ready is not None:
                        normalise(1, ready, x2[:, b * TT + ready, :])
                    ready = i if kind == "wout" else None
                if ready is not None:
                    normalise(1, ready, x2[:, b * TT + ready, :])

            every_iteration(v, body)
            v.wait_ge(s_norm, B * 2 * TT)

        @block.tensor
        def _(t):
            def feature_major(k, name, w, src, kts):
                k.wait_free(name)
                k.filled(name, split_products(t, banks[k.plan.bank(name)][:, 0:S], w, src, kts))

            def token_major(k, name, src, w, kts, width):
                k.wait_free(name)
                k.filled(name, split_products(t, banks[k.plan.bank(name)][:, 0:width], src, w, kts))

            def weight(off, h, row, first, n):
                return W[:, h, off + row * D + first:off + row * D + first + n]

            def projection(k, kind, i):
                name, tok = (kind, i), slice(i * P, (i + 1) * P)
                if kind == "sk":
                    feature_major(k, name, lambda h, c: W[:, h, OFF_K + c * KV:OFF_K + (c + 1) * KV], lambda h, c: xT[:, h, c, :], range(KT))
                elif kind == "sv":
                    token_major(k, name, lambda h, c: xT[:, h, c, tok], lambda h, c: W[:, h, OFF_V + c * KV:OFF_V + (c + 1) * KV], range(KT), KV)
                elif kind == "sq":
                    feature_major(k, name, lambda h, c: weight(OFF_Q, h, c, i * P, P), lambda h, c: xT[:, h, c, :], range(KT))
                elif kind == "ck":
                    feature_major(k, name, lambda h, c: weight(OFF_CKV, h, 0, i * P, P), lambda h, c: ctxT[:, h, :], [0])
                elif kind == "cv":
                    token_major(k, name, lambda h, c: ctxT[:, h, tok], lambda h, c: weight(OFF_CKV, h, 1, 0, D), [0], D)
                elif kind == "cq":
                    feature_major(k, name, lambda h, c: weight(OFF_CQ, h, c, i * P, P), lambda h, c: x1T[:, h, c, :], range(KT))

            k = Banks(t, plan_pro, 0)
            t.wait_ge(s_xs, 1)
            t.wait_ge(s_wlo, KEYS)
            projection(k, "sk", 0)
            t.wait_ge(s_wlo, QUERIES)
            projection(k, "sq", 0)
            t.wait_ge(s_wlo, VALUES)
            t.wait_ge(s_const, 7)

            def body(b, plan, cross, nxt, proj):
                k = Banks(t, plan, b)
                groups = groups_of(cross, nxt)

                def query_tile(bank, qT, kT, g, qt, heads):
                    for x, y in ((0, 0), (0, 1), (1, 0)):
                        last = []
                        for j in heads:
                            rows = slice(HD * j, HD * (j + 1))
                            last.append(t.matmul(bank[j][:, P * qt:P * qt + P * (qt + 1)], qT[rows, x, g, qt * P:(qt + 1) * P],
                                                 kT(y)[rows, 0:P * (qt + 1)], start=False, stop=qt == TT - 1 and (x, y) == (1, 0), skip_group_check=True))
                    return last

                def scores(i):
                    g = groups[i] % NG
                    qT, kT = (cqT, lambda h: ckT[:, h, g, :]) if groups[i] < NG else (sqT, lambda h: skT[:, h, :])
                    own = [plan.bank(("S", i, j)) for j in range(HG - 1)]
                    for name in ([("cq", g), ("ck", g)] if groups[i] < NG else [("sq", g)] if g > 0 else []):
                        if plan.bank(name) not in own:
                            k.wait_drained(name)
                    bank = [banks[plan.bank(("S", i, j))] for j in range(HG)]
                    for heads in (range(HG - 1), [HG - 1]):
                        for j in heads:
                            k.wait_free(("S", i, j))
                            diag = bank[j][:, :].rearrange("p (a b c) -> p a b c", a=2, b=2)[:, :, 0, :]
                            t.matmul(diag, ident16[:, :], mask16[:, :, :], start=True, stop=False, skip_group_check=True)
                        query_tile(bank, qT, kT, g, 0, heads)
                    for j, ins in enumerate(query_tile(bank, qT, kT, g, 1, range(HG))):
                        k.filled(("S", i, j), ins)

                def transposes(i, j):
                    k.wait_drained(("S", i, j))
                    k.wait_free(("T", i, j))
                    bank = banks[plan.bank(("T", i, j))]
                    for c in range(3):
                        ins = t.transpose(bank[:, c * P:(c + 1) * P], prob[:, (i % 2) * HG + j, c * P:(c + 1) * P], ident[:, :])
                    k.filled(("T", i, j), ins)

                def outputs(i):
                    g = groups[i] % NG
                    k.wait_free(("O", i))
                    bank = banks[O_BANK]
                    for j in range(HG):
                        k.wait_drained(("T", i, j))
                    if g == 0:
                        for kt in range(TT):
                            k.wait_drained(("cv" if groups[i] < NG else "sv", kt))
                    for kt in range(2):
                        for j in range(HG):
                            v_ = cv[:, kt, HD * (HG * g + j):HD * (HG * g + j + 1)] if groups[i] < NG else sv[:, kt, HD * j:HD * (j + 1)]
                            t.matmul(bank[HD * j:HD * (j + 1), kt * P:S], v_, probT[:, (i % 2) * HG + j, kt * S:S + kt * P],
                                     start=kt == 0, stop=kt == 1, skip_group_check=True)
                    t.wait_ge(s_wide, group_number(b, groups, i))
                    for qt in range(TT):
                        ins = t.transpose(bank[:, S + qt * P:S + (qt + 1) * P], rwide[:, i % 2, qt, :], ident[:, :])
                    k.filled(("O", i), ins)

                def project_out(ai, i):
                    name, off, oT = ((("wo", i), OFF_WO, oT_self), (("wout", i), OFF_COUT, oT_cross))[ai]
                    k.wait_free(name)
                    for c in range(KT):
                        if i == 0:
                            t.wait_ge(s_os, b * (2 * NG) + (ai * NG + c + 1))
                        ins = split_products(t, banks[plan.bank(name)][:, :], lambda h, c: oT[:, h, c, i * P:(i + 1) * P],
                                             lambda h, c: weight(off, h, c, 0, D), [c], first=c == 0, last=c == KT - 1)
                    k.filled(name, ins)

                for kind, i in schedule(cross, nxt, proj):
                    if kind == "step":
                        if i < len(groups):
                            scores(i)
                        if 1 <= i <= len(groups):
                            transposes(i - 1, 0)
                            transposes(i - 1, 1)
                        if i >= 2:
                            outputs(i - 2)
                        if 1 <= i <= len(groups):
                            transposes(i - 1, 2)
                            transposes(i - 1, 3)
                    elif kind == "wo":
                        project_out(0, i)
                    elif kind == "wout":
                        project_out(1, i)
                    elif kind == "x1t":
                        t.wait_ge(s_norm, b * (2 * TT) + (i + 1))
                        k.wait_free((kind, i))
                        for c in range(KT):
                            ins = t.transpose(banks[plan.bank((kind, i))][:, c * P:(c + 1) * P], xres[:, i, c * P:(c + 1) * P], ident[:, :])
                        k.filled((kind, i), ins)
                    elif kind != "weights":
                        if (kind, i) == ("ck", 0):
                            t.wait_ge(s_cs, b + 1)
                            t.wait_ge(s_wlo, len(pieces))
                        if (kind, i) == ("sk", 0):
                            t.wait_ge(s_xs, b + 3)
                        if (kind, i) == ("cq", 0):
                            for u in range(TT):
                                k.wait_drained(("x1t", u))
                        projection(k, kind, i)

            every_iteration(t, body)


def fusion_phase(nc, ctx, sb, sem, A, banks, W, bias, x2, xT, cols, half_ampb, ident, s_passed):
    R, HR = 4, 2
    raw = sb(ctx, "raw", [P, R, 2, D])
    tile = sb(ctx, "tile", [P, HR, 2, 2, D], F32R)
    aux = sb(ctx, "aux", [P, 2, NP, D])
    ones = sb(ctx, "ones", [P, P])
    prod = sb(ctx, "prod", [P, D])
    acc = sb(ctx, "acc", [P, D])
    t32 = sb(ctx, "t32", [P, 2, D])
    NM = NP * KT
    mod = sb(ctx, "mod", [P, NL * NM])
    turns = sb(ctx, "turns", [P, NL * NM])
    diag = t32[:, :, :].rearrange("p z (c j) -> p (z c) j", j=P)
    pbias = sb(ctx, "pbias", [P, NP, D])
    ebias = sb(ctx, "ebias", [P, D])
    eb = sb(ctx, "eb", [P, ET])
    s_raw = [sem(f"s_raw{i}") for i in range(R)]
    s_aux = [sem("s_aux0"), sem("s_aux1")]
    s_small, s_eb, s_phase, s_cols = sem("s_small"), sem("s_eb"), sem("s_phase"), sem("s_cols")
    s_ones = sem("s_ones")
    s_xt, s_xhi = sem("s2_xt"), sem("s2_xhi")
    s_hi, s_lo = sem("s2_hi"), sem("s2_lo")
    s_tile = sem("s2_tile")
    s_prod, s_acc = sem("s2_prod"), sem("s2_acc")
    s_mod = sem("s2_mod")
    s_sin = sem("s2_sin")
    s_diag, s_mfull = sem("s2_diag"), sem("s2_mfull")
    s_whi = sem("s2_whi")
    s_t32 = sem("s2_t32")
    s_wlo = sem("s2_wlo")
    s_sum = sem("s2_sum")
    full = [sem(f"s2_full{i}") for i in range(KT + 1)]
    drained = [sem(f"s2_drained{i}") for i in range(KT + 1)]
    MOD_BANKS = (KT + 1, KT + 2)
    layers = W[:, :, 2 * KT * D:].rearrange("p h (l z c) -> p h l z c", l=NL, z=2)
    gates = W[:, :, 0:2 * KT * D].rearrange("p h (l c) -> p h l c", l=2)
    SUM_LINKS = 3 + 3 * KT
    AUX = 2 * KT
    FIN = 3 * KT
    AHEAD = {s_lo.name: R, s_prod.name: R, s_tile.name: 1, s_acc.name: 1, s_t32.name: 1}
    ahead = lambda s_: AHEAD[s_.name]

    def own(k):
        return slice(k * P, (k + 1) * P)

    with nc.Block() as block:
        @block.sync
        def _(q):
            q.dma_start(mod[:, :], A["phase"]).then_inc(s_phase, 16)
            q.dma_start(cols[:, :], A["cols"]).then_inc(s_cols, 16)
            with q.Fori(0, NL) as l:
                def load(kt):
                    wait_alone(q, s_lo, l * ET + (kt + 1 - R + ahead(s_lo)), s_passed)
                    wait_alone(q, s_prod, l * ET + (kt + 1 - R + ahead(s_prod)), s_passed)
                    q.dma_start(raw[:, kt % R, 0, :], A["ent_wT"][l, kt * P:(kt + 1) * P, :]).then_inc(s_raw[kt % R], 16)
                    q.dma_start(raw[:, kt % R, 1, :], A["ent_pw"][l, kt * P:(kt + 1) * P, :]).then_inc(s_raw[kt % R], 16)

                def load_aux(n):
                    if n < 2:
                        wait_alone(q, s_t32, l * KT + ahead(s_t32), s_passed)
                    elif n - 2 < KT:
                        wait_alone(q, s_wlo, l * (2 * KT) + (n - 1), s_passed)
                    else:
                        wait_alone(q, s_t32, l * KT + (n - 1 - KT + ahead(s_t32)), s_passed)
                    if n < KT:
                        q.dma_start(aux[:, n % 2, 0, :], A["gate_w"][l, n * P:(n + 1) * P, :]).then_inc(s_aux[n % 2], 16)
                    else:
                        k = n - KT
                        q.dma_start(aux[:, n % 2, :, :], A["path_w"][l, :, k * P:(k + 1) * P, :].rearrange("w p d -> p w d")).then_inc(s_aux[n % 2], 16)

                for kt in range(R):
                    load(kt)
                q.dma_start(eb[:, :], A["ent_b"][l]).then_inc(s_eb, 16)
                load_aux(0)
                load_aux(1)
                wait_alone(q, drained[KT], l + 1, s_passed)
                q.dma_start(pbias[:, :, :], A["path_b"][l].partition_broadcast(P)).then_inc(s_small, 16)
                q.dma_start(ebias[:, :], A["ent_pb"][l].partition_broadcast(P)).then_inc(s_small, 16)
                for kt in range(R, ET):
                    load(kt)
                    if kt % 2 and (kt - R) // 2 + 2 < AUX:
                        load_aux((kt - R) // 2 + 2)

        @block.gpsimd
        def _(g):
            for s_, n in ((s_lo, R), (s_prod, R), (s_tile, 1), (s_acc, 1), (s_t32, 1), (drained[KT], 1)):
                for _ in range(n):
                    g.sem_inc(s_, 1)
            for s_ in full:
                g.sem_inc(s_, 1)
            g.memset(ones[:, :], 1.0).then_inc(s_ones, 1)
            with g.Fori(0, NL) as l:
                for kt in range(ET):
                    if kt == 0:
                        g.wait_ge(s_eb, l * 16 + 16)
                        g.wait_ge(full[KT], l + 1)
                    else:
                        g.wait_ge(s_acc, l * (ET - 1) + (kt - 1 + ahead(s_acc)))
                    wait_alone(g, s_raw[kt % R], l * (32 * ET // R) + 32 * (kt // R + 1), s_passed)
                    out = acc if kt == 0 else prod
                    g.tensor_scalar(out[:, :], raw[:, kt % R, 1, :], eb[:, kt:kt + 1], 1.0, ALU.mult, ALU.mult).then_inc(s_prod, 1)
                    g.wait_ge(s_prod, l * ET + (kt + 1 + ahead(s_prod)))
                    if kt >= 1:
                        g.tensor_tensor(acc[:, :], acc[:, :], prod[:, :], ALU.add).then_inc(s_acc, 1)

        @block.scalar
        def _(s):
            s.preload_act_table_set("silu_and_others")
            for i in range(BT):
                s.wait_ge(s_xt, i + 1)
                s.activation(xT[:, 0, :, i * P:(i + 1) * P], banks[i][:, :].rearrange("p (k s) -> p k s", k=KT), ACT.Copy).then_inc(s_xhi, 1)
            s.wait_ge(s_mod, MOD_LINKS - 1)
            s.activation(mod[:, :], mod[:, :], ACT.Sin).then_inc(s_sin, 1)
            with s.Fori(0, NL) as l:
                def finished(z, k):
                    if z:
                        s.wait_ge(s_t32, l * KT + (k + 1 + ahead(s_t32)))
                    else:
                        s.wait_ge(full[k], l + 2)
                    s.activation(layers[:, 0, l, z, k * D:(k + 1) * D], t32[:, k % 2, :] if z else banks[k][:, :], ACT.Copy).then_inc(s_whi, 1)

                for kt in range(ET):
                    s.wait_ge(s_raw[kt % R], l * (32 * ET // R) + 32 * (kt // R + 1))
                    if kt == HR - 1:
                        s.wait_ge(full[KT - 1], l + 1)
                    else:
                        s.wait_ge(s_tile, l * (ET - 1) + (max(kt - HR + 1, 0) + ahead(s_tile)))
                    s.activation(tile[:, kt % HR, 0, :, :], raw[:, kt % R, :, :], ACT.Copy).then_inc(s_hi, 1)
                    if kt in (1, 3, 5, 7):
                        n = kt // 2
                        s.wait_ge(s_aux[n % 2], l * (16 * AUX // 2) + 16 * (n // 2 + 1))
                        s.activation(gates[:, 0, l, n * D:(n + 1) * D], aux[:, n % 2, 0, :], ACT.Copy).then_inc(s_whi, 1)
                    if kt in (10, 12, 14):
                        finished(1, (kt - 10) // 2)
                finished(1, KT - 1)
                for m in range(KT):
                    finished(0, m)

        @block.vector
        def _(v):
            links = {}

            def link(ins, sem_, before=0):
                links[sem_.name] = links.get(sem_.name, 0) + 1
                ins.then_inc(sem_, 1)
                v.wait_ge(sem_, before + links[sem_.name])

            for i in range(BT):
                v.wait_ge(s_xhi, i + 1)
                v.tensor_tensor(xT[:, 1, :, i * P:(i + 1) * P], banks[i][:, :].rearrange("p (k s) -> p k s", k=KT),
                                xT[:, 0, :, i * P:(i + 1) * P].bitcast(F32), ALU.subtract).then_inc(drained[i], 1)
                if i == 0:
                    M = 1.5 * 2 ** 23
                    v.wait_ge(s_phase, 16)
                    link(v.tensor_scalar(turns[:, :], mod[:, :], 0.5 / PI, 0.125, ALU.mult, ALU.add), s_mod)
                    link(v.tensor_scalar(turns[:, :], turns[:, :], M, M, ALU.add, ALU.subtract), s_mod)
                    for c in (6.28125, 0.0019350051879882812, 3.0199159819385986e-07):
                        link(v.scalar_tensor_tensor(mod[:, :], turns[:, :], -c, mod[:, :], ALU.mult, ALU.add), s_mod)
                    link(v.tensor_scalar(mod[:, :], mod[:, :], PI / 4, 3.1415925, ALU.add, ALU.min), s_mod)
                    link(v.tensor_scalar(mod[:, :], mod[:, :], -3.1415925, None, ALU.max), s_mod)
            v.wait_ge(s_sin, 1)
            link(v.tensor_scalar(mod[:, :], mod[:, :], 2 ** 0.5, None, ALU.mult), s_mod)
            assert links[s_mod.name] == MOD_LINKS
            v.wait_ge(s_cols, 16)
            v.tensor_scalar(half_ampb[:, :], cols[:, 0:KT], 0.5, None, ALU.mult)
            with v.Fori(0, NL) as l:
                def spread():
                    col = mod[:, :].rearrange("p (l c o) -> p l c o", l=NL, o=1)[:, l, :, :].broadcast_to([P, NM, P])
                    v.wait_ge(s_wlo, l * (2 * KT) + 1)
                    one = ident[:, :].rearrange("p (o j) -> p o j", o=1).broadcast_to([P, NM, P])
                    v.tensor_tensor(diag[:, :, :], one, col, ALU.mult).then_inc(s_diag, 1)

                def path_bias():
                    v.wait_ge(s_small, l * 32 + 32)
                    v.wait_ge(s_mfull, l + 1)
                    for w in range(NP):
                        link(v.tensor_tensor(pbias[:, w, :], pbias[:, w, :], banks[MOD_BANKS[w]][:, :], ALU.mult), s_sum, l * SUM_LINKS)
                    link(v.tensor_tensor(bias[:, 2 * l + 1, :], pbias[:, 0, :], pbias[:, 1, :], ALU.add), s_sum, l * SUM_LINKS)

                def lo_of_path(k):
                    v.wait_ge(s_whi, l * FIN + (KT + k + 1))
                    v.tensor_tensor(layers[:, 1, l, 1, k * D:(k + 1) * D], t32[:, k % 2, :],
                                    layers[:, 0, l, 1, k * D:(k + 1) * D].bitcast(F32), ALU.subtract).then_inc(s_wlo, 1)

                def path(k):
                    n = KT + k
                    v.wait_ge(s_aux[n % 2], l * (16 * AUX // 2) + 16 * (n // 2 + 1))
                    a = aux[:, n % 2, :, :]
                    for w in range(NP):
                        link(v.tensor_tensor(a[:, w, :], a[:, w, :], banks[MOD_BANKS[w]][:, :], ALU.mult), s_sum, l * SUM_LINKS)
                    link(v.tensor_tensor(a[:, 0, own(k)], a[:, 0, own(k)], ident[:, :], ALU.add), s_sum, l * SUM_LINKS)
                    if k >= 2:
                        v.wait_ge(s_wlo, l * (2 * KT) + (KT + k - 1))
                    v.tensor_tensor(t32[:, k % 2, :], a[:, 0, :], a[:, 1, :], ALU.add).then_inc(s_t32, 1)

                def gate_lo(n):
                    v.wait_ge(s_whi, l * FIN + (n + 1))
                    v.tensor_tensor(gates[:, 1, l, n * D:(n + 1) * D], aux[:, n % 2, 0, :],
                                    gates[:, 0, l, n * D:(n + 1) * D].bitcast(F32), ALU.subtract).then_inc(s_wlo, 1)

                links[s_sum.name] = 0
                extra = {3: [spread], 7: [path_bias], 9: [lambda: path(0)], 11: [lambda: lo_of_path(0), lambda: path(1)],
                         13: [lambda: lo_of_path(1), lambda: path(2)], 15: [lambda: lo_of_path(2), lambda: path(3)]}
                for n in range(KT):
                    extra.setdefault(2 * n + 2, []).append(lambda n=n: gate_lo(n))
                for kt in range(ET):
                    v.wait_ge(s_hi, l * ET + (kt + 1))
                    v.tensor_tensor(tile[:, kt % HR, 1, :, :], raw[:, kt % R, :, :], tile[:, kt % HR, 0, :, :].bitcast(F32),
                                    ALU.subtract).then_inc(s_lo, 1)
                    for f in extra.get(kt, []):
                        f()
                lo_of_path(KT - 1)
                for m in range(KT):
                    v.wait_ge(s_whi, l * FIN + (2 * KT + m + 1))
                    v.tensor_tensor(layers[:, 1, l, 0, m * D:(m + 1) * D], banks[m][:, :],
                                    layers[:, 0, l, 0, m * D:(m + 1) * D].bitcast(F32), ALU.subtract).then_inc(drained[m], 1)
                v.wait_ge(s_small, l * 32 + 32)
                v.wait_ge(full[KT], l + 2)
                v.tensor_tensor(bias[:, 2 * l, :], banks[KT][:, :], ebias[:, :], ALU.add).then_inc(drained[KT], 1)
                assert links[s_sum.name] == SUM_LINKS, links

        @block.tensor
        def _(t):
            for i in range(BT):
                for c in range(KT):
                    ins = t.transpose(banks[i][:, c * P:(c + 1) * P], x2[:, i, c * P:(c + 1) * P], ident[:, :])
                ins.then_inc(s_xt, 1)
            with t.Fori(0, NL) as l:
                for kt in range(ET):
                    t.wait_ge(s_lo, l * ET + (kt + 1 + ahead(s_lo)))
                    for m in range(KT):
                        if kt == 0:
                            t.wait_ge(drained[m], l + 1)
                        ins = split_products(t, banks[m][:, :], lambda h, c: tile[:, kt % HR, h, 0, m * P:(m + 1) * P],
                                             lambda h, c: tile[:, kt % HR, h, 1, :], [0], first=kt == 0, last=kt == ET - 1)
                        if kt == 0:
                            t.matmul(banks[m][:, own(m)], ident[:, :], ident[:, :], start=False, stop=False, skip_group_check=True)
                        if kt == ET - 1:
                            ins.then_inc(full[m], 1)
                    if kt < ET - 1:
                        ins.then_inc(s_tile, 1)
                    if kt == 4:
                        t.wait_ge(s_ones, 1)
                        t.wait_ge(s_diag, l + 1)
                        t.wait_ge(s_t32, l * KT + ahead(s_t32))
                        for w in range(NP):
                            ins = t.matmul(banks[MOD_BANKS[w]][:, :], ones[:, :], diag[:, w * KT:(w + 1) * KT, :], start=True, stop=True)
                        ins.then_inc(s_mfull, 1)
                t.wait_ge(s_acc, l * (ET - 1) + (ET - 1 + ahead(s_acc)))
                t.wait_ge(drained[KT], l + 1)
                t.matmul(banks[KT][:, :], ones[:, :], acc[:, :], start=True, stop=True).then_inc(full[KT], 1)
            t.wait_ge(s_t32, NL * KT + ahead(s_t32))
            t.wait_ge(s_wlo, NL * 2 * KT)
            for name, m, bank in EARLY:
                gate_products(t, banks[bank], W, xT, name, m)


EARLY = [("ph", 0, 6), ("amp", 0, 7)]


def gate_products(t, bank, W, xT, gate, m):
    off = {"amp": OFF_AMP, "ph": OFF_PH}[gate]
    return split_products(t, bank[:, :], lambda h, c: W[:, h, off + c * D + m * P:off + c * D + (m + 1) * P],
                          lambda h, c: xT[:, h, c, :], range(KT))


def ffn_order(last):
    UN = 2 * NL * BT
    order = [("mm", 0), ("mm", 1)]
    for u in range(2, UN + 2):
        if u < UN:
            order.append(("mm", u))
        if not last and u == 2:
            order += [("xt", i) for i in range(BT)]
        if u - 2 < UN - BT:
            order.append(("tr", u - 2))
    return order + ([] if last else [(w, m) for m in range(KT) for w in ("ph", "amp")])


def ffn_phase(nc, ctx, sb, sem, A, banks, W, bias, x2, xT, cols, half_ampb, ident, s_passed):
    BS = BT * P
    UN = 2 * NL * BT
    xb = sb(ctx, "xb", [P, BT, D])
    hT = sb(ctx, "hT", [P, 2, KT, BS], F32R)
    y = sb(ctx, "y", [P, BT, D])
    amp = sb(ctx, "amp", [P, 2, BS])
    wave = sb(ctx, "wave", [P, 2, BS])
    HT = 4
    ht = sb(ctx, "ht", [P, HT, KT, P])
    lng = sb(ctx, "lng", [P, D])
    lnb = sb(ctx, "lnb", [P, D])
    stats = sb(ctx, "stats3", [P, BT, 6])
    mv = sb(ctx, "mv3", [P, BT, 2])
    rstd = sb(ctx, "rstd3", [P, BT, 2])
    nhalf = sb(ctx, "nhalf", [P, 1])
    angles = sb(ctx, "angles", [P, 2])

    s_ln = sem("s3_ln")
    s_c = sem("s3_const")
    s_xb = sem("s3_xb")
    s_hi = sem("s3_hi")
    s_u, s_sin = sem("s3_u"), sem("s3_sin")
    s_h0 = sem("s3_h0")
    s_h0hi, s_h0lo = sem("s3_h0hi"), sem("s3_h0lo")
    s_bn, s_agg, s_var, s_rstd = sem("s3_bn"), sem("s3_agg"), sem("s3_var"), sem("s3_rstd")
    s_norm = sem("s3_norm")
    s_hhi, s_hlo = sem("s3_hhi"), sem("s3_hlo")
    s_res = sem("s3_res")
    s_g, s_sum = sem("s3_g"), sem("s3_sum")
    s_fin = sem("s3_fin")
    s_out = sem("s3_out")
    full = [sem(f"s3_full{i}") for i in range(8)]
    drained = [sem(f"s3_drained{i}") for i in range(8)]
    LN = UN + BT
    NORMS = list(range(UN - 1)) + [UN, UN - 1] + [UN + i for i in range(1, BT)]
    number = {u: n + 1 for n, u in enumerate(NORMS)}

    plan_pro = Plan(full, drained)

    def ring(plan, names):
        for name in names:
            plan.take(name, plan.ring % 8)
            plan.ring += 1
        return plan

    plan_pro.ring = EARLY[0][2]
    ring(plan_pro, [(w, m) for m in range(KT) for w in ("ph", "amp")])
    plan_body = ring(plan_pro.after(), ffn_order(False)).loop()
    assert plan_body.ring % 8 == plan_pro.ring % 8
    plan_last = ring(plan_body.after(NB - 2), ffn_order(True))

    def every_block(eng, body):
        with eng.Fori(0, NB - 1) as b:
            body(b, plan_body, False)
        body(NB - 1, plan_last, True)

    def gain(s, k):
        c = 2 * KT + 2 * KT * s + k
        return cols[:, c:c + 1]

    def shift(s, k):
        c = 2 * KT + 2 * KT * s + KT + k
        return cols[:, c:c + 1]

    with nc.Block() as block:
        @block.sync
        def _(q):
            q.dma_start(xb[:, :, :], x2[:, BT:2 * BT, :]).then_inc(s_xb, 16)
            q.dma_start(lng[:, :], A["ln_g"].partition_broadcast(P)).then_inc(s_ln, 16)
            q.dma_start(lnb[:, :], A["ln_b"].partition_broadcast(P)).then_inc(s_ln, 16)
            out = A["out"].rearrange("b (t p) d -> (b t) p d", p=P)
            blocks = x2[:, :, :].rearrange("p (b t) d -> p b t d", t=BT)

            def body(b, plan, load):
                if load:
                    Banks(q, plan, b).wait_full(("xt", BT - 1))
                    q.sem_inc(s_passed, 1)
                    q.dma_start(xb[:, :, :], blocks[:, b + 2, :, :]).then_inc(s_xb, 16)
                for i in range(BT):
                    wait_alone(q, s_fin, b * BT + (i + 1), s_passed)
                    q.dma_start(out[b * BT + i], y[:, i, :]).then_inc(s_out, 16)

            with q.Fori(0, NB - 2) as b:
                body(b, plan_body, True)
            body(NB - 2, plan_body, False)
            body(NB - 1, plan_last, False)
            q.wait_ge(s_out, 16 * NB * BT + 1)

        @block.gpsimd
        def _(g):
            g.memset(nhalf[:, :], -0.5).then_inc(s_c, 1)
            g.memset(angles[:, 0:1], PI / 2).then_inc(s_c, 1)
            g.memset(angles[:, 1:2], -0.25).then_inc(s_c, 1)
            plan_pro.begin(g)
            g.sem_inc(s_out, 1)
            g.wait_ge(s_c, 3)
            g.wait_ge(s_ln, 32)

            def body(b, plan, last):
                def rstd_of(u):
                    i = u % BT
                    m = b * LN + number[u]
                    wait_alone(g, s_agg, m, s_passed)
                    g.tensor_scalar(rstd[:, i, 0:1], mv[:, i, 1:2], EPS, None, ALU.add).then_inc(s_var, 1)
                    g.wait_ge(s_var, m)
                    g.tensor_tensor(rstd[:, i, 1:2], rstd[:, i, 0:1], nhalf[:, :], ALU.pow).then_inc(s_rstd, 1)

                def lo(u):
                    i = u % BT
                    g.wait_ge(s_hhi, b * (UN - BT) + (u + 1))
                    g.tensor_tensor(hT[:, 1, :, i * P:(i + 1) * P], ht[:, u % HT, :, :],
                                    hT[:, 0, :, i * P:(i + 1) * P].bitcast(F32), ALU.subtract).then_inc(s_hlo, 1)

                def residual(i):
                    x = x2[:, b * BT + i, :]
                    g.tensor_tensor(x, x, lnb[:, :], ALU.add).then_inc(s_res, 1)

                def last_gain(i):
                    g.wait_ge(s_norm, b * UN + (UN - BT + i + 1))
                    g.tensor_tensor(y[:, i, :], y[:, i, :], lng[:, :], ALU.mult).then_inc(s_g, 1)

                for u in range(UN - 2):
                    if 2 <= u:
                        lo(u - 2)
                    rstd_of(u)
                    if u < BT:
                        residual(u)
                last_gain(0)
                rstd_of(UN - 2)
                last_gain(1)
                rstd_of(UN)
                rstd_of(UN - 1)
                last_gain(2)
                rstd_of(UN + 1)
                last_gain(3)
                rstd_of(UN + 2)
                rstd_of(UN + 3)

            every_block(g, body)

        @block.scalar
        def _(s):
            s.wait_ge(s_c, 3)

            def x2T_hi(k, i):
                k.wait_full(("xt", i))
                bank = banks[k.plan.bank(("xt", i))][:, :].rearrange("p (k s) -> p k s", k=KT)
                s.activation(xT[:, 0, :, i * P:(i + 1) * P], bank, ACT.Copy).then_inc(s_hi, 1)

            def gates(k, block):
                for m in range(KT):
                    n = block * KT + (m + 1)
                    if m >= 2:
                        s.wait_ge(s_h0lo, n - 2)
                    k.wait_full(("ph", m))
                    k.drain(("ph", m), s.activation(wave[:, m % 2, :], banks[k.plan.bank(("ph", m))][:, :], ACT.Tanh, bias=cols[:, KT + m:KT + m + 1]))
                    k.wait_drained(("ph", m))
                    s.activation(wave[:, m % 2, :], wave[:, m % 2, :], ACT.Abs, bias=angles[:, 1:2]).then_inc(s_u, 1)
                    s.wait_ge(s_u, n)
                    s.activation(wave[:, m % 2, :], wave[:, m % 2, :], ACT.Sin, bias=angles[:, 0:1], scale=-PI).then_inc(s_sin, 1)
                    k.wait_full(("amp", m))
                    k.drain(("amp", m), s.activation(amp[:, m % 2, :], banks[k.plan.bank(("amp", m))][:, :], ACT.Tanh, bias=half_ampb[:, m:m + 1], scale=0.5))
                    s.wait_ge(s_h0, n)
                    s.activation(hT[:, 0, m, :], wave[:, m % 2, :], ACT.Copy, scale=SQRT_HALF).then_inc(s_h0hi, 1)

            gates(Banks(s, plan_pro, 0), 0)

            def body(b, plan, last):
                k = Banks(s, plan, b)

                def hT_of(u):
                    k.wait_full(("tr", u))
                    if u >= HT:
                        s.wait_ge(s_hlo, b * (UN - BT) + (u - HT + 1))
                    bank = banks[plan.bank(("tr", u))]
                    for c in range(KT):
                        ins = s.activation(ht[:, u % HT, c, :], bank[:, c * P:(c + 1) * P], ACT.Identity,
                                           bias=shift(u // BT, c), scale=gain(u // BT, c))
                    k.drain(("tr", u), ins)
                    k.wait_drained(("tr", u))
                    i = u % BT
                    s.activation(hT[:, 0, :, i * P:(i + 1) * P], ht[:, u % HT, :, :], ACT.Copy).then_inc(s_hhi, 1)

                for kind, n in ffn_order(last):
                    if kind == "tr":
                        hT_of(n)
                    elif kind == "xt":
                        x2T_hi(k, n)
                if not last:
                    gates(k, b + 1)

            every_block(s, body)

        @block.vector
        def _(v):
            def x2T_lo(k, i, n):
                v.wait_ge(s_hi, n)
                bank = banks[k.plan.bank(("xt", i))][:, :].rearrange("p (k s) -> p k s", k=KT)
                k.drain(("xt", i), v.tensor_tensor(xT[:, 1, :, i * P:(i + 1) * P], bank, xT[:, 0, :, i * P:(i + 1) * P].bitcast(F32), ALU.subtract))

            def h0(k, block, m):
                n = block * KT + (m + 1)
                k.wait_drained(("amp", m))
                v.wait_ge(s_sin, n)
                v.scalar_tensor_tensor(wave[:, m % 2, :], amp[:, m % 2, :], 1.0, wave[:, m % 2, :], ALU.add, ALU.mult).then_inc(s_h0, 1)
                v.wait_ge(s_h0hi, n)
                v.scalar_tensor_tensor(hT[:, 1, m, :], wave[:, m % 2, :], SQRT_HALF, hT[:, 0, m, :].bitcast(F32), ALU.mult, ALU.subtract).then_inc(s_h0lo, 1)

            k = Banks(v, plan_pro, 0)
            for m in range(KT):
                h0(k, 0, m)

            def body(b, plan, last):
                k = Banks(v, plan, b)

                def statistics(u):
                    i = u % BT
                    v.bn_stats(stats[:, i, :], y[:, i, :]).then_inc(s_bn, 1)
                    wait_alone(v, s_bn, b * LN + number[u], s_passed)
                    v.bn_aggr(mv[:, i, :], stats[:, i, :]).then_inc(s_agg, 1)

                def normalise(u, s_done):
                    i = u % BT
                    v.wait_ge(s_rstd, b * LN + number[u])
                    v.tensor_scalar(y[:, i, :], y[:, i, :], mv[:, i, 0:1], rstd[:, i, 1:2], ALU.subtract, ALU.mult).then_inc(s_done, 1)

                def unit(u):
                    s_, i = divmod(u, BT)
                    k.wait_full(("mm", u))
                    if s_ == 0:
                        v.wait_ge(s_out, b * (16 * BT) + 1)
                    k.drain(("mm", u), v.tensor_tensor(y[:, i, :], banks[plan.bank(("mm", u))][:, :], bias[:, s_, :], ALU.add))
                    if u >= 1:
                        normalise(u - 1, s_norm)
                    k.wait_drained(("mm", u))
                    statistics(u)

                def finish(i):
                    n = b * BT + (i + 1)
                    v.wait_ge(s_g, n)
                    v.wait_ge(s_res, n)
                    v.tensor_tensor(y[:, i, :], y[:, i, :], x2[:, b * BT + i, :], ALU.add).then_inc(s_sum, 1)
                    v.wait_ge(s_sum, n)
                    statistics(UN + i)

                for kind, n in ffn_order(last):
                    if kind == "mm":
                        if n == UN - 1:
                            finish(0)
                        unit(n)
                        if not last and 2 <= n < 2 + BT // 2:
                            for i in (2 * n - 4, 2 * n - 3):
                                x2T_lo(k, i, b * BT + (i + 1))
                finish(1)
                normalise(UN, s_fin)
                normalise(UN - 1, s_norm)
                finish(2)
                normalise(UN + 1, s_fin)
                if not last:
                    h0(k, b + 1, 0)
                finish(3)
                normalise(UN + 2, s_fin)
                if not last:
                    h0(k, b + 1, 1)
                normalise(UN + 3, s_fin)
                if not last:
                    h0(k, b + 1, 2)
                    h0(k, b + 1, 3)

            every_block(v, body)

        @block.tensor
        def _(t):
            def x2T(k, i):
                k.wait_free(("xt", i))
                for c in range(KT):
                    ins = t.transpose(banks[k.plan.bank(("xt", i))][:, c * P:(c + 1) * P], xb[:, i, c * P:(c + 1) * P], ident[:, :])
                k.filled(("xt", i), ins)

            def gate(k, name, m):
                k.wait_free((name, m))
                k.filled((name, m), gate_products(t, banks[k.plan.bank((name, m))], W, xT, name, m))

            k = Banks(t, plan_pro, 0)
            for name, m, bank in EARLY:
                assert k.plan.bank((name, m)) == bank
                t.sem_inc(full[bank], 1)
            for m in range(KT):
                for name in ("ph", "amp"):
                    if all((name, m) != e[:2] for e in EARLY):
                        gate(k, name, m)

            def body(b, plan, last):
                k = Banks(t, plan, b)

                def mm(u, cs):
                    s_, i = divmod(u, BT)
                    off = (OFF_ENT, OFF_PATH)[s_ % 2][s_ // 2]
                    if cs[0] == 0:
                        k.wait_free(("mm", u))
                    ins = split_products(t, banks[plan.bank(("mm", u))][:, :], lambda h, c: hT[:, h, c, i * P:(i + 1) * P],
                                         lambda h, c: W[:, h, off + c * D:off + (c + 1) * D], cs, first=cs[0] == 0, last=cs[-1] == KT - 1)
                    if cs[-1] == KT - 1:
                        k.filled(("mm", u), ins)

                def transpose_norm(u):
                    t.wait_ge(s_norm, b * UN + (u + 1))
                    k.wait_free(("tr", u))
                    for c in range(KT):
                        ins = t.transpose(banks[plan.bank(("tr", u))][:, c * P:(c + 1) * P], y[:, u % BT, c * P:(c + 1) * P], ident[:, :])
                    k.filled(("tr", u), ins)

                for c in range(KT):
                    t.wait_ge(s_h0lo, b * KT + (c + 1))
                    for u in (0, 1):
                        mm(u, [c])
                for kind, n in ffn_order(last):
                    if kind == "mm" and n >= 2:
                        if n >= BT:
                            t.wait_ge(s_hlo, b * (UN - BT) + (n - BT + 1))
                        mm(n, list(range(KT // 2)))
                        if n == 2 and not last:
                            t.wait_ge(s_xb, b * 16 + 16)
                            for i in range(BT):
                                x2T(k, i)
                        if n - 2 < UN - BT:
                            transpose_norm(n - 2)
                        mm(n, list(range(KT // 2, KT)))
                    elif kind in ("ph", "amp"):
                        if (kind, n) == ("ph", 0):
                            for i in range(BT):
                                k.wait_drained(("xt", i))
                        gate(k, kind, n)

            every_block(t, body)


def layout(inputs):
    import numpy as np
    a = {k.replace("L0_", ""): np.asarray(v) for k, v in inputs.items()}
    c = np.ascontiguousarray
    x = c(a["x"])
    wq = a["attn_Wq"].reshape(D, NKV, NH // NKV, HD).transpose(0, 2, 1, 3).reshape(D, D)
    wo = a["attn_Wo"].reshape(NKV, NH // NKV, HD, D).transpose(1, 0, 2, 3).reshape(D, D)
    col = lambda v: v.reshape(-1, P).T
    g3, b3, g4, b4 = (a[f"ffn_{n}"] for n in ("ln3_g", "ln3_b", "ln4_g", "ln4_b"))
    return {
        "x": x,
        "xT": c(x.reshape(B * S, D).T),
        "ctxT": c(a["ctx_512"].reshape(B * S, L).T),
        "w_k": c(a["attn_Wk"]),
        "w_v": c(a["attn_Wv"]),
        "w_q": c(wq),
        "w_o": c(wo),
        "w_cq": c(a["xattn_Wq"].T),
        "w_ckv": c(a["xattn_Wkv_expand"].T),
        "w_cout": c(a["xattn_Wout"].T),
        "ent_wT": c(a["ffn_ent_w"].transpose(0, 2, 1)),
        "ent_pw": c(a["ffn_ent_pw"]),
        "ent_b": c(a["ffn_ent_b"].reshape(NL, ET, P).transpose(0, 2, 1)),
        "ent_pb": c(a["ffn_ent_pb"]),
        "gate_w": c(np.stack([a["ffn_amp_w"], a["ffn_ph_w"]])),
        "path_w": c(a["ffn_path_w"]),
        "path_b": c(a["ffn_path_b"]),
        "phase": c(a["ffn_phase"].reshape(NL * NP * KT, P).T),
        "cols": c(np.concatenate([col(v) for v in (a["ffn_amp_b"], a["ffn_ph_b"], g3[0], b3[0], g4[0], b4[0], g3[1], b3[1])], axis=1)),
        "ln_g": c(g4[1]),
        "ln_b": c(b4[1]),
    }


def kernel(**inputs):
    import concourse.bacc as bacc
    from concourse.bass_utils import run_bass_kernel_spmd

    nc = bacc.Bacc("TRN2", target_bir_lowering=False, num_devices=1)
    arrays = layout(inputs)
    A = {n: nc.dram_tensor(f"in_{n}", v.shape, mybir.dt.from_np(v.dtype), kind="ExternalInput").ap() for n, v in arrays.items()}
    A["out"] = nc.dram_tensor("out", (B, S, D), F32, kind="ExternalOutput").ap()
    build(nc, A)
    r = run_bass_kernel_spmd(nc, [{f"in_{n}": v for n, v in arrays.items()}], core_ids=[0])
    return r.results[0]["out"]
```
